# Optimizing a Trainium2 kernel written in Bass

```python
import numpy as np
import jax
import jax.numpy as jnp

def _softmax(x, axis=-1):
    return jax.nn.softmax(x, axis=axis)

def _gelu(x):
    return jax.nn.gelu(x, approximate=True)

def _silu(x):
    return jax.nn.silu(x)

def _sigmoid(x):
    return jax.nn.sigmoid(x)

def _layernorm(x, axis=-1, eps=1e-05):
    m = jnp.mean(x, axis=axis, keepdims=True)
    v = jnp.var(x, axis=axis, keepdims=True)
    return (x - m) / jnp.sqrt(v + eps)

def _scatter_add(tgt, idx, src, axis=0):
    return tgt.at[idx].add(src)

def _segment_sum(src, seg, n):
    return jax.ops.segment_sum(src, seg, n)
kernel_name = 'mk_recurrent_d1_jaxref_r4_28ca3b'

def setup_inputs(seed: int=0):
    np.random.seed(seed)
    _w = jnp.asarray

    def _L0_attn_setup():
        import jax, jax.numpy as jnp
        import numpy as np
        DIM = 256
        STATE = 64
        HEADS = 8
        EXPAND = 2
        INNER = DIM * EXPAND
        HEAD_DIM = INNER // HEADS
        KERNEL = 4
        B, L = (2, 512)
        EPS = 1e-05

        def _causal_conv(x, conv_w, conv_b):
            x_pad = jnp.pad(x, ((0, 0), (KERNEL - 1, 0), (0, 0)))
            w = conv_w[:, 0, :]
            y = sum((x_pad[:, k:k + x.shape[1], :] * w[:, k] for k in range(KERNEL)))
            return y + conv_b

        def _ssd_scan(x, b, c, dt, a):
            state0 = jnp.zeros((x.shape[0], HEADS, STATE, HEAD_DIM), x.dtype)

            def step(state, inp):
                x_t, b_t, c_t, dt_t = inp
                decay = jnp.exp(dt_t * a)[..., None, None]
                b_bar = dt_t[..., None] * b_t
                state = decay * state + b_bar[..., None] * x_t[:, :, None, :]
                y_t = jnp.einsum('bhn,bhnp->bhp', c_t, state)
                return (state, y_t)
            xs = (x.transpose(1, 0, 2, 3), b.transpose(1, 0, 2, 3), c.transpose(1, 0, 2, 3), dt.transpose(1, 0, 2))
            _, ys = jax.lax.scan(step, state0, xs)
            return ys.transpose(1, 0, 2, 3)
        key = jax.random.key(seed)
        ks = jax.random.split(key, 12)
        s = 0.02
        return {'input_tensor': jax.random.normal(ks[0], (B, L, DIM), jnp.float32), 'Wx': jax.random.normal(ks[1], (INNER, DIM), jnp.float32) * s, 'Wz': jax.random.normal(ks[2], (INNER, DIM), jnp.float32) * s, 'conv_w': jax.random.normal(ks[3], (INNER, 1, KERNEL), jnp.float32) * s, 'conv_b': jnp.zeros((INNER,), jnp.float32), 'Wb': jax.random.normal(ks[4], (HEADS * STATE, INNER), jnp.float32) * s, 'Wc': jax.random.normal(ks[5], (HEADS * STATE, INNER), jnp.float32) * s, 'Wdt': jax.random.normal(ks[6], (HEADS, INNER), jnp.float32) * s, 'b_dt': jnp.zeros((HEADS,), jnp.float32), 'log_a': jnp.log(jnp.full((HEADS,), 0.5, jnp.float32)), 'd_param': jnp.ones((HEADS,), jnp.float32), 'gn_w': jnp.ones((INNER,), jnp.float32), 'gn_b': jnp.zeros((INNER,), jnp.float32), 'Wout': jax.random.normal(ks[7], (DIM, INNER), jnp.float32) * s}
    _L0_attn_in = _L0_attn_setup()

    def _L0_ffn_setup():
        import jax, jax.numpy as jnp
        import numpy as np
        B, S, H = (4, 512, 256)
        E = 8
        GS = 2
        NG = E // GS
        F = int(H * 4 * (2.0 / 3.0))
        key = jax.random.key(seed)
        ks = jax.random.split(key, 7)
        sc_h = 1.0 / np.sqrt(H)
        sc_f = 1.0 / np.sqrt(F)
        return {'x': jax.random.normal(ks[0], (B, S, H), dtype=jnp.float32), 'Wr': jax.random.normal(ks[1], (H, E), dtype=jnp.float32) * sc_h, 'br': jnp.zeros((E,), dtype=jnp.float32), 'W_up': jax.random.normal(ks[2], (NG, H, F), dtype=jnp.float32) * sc_h, 'b_up': jax.random.normal(ks[3], (NG, F), dtype=jnp.float32) * 0.01, 'W_down': jax.random.normal(ks[4], (E, F, H), dtype=jnp.float32) * sc_f, 'b_down': jax.random.normal(ks[5], (E, H), dtype=jnp.float32) * 0.01}
    _L0_ffn_in = _L0_ffn_setup()
    _d = {'L0_attn_input_tensor': _L0_attn_in['input_tensor'], 'L0_attn_Wx': _L0_attn_in['Wx'], 'L0_attn_Wz': _L0_attn_in['Wz'], 'L0_attn_conv_w': _L0_attn_in['conv_w'], 'L0_attn_conv_b': _L0_attn_in['conv_b'], 'L0_attn_Wb': _L0_attn_in['Wb'], 'L0_attn_Wc': _L0_attn_in['Wc'], 'L0_attn_Wdt': _L0_attn_in['Wdt'], 'L0_attn_b_dt': _L0_attn_in['b_dt'], 'L0_attn_log_a': _L0_attn_in['log_a'], 'L0_attn_d_param': _L0_attn_in['d_param'], 'L0_attn_gn_w': _L0_attn_in['gn_w'], 'L0_attn_gn_b': _L0_attn_in['gn_b'], 'L0_attn_Wout': _L0_attn_in['Wout'], 'L0_ffn_Wr': _L0_ffn_in['Wr'], 'L0_ffn_br': _L0_ffn_in['br'], 'L0_ffn_W_up': _L0_ffn_in['W_up'], 'L0_ffn_b_up': _L0_ffn_in['b_up'], 'L0_ffn_W_down': _L0_ffn_in['W_down'], 'L0_ffn_b_down': _L0_ffn_in['b_down']}
    _x0 = _d['L0_attn_input_tensor']
    _d['L0_attn_input_tensor'] = jax.random.normal(jax.random.fold_in(jax.random.key(seed), 1), (2, 4096, 256), dtype=_x0.dtype)
    del _x0
    return _d

def reference(L0_attn_input_tensor, L0_attn_Wx, L0_attn_Wz, L0_attn_conv_w, L0_attn_conv_b, L0_attn_Wb, L0_attn_Wc, L0_attn_Wdt, L0_attn_b_dt, L0_attn_log_a, L0_attn_d_param, L0_attn_gn_w, L0_attn_gn_b, L0_attn_Wout, L0_ffn_Wr, L0_ffn_br, L0_ffn_W_up, L0_ffn_b_up, L0_ffn_W_down, L0_ffn_b_down):

    def _L0_attn_ref(input_tensor, Wx, Wz, conv_w, conv_b, Wb, Wc, Wdt, b_dt, log_a, d_param, gn_w, gn_b, Wout):
        import jax, jax.numpy as jnp
        import numpy as np
        DIM = 256
        STATE = 64
        HEADS = 8
        EXPAND = 2
        INNER = DIM * EXPAND
        HEAD_DIM = INNER // HEADS
        KERNEL = 4
        B, L = (2, 512)
        EPS = 1e-05

        def _causal_conv(x, conv_w, conv_b):
            x_pad = jnp.pad(x, ((0, 0), (KERNEL - 1, 0), (0, 0)))
            w = conv_w[:, 0, :]
            y = sum((x_pad[:, k:k + x.shape[1], :] * w[:, k] for k in range(KERNEL)))
            return y + conv_b

        def _ssd_scan(x, b, c, dt, a):
            state0 = jnp.zeros((x.shape[0], HEADS, STATE, HEAD_DIM), x.dtype)

            def step(state, inp):
                x_t, b_t, c_t, dt_t = inp
                decay = jnp.exp(dt_t * a)[..., None, None]
                b_bar = dt_t[..., None] * b_t
                state = decay * state + b_bar[..., None] * x_t[:, :, None, :]
                y_t = jnp.einsum('bhn,bhnp->bhp', c_t, state)
                return (state, y_t)
            xs = (x.transpose(1, 0, 2, 3), b.transpose(1, 0, 2, 3), c.transpose(1, 0, 2, 3), dt.transpose(1, 0, 2))
            _, ys = jax.lax.scan(step, state0, xs)
            return ys.transpose(1, 0, 2, 3)
        bsz, seq, _ = input_tensor.shape
        x = input_tensor @ Wx.T
        z = input_tensor @ Wz.T
        x = _causal_conv(x, conv_w, conv_b)
        x = jax.nn.silu(x)
        b = (x @ Wb.T).reshape(bsz, seq, HEADS, STATE)
        c = (x @ Wc.T).reshape(bsz, seq, HEADS, STATE)
        dt = jax.nn.softplus(x @ Wdt.T + b_dt)
        xh = x.reshape(bsz, seq, HEADS, HEAD_DIM)
        a = -jnp.exp(log_a)
        y = _ssd_scan(xh, b, c, dt, a)
        y = y + d_param[None, None, :, None] * xh
        yg = y
        mean = yg.mean(axis=(1, 3), keepdims=True)
        var = yg.var(axis=(1, 3), keepdims=True)
        yn = (yg - mean) / jnp.sqrt(var + EPS)
        yn = yn * gn_w.reshape(1, 1, HEADS, HEAD_DIM) + gn_b.reshape(1, 1, HEADS, HEAD_DIM)
        yn = yn.reshape(bsz, seq, INNER)
        out = yn * jax.nn.silu(z)
        return out @ Wout.T

    def _L0_ffn_ref(x, Wr, br, W_up, b_up, W_down, b_down):
        import jax, jax.numpy as jnp
        import numpy as np
        B, S, H = (4, 512, 256)
        E = 8
        GS = 2
        NG = E // GS
        F = int(H * 4 * (2.0 / 3.0))
        b, s, h = x.shape
        n_tok = b * s
        k = n_tok // E
        xf = x.reshape(n_tok, h)
        logits = xf @ Wr + br
        Sm = jax.nn.softmax(logits, axis=-1)
        G_t, idx_t = jax.lax.top_k(Sm.T, k)
        G = G_t.T
        idx = idx_t.T
        tokens = xf[idx]
        group = jnp.arange(E) // GS
        Wu = W_up[group]
        bu = b_up[group]
        mid = jax.nn.silu(jnp.einsum('keh,ehf->kef', tokens, Wu) + bu)
        out = jnp.einsum('kef,efh->keh', mid, W_down) + b_down
        y = jnp.zeros_like(xf).at[idx].add(G[..., None] * out)
        return y.reshape(b, s, h)
    x = L0_attn_input_tensor
    xn = _layernorm(x, axis=-1)
    s = _L0_attn_ref(xn, L0_attn_Wx, L0_attn_Wz, L0_attn_conv_w, L0_attn_conv_b, L0_attn_Wb, L0_attn_Wc, L0_attn_Wdt, L0_attn_b_dt, L0_attn_log_a, L0_attn_d_param, L0_attn_gn_w, L0_attn_gn_b, L0_attn_Wout)
    g = _silu(_L0_ffn_ref(xn, L0_ffn_Wr, L0_ffn_br, L0_ffn_W_up, L0_ffn_b_up, L0_ffn_W_down, L0_ffn_b_down))
    x = x + s * g
    return x

_drawn_inputs = setup_inputs


def setup_inputs(seed=0):
    import zlib

    import numpy as np

    out = dict(_drawn_inputs(seed))
    spreads = {'L0_attn_conv_b': (0.0, 0.674),
     'L0_attn_b_dt': (0.0, 0.8),
     'L0_attn_log_a': (-0.6931471824645996, 0.6),
     'L0_attn_d_param': (1.0, 0.6),
     'L0_attn_gn_w': (1.0, 0.6),
     'L0_attn_gn_b': (0.0, 0.8),
     'L0_ffn_br': (0.0, 0.8)}
    factors = {'L0_attn_Wx': 8.0,
     'L0_attn_Wz': 6.015,
     'L0_attn_conv_w': 8.0,
     'L0_attn_Wb': 8.0,
     'L0_attn_Wc': 8.0,
     'L0_attn_Wdt': 8.0,
     'L0_attn_Wout': 5.895,
     'L0_ffn_Wr': 6.425,
     'L0_ffn_W_up': 6.367,
     'L0_ffn_b_up': 35.098,
     'L0_ffn_W_down': 5.996,
     'L0_ffn_b_down': 64.0}
    for name, (base, spread) in spreads.items():
        noise = np.random.default_rng([zlib.crc32(name.encode()), seed]).standard_normal(out[name].shape)
        drawn = base * np.exp(spread * noise) if base else spread * noise
        out[name] = jnp.asarray(drawn.astype(out[name].dtype))
    for name, factor in factors.items():
        out[name] = (out[name] * factor).astype(out[name].dtype)
    return out
```

```python
from contextlib import ExitStack

import concourse.bass as bass
from concourse import mybir

F32 = mybir.dt.float32
F32R = mybir.dt.float32r
BF16 = mybir.dt.bfloat16
I32 = mybir.dt.int32
U32 = mybir.dt.uint32
ALU = mybir.AluOpType
ACT = mybir.ActivationFunctionType
AX = mybir.AxisListType

P = 128
BLK = 512
CH = BLK // P
EPS = 1e-5

PRE = 2

C_ID, C_TRI, C_ONES, C_RSUM, C_RTRI, C_IOTA, C_HEAD, C_TAU, C_PIDX, C_LO = (
    0, 128, 256, 384, 512, 640, 768, 896, 960, 961)
C_END = 969


class Shapes:

    def __init__(self, x, wx, wdt, wr, wup):
        self.B, self.L, self.D = x.shape
        self.INNER = wx.shape[1]
        self.KT = self.D // P
        self.MT = self.INNER // P
        self.H = wdt.shape[1]
        self.HD = self.INNER // self.H
        self.E = wr.shape[1]
        self.G, _, self.F = wup.shape
        self.GS = self.E // self.G
        self.FT = -(-self.F // P)
        self.FR = self.F - (self.FT - 1) * P
        self.T = self.B * self.L
        self.NB = self.T // BLK
        self.NT = self.T // P
        self.BPB = self.L // BLK
        self.CAP = self.T // self.E
        self.LW = self.CAP // P
        self.HALF = min(BLK, self.CAP)
        self.NH = self.CAP // self.HALF
        self.HC = self.HALF // P
        self.NSEG = P // self.E
        self.GT = self.NT // self.NSEG
        self.SEG = self.GT * P
        self.ROW = self.D + self.E
        assert self.KT == 2 and self.MT == 4 and self.H == 2 * self.MT and self.HD == 64
        assert self.LW & (self.LW - 1) == 0 and self.BPB % 2 == 0 and self.E == 8 and self.GS == 2


class Tiles:
    pass


def phase_stats(nc, s, t, x_blk, consts):
    with ExitStack() as ctx:
        def sem(name):
            return ctx.enter_context(nc.semaphore(name))

        xin = [ctx.enter_context(nc.sbuf_tensor(f"stat_x{i}", [P, CH, s.D], F32)) for i in range(4)]
        stat6 = ctx.enter_context(nc.sbuf_tensor("stat6", [P, s.NT, 6], F32))
        dmean, var, dev, inv, tmp = (
            ctx.enter_context(nc.sbuf_tensor(f"stat_t{i}", [P, s.NT], F32)) for i in range(5))
        const_loaded = sem("const_loaded")
        x_loaded = [sem(f"stat_x_loaded{i}") for i in range(4)]
        stat_done = sem("stat_done")
        step = sem("stat_step")
        dev_done = sem("dev_done")
        block = ctx.enter_context(nc.Block())

        @block.sync
        def _(sp):
            for i in range(4):
                sp.dma_start(xin[i][:, :, :], x_blk[i]).then_inc(x_loaded[i], 16)
            if s.NB > 4:
                with sp.Fori(1, s.NB // 4) as j:
                    for i in range(4):
                        sp.wait_ge(stat_done, 4 * j + (i - 3))
                        sp.dma_start(xin[i][:, :, :], x_blk[4 * j + i]).then_inc(x_loaded[i], 16)

        @block.gpsimd
        def _(pool):
            for dst, src in consts:
                pool.dma_start(dst, src).then_inc(const_loaded, 16)
            pool.wait_ge(const_loaded, 16 * len(consts))

        @block.vector
        def _(dve):
            with dve.Fori(0, s.NB // 4) as j:
                for i in range(4):
                    dve.wait_ge(x_loaded[i], 16 * j + 16)
                    for c in range(CH):
                        n = nc.vector.bn_stats(stat6[:, 4 * CH * j + (CH * i + c), :], xin[i][:, c, :])
                    n.then_inc(stat_done, 1)
            dve.wait_ge(stat_done, s.NB)
            half_mean = [stat6[:, :, k] for k in (1, 4)]
            half_m2 = [stat6[:, :, k] for k in (2, 5)]
            mean, rstd = t.norm[:, 0, :], t.norm[:, 1, :]
            nc.vector.tensor_tensor(tmp[:, :], half_mean[0], half_mean[1], ALU.add).then_inc(step, 1)
            nc.vector.tensor_tensor(dmean[:, :], half_mean[0], half_mean[1], ALU.subtract).then_inc(step, 1)
            nc.vector.tensor_tensor(var[:, :], half_m2[0], half_m2[1], ALU.add).then_inc(step, 1)
            dve.wait_ge(step, 3)
            nc.vector.tensor_scalar(mean, tmp[:, :], 0.5, None, ALU.mult).then_inc(step, 1)
            nc.vector.scalar_tensor_tensor(dev[:, :], dmean[:, :], 0.25, dmean[:, :], ALU.mult,
                                           ALU.mult).then_inc(step, 1)
            dve.wait_ge(step, 5)
            nc.vector.scalar_tensor_tensor(tmp[:, :], var[:, :], 1.0 / s.D, dev[:, :], ALU.mult,
                                           ALU.add).then_inc(step, 1)
            dve.wait_ge(step, 6)
            nc.vector.tensor_scalar(var[:, :], tmp[:, :], EPS, None, ALU.add).then_inc(step, 1)
            dve.wait_ge(dev_done, 1)
            nc.vector.reciprocal(inv[:, :], dev[:, :]).then_inc(step, 1)
            dve.wait_ge(step, 8)
            nc.vector.tensor_tensor(tmp[:, :], inv[:, :], inv[:, :], ALU.mult).then_inc(step, 1)
            dve.wait_ge(step, 9)
            nc.vector.scalar_tensor_tensor(dmean[:, :], tmp[:, :], -0.5, var[:, :], ALU.mult,
                                           ALU.mult).then_inc(step, 1)
            dve.wait_ge(step, 10)
            nc.vector.scalar_tensor_tensor(rstd, dmean[:, :], 1.5, inv[:, :], ALU.add,
                                           ALU.mult).then_inc(step, 1)

        @block.scalar
        def _(act):
            act.wait_ge(step, 7)
            nc.scalar.activation(dev[:, :], var[:, :], ACT.Sqrt).then_inc(dev_done, 1)


def phase_project(nc, s, t, x_blk):
    KT, MT = s.KT, s.MT
    with ExitStack() as ctx:
        def sem(name):
            return ctx.enter_context(nc.semaphore(name))

        def sb(name, shape, dt=F32):
            return ctx.enter_context(nc.sbuf_tensor(name, shape, dt))

        wx_hi, wx_lo, wz_hi, wz_lo = (sb(f"w{n}", [P, KT, s.INNER], F32R) for n in ("xh", "xl", "zh", "zl"))
        wr2 = sb("wr2", [P, KT, 2, s.E], F32R)
        xin = [sb(f"xin{i}", [P, CH, s.D]) for i in range(2)]
        xn = [sb(f"xn{i}", [P, CH, s.D]) for i in range(2)]
        norm_blk = [sb(f"norm_blk{i}", [P, 2, CH]) for i in range(2)]
        xn_hi = [sb(f"xn_hi{i}", [P, KT, BLK], F32R) for i in range(2)]
        xn_lo = [sb(f"xn_lo{i}", [P, KT, BLK], F32R) for i in range(2)]
        xpre = [sb(f"xpre{m}", [P, 3 + BLK]) for m in range(MT)]
        acc = [sb(f"acc{m}", [P, BLK]) for m in range(MT)]
        x2 = [sb(f"x2a{i}", [P, MT, BLK]) for i in range(2)]
        zs = [sb(f"zsa{i}", [P, MT, BLK]) for i in range(2)]
        ps_t, ps_x, ps_z, ps_lg, ps_dt = t.ps[0:2], t.ps[2:4], t.ps[4:6], t.ps[6], t.ps[7]

        w_hi = sem("a_w_hi")
        w_lo = sem("a_w_lo")
        x_loaded = [sem(f"a_x_loaded{i}") for i in range(2)]
        norm_copied = sem("a_norm_copied")
        xn_ready = sem("a_xn_ready")
        xn_stored = [sem(f"a_xn_stored{i}") for i in range(2)]
        xnT_ready = sem("a_xnT_ready")
        xn_hi_ready = sem("a_xn_hi_ready")
        xn_lo_ready = sem("a_xn_lo_ready")
        x_ready = sem("a_x_ready")
        z_ready = sem("a_z_ready")
        xpre_ready = sem("a_xpre_ready")
        tap0_done = sem("a_tap0_done")
        taps = sem("a_taps")
        conv_done = sem("a_conv_done")
        halo_done = sem("a_halo_done")
        halo_reset = sem("a_halo_reset")
        x2_ready = sem("a_x2_ready")
        zs_ready = sem("a_zs_ready")
        lg_ready = sem("a_lg_ready")
        dt_ready = sem("a_dt_ready")
        lg_copied = sem("a_lg_copied")
        dt_copied = sem("a_dt_copied")
        x2_stored = [sem(f"a_x2_stored{i}") for i in range(2)]
        zs_stored = [sem(f"a_zs_stored{i}") for i in range(2)]
        waited = sem("a_waited")
        block = ctx.enter_context(nc.Block())

        @block.sync
        def _(sp):
            with sp.Fori(0, s.NB // 2) as j:
                for p in range(2):
                    b = 2 * j + p
                    sp.wait_ge(xn_ready, b + (PRE - 1))
                    sp.dma_start(xin[p][:, :, :], x_blk[b]).then_inc(x_loaded[p], 16)
                    sp.wait_ge(xn_ready, b + (PRE + 1))
                    sp.dma_start(t.xn_blk[b], xn[p][:, :, :]).then_inc(xn_stored[p], 16)

        @block.gpsimd
        def _(pool):
            pool.sem_inc(xn_ready, PRE)
            pool.sem_inc(tap0_done, MT * PRE)

            def block_steps(j, p):
                    b = 2 * j + p
                    nc.gpsimd.tensor_copy(norm_blk[p][:, :, :], t.norm[:, :, bass.ds(CH * b, CH)]).then_inc(
                        norm_copied, 1)
                    pool.wait_ge(norm_copied, b + 1)
                    pool.wait_ge(x_loaded[p], 16 * j + 16)
                    pool.wait_ge(xn_stored[p], 16 * j + 16)
                    pool.wait_ge(xnT_ready, KT * b + KT * (PRE - 1))
                    pool.sem_inc(waited, 1)
                    for c in range(CH):
                        n = nc.gpsimd.tensor_scalar(xn[p][:, c, :], xin[p][:, c, :], norm_blk[p][:, 0, c:c + 1],
                                                    norm_blk[p][:, 1, c:c + 1], ALU.subtract, ALU.mult)
                    n.then_inc(xn_ready, 1)
                    for m in range(MT):
                        pool.wait_ge(xpre_ready, MT * b + (MT * PRE + m + 1))
                        pool.wait_ge(x2_ready, MT * b + (MT * (PRE - 1) + m + 1))
                        pool.sem_inc(waited, 1)
                        nc.gpsimd.tensor_scalar(acc[m][:, :], xpre[m][:, 0:BLK], t.cw[:, m, 0:1], t.cb[:, m:m + 1],
                                                ALU.mult, ALU.add).then_inc(tap0_done, 1)

            for bt in range(s.B):
                pool.wait_ge(halo_reset, MT * (bt + 1))
                with pool.Fori(bt * s.BPB // 2, (bt + 1) * s.BPB // 2) as j:
                    for p in range(2):
                        block_steps(j, p)

        @block.scalar
        def _(act):
            for c, n in ((xn_hi_ready, KT * PRE), (xpre_ready, MT * PRE), (x2_ready, MT * PRE),
                         (zs_ready, MT * PRE), (xn_stored[0], 16), (xn_stored[1], 16), (x2_stored[0], 16),
                         (x2_stored[1], 16), (zs_stored[0], 16), (zs_stored[1], 16)):
                act.sem_inc(c, n)
            nc.scalar.activation(wx_hi[:, :, :], t.wx[:, :, :], ACT.Copy).then_inc(w_hi, 1)
            nc.scalar.activation(wz_hi[:, :, :], t.wz[:, :, :], ACT.Copy).then_inc(w_hi, 1)
            nc.scalar.activation(wr2[:, :, 0, :], t.wr[:, :, :], ACT.Copy).then_inc(w_hi, 1)

            def x_out(b, m):
                act.wait_ge(x_ready, MT * b + (MT * PRE + m + 1))
                act.wait_ge(halo_done, MT * b + (MT * (PRE - 1) + m + 1))
                nc.scalar.activation(xpre[m][:, 3:3 + BLK], ps_x[m % 2][:, :], ACT.Copy).then_inc(xpre_ready, 1)

            def x_silu(b, p, m):
                act.wait_ge(conv_done, MT * b + (MT * PRE + m + 1))
                nc.scalar.activation(x2[p][:, m, :], acc[m][:, :], ACT.Silu).then_inc(x2_ready, 1)

            def z_silu(b, p, m):
                act.wait_ge(z_ready, MT * b + (MT * PRE + m + 1))
                nc.scalar.activation(zs[p][:, m, :], ps_z[m % 2][:, :], ACT.Silu).then_inc(zs_ready, 1)

            with act.Fori(0, s.NB // 2) as j:
                for p in range(2):
                    b = 2 * j + p
                    act.wait_ge(z_ready, MT * b + MT * (PRE - 1))
                    for k in range(KT):
                        act.wait_ge(xnT_ready, KT * b + (KT * PRE + k + 1))
                        nc.scalar.activation(xn_hi[p][:, k, :], ps_t[k][:, :], ACT.Copy).then_inc(xn_hi_ready, 1)
                    act.wait_ge(x2_stored[p], 16 * j + 16)
                    act.wait_ge(dt_ready, b + (PRE - 1))
                    act.wait_ge(zs_stored[p], 16 * j + 16)
                    x_out(b, 0)
                    x_out(b, 1)
                    x_out(b, 2)
                    x_silu(b, p, 0)
                    x_out(b, 3)
                    for m in range(1, MT):
                        z_silu(b, p, m - 1)
                        x_silu(b, p, m)
                    z_silu(b, p, MT - 1)
                    act.wait_ge(x2_ready, MT * b + MT * (PRE + 1))
                    act.dma_start(t.x2_dram[b], x2[p][:, :, :]).then_inc(x2_stored[p], 16)
                    act.wait_ge(zs_ready, MT * b + MT * (PRE + 1))
                    act.dma_start(t.zs_dram[b], zs[p][:, :, :]).then_inc(zs_stored[p], 16)
            for p in range(2):
                for c in (xn_stored[p], x2_stored[p], zs_stored[p]):
                    act.wait_ge(c, 16 * (s.NB // 2 + 1))

        @block.vector
        def _(dve):
            for c, n in ((xn_lo_ready, KT * PRE), (conv_done, MT * PRE), (halo_done, MT * PRE),
                         (lg_copied, PRE), (dt_copied, PRE)):
                dve.sem_inc(c, n)
            for n, (lo, raw, hi) in enumerate(((wx_lo[:, :, :], t.wx[:, :, :], wx_hi[:, :, :]),
                                               (wz_lo[:, :, :], t.wz[:, :, :], wz_hi[:, :, :]),
                                               (wr2[:, :, 1, :], t.wr[:, :, :], wr2[:, :, 0, :]))):
                dve.wait_ge(w_hi, n + 1)
                nc.vector.tensor_tensor(lo, raw, hi.bitcast(F32), ALU.subtract).then_inc(w_lo, 1)

            def conv(b, m):
                for k in range(1, 4):
                    if k == 1:
                        dve.wait_ge(tap0_done, MT * b + (MT * PRE + m + 1))
                    else:
                        dve.wait_ge(taps, 2 * MT * b + (2 * m + k - 1))
                    n = nc.vector.scalar_tensor_tensor(acc[m][:, :], xpre[m][:, k:k + BLK], t.cw[:, m, k:k + 1],
                                                       acc[m][:, :], ALU.mult, ALU.add)
                    n.then_inc(taps if k < 3 else conv_done, 1)
                dve.wait_ge(conv_done, MT * b + (MT * PRE + m + 1))
                nc.vector.tensor_copy(xpre[m][:, 0:3], xpre[m][:, BLK:BLK + 3]).then_inc(halo_done, 1)

            def block_steps(j, p):
                b = 2 * j + p
                for k in range(KT):
                    dve.wait_ge(xn_hi_ready, KT * b + (KT * PRE + k + 1))
                    nc.vector.tensor_tensor(xn_lo[p][:, k, :], ps_t[k][:, :], xn_hi[p][:, k, :].bitcast(F32),
                                            ALU.subtract).then_inc(xn_lo_ready, 1)
                for m in range(MT):
                    conv(b, m)
                dve.wait_ge(lg_ready, b + 1)
                nc.vector.tensor_copy(t.logit2[:, bass.ds(CH * b, CH), :, :],
                                      ps_lg[:, 0:CH * 2 * s.E].rearrange("p (c k e) -> p c k e", c=CH, k=2)
                                      ).then_inc(lg_copied, 1)
                dve.wait_ge(dt_ready, b + (PRE + 1))
                nc.vector.tensor_copy(t.dt[:, bass.ds(CH * b, CH), :],
                                      ps_dt[:, 0:CH * s.H].rearrange("p (c h) -> p c h", c=CH)).then_inc(dt_copied, 1)

            for bt in range(s.B):
                if bt:
                    dve.wait_ge(halo_done, MT * (bt * s.BPB + PRE))
                for m in range(MT):
                    n = nc.vector.memset(xpre[m][:, 0:3], 0.0)
                    n.then_inc(halo_reset, 1)
                dve.wait_ge(halo_reset, MT * (bt + 1))
                with dve.Fori(bt * s.BPB // 2, (bt + 1) * s.BPB // 2) as j:
                    for p in range(2):
                        block_steps(j, p)

        @block.tensor
        def _(pe):
            for c, n in ((xnT_ready, KT * PRE), (x_ready, MT * PRE), (z_ready, MT * PRE), (dt_ready, PRE)):
                pe.sem_inc(c, n)
            pe.wait_ge(w_lo, 3)

            def project(b, p, m, w, ps, ready, drained):
                pe.wait_ge(drained, MT * b + (MT * PRE + m - 2 + 1))
                n = 0
                for k in range(KT):
                    for wgt, act_in in ((w[0], xn_hi[p]), (w[1], xn_hi[p]), (w[0], xn_lo[p])):
                        if m == 0 and ready is x_ready:
                            pe.wait_ge(xn_hi_ready if act_in is xn_hi[p] else xn_lo_ready,
                                       KT * b + (KT * PRE + k + 1))
                        mm = pe.matmul(ps[m % 2][:, :], wgt[:, k, m * P:(m + 1) * P], act_in[:, k, :],
                                       start=(n == 0), stop=(n == 3 * KT - 1))
                        n += 1
                mm.then_inc(ready, 1)

            with pe.Fori(0, s.NB // 2) as j:
                for p in range(2):
                    b = 2 * j + p
                    pe.wait_ge(xn_ready, b + (PRE + 1))
                    for k in range(KT):
                        pe.wait_ge(xn_lo_ready, KT * b + (KT * (PRE - 1) + k + 1))
                        for c in range(CH):
                            mm = pe.transpose(ps_t[k][:, c * P:(c + 1) * P], xn[p][:, c, k * P:(k + 1) * P], t.ident)
                        mm.then_inc(xnT_ready, 1)
                    for m in range(MT):
                        project(b, p, m, (wx_hi, wx_lo), ps_x, x_ready, xpre_ready)
                    pe.wait_ge(lg_copied, b + PRE)
                    for c in range(CH):
                        for n, (k, half) in enumerate((k, half) for k in range(KT) for half in (xn_hi[p], xn_lo[p])):
                            mm = pe.matmul(ps_lg[:, c * 2 * s.E:(c + 1) * 2 * s.E], half[:, k, c * P:(c + 1) * P],
                                           wr2[:, k, :, :], start=(n == 0), stop=(n == 2 * KT - 1))
                    mm.then_inc(lg_ready, 1)
                    for m in range(MT):
                        project(b, p, m, (wz_hi, wz_lo), ps_z, z_ready, zs_ready)
                    pe.wait_ge(dt_copied, b + PRE)
                    pe.wait_ge(x2_ready, MT * b + MT * (PRE + 1))
                    for c in range(CH):
                        for k in range(MT):
                            mm = pe.matmul(ps_dt[:, c * s.H:(c + 1) * s.H], x2[p][:, k, c * P:(c + 1) * P],
                                           t.wdt[:, k, :], start=(k == 0), stop=(k == MT - 1))
                    mm.then_inc(dt_ready, 1)


def phase_route(nc, s, t):
    NT, E, H, LW, GT, SEG = s.NT, s.E, s.H, s.LW, s.GT, s.SEG
    with ExitStack() as ctx:
        def sem(name):
            return ctx.enter_context(nc.semaphore(name))

        def sb(name, shape, dt=F32):
            return ctx.enter_context(nc.sbuf_tensor(name, shape, dt))

        u, e1, w1, ln, q, z, rec, dta, gap, ecum, wexp, dec8, lsum = (
            sb(f"r_{n}", [P, NT, 8]) for n in ("u", "e1", "w1", "ln", "q", "z", "rec", "dta", "gap", "ecum",
                                               "wexp", "dec8", "lsum"))
        a_pos = sb("r_a_pos", [P, 1, 8])
        top, esum, einv = (sb(f"r_{n}", [P, NT, 1]) for n in ("top", "esum", "einv"))
        gates_g = sb("r_gates_g", [P, GT, s.NSEG, E])
        rowsT = sb("rowsT", [P, 2, GT, P])
        gateT, junk, sel, eq, cumc, ones_row, keep, slot = (
            sb(f"r_{n}", [P, SEG]) for n in ("gateT", "junk", "sel", "eq", "cumc", "ones_row", "keep", "slot"))
        thr, cand, bit_i, delta = (sb(f"r_{n}", [P, 1], I32) for n in ("thr", "cand", "bit_i", "delta"))
        bit_f, part, lim, lim2 = (sb(f"r_{n}", [P, 1]) for n in ("bit_f", "part", "lim", "lim2"))
        counts = sb("counts", [P, 4])
        slot_i, hi_i, lo_i = (sb(f"r_{n}", [P, NT, E], I32) for n in ("slot_i", "hi_i", "lo_i"))
        hi, lo = (sb(f"r_{n}", [P, NT, E]) for n in ("hi", "lo"))
        iota_b = sb("iota_b", [P, P], BF16)
        one_hi = [sb(f"one_hi{i}", [P, E, P], BF16) for i in range(2)]
        one_lo = [sb(f"one_lo{i}", [P, E, LW]) for i in range(2)]
        val_lo = [sb(f"val_lo{i}", [P, E, 2, LW], BF16) for i in range(2)]
        zero_b = sb("zero_b", [P, P], BF16)
        lists = sb("lists", [P, E, 2, LW])
        idx_f = sb("idx_f", [P, E, LW])
        zero = sb("zero", [P, 8, s.D])
        ps = t.ps

        vec, sca, ten = sem("r_vec"), sem("r_sca"), sem("r_ten")
        zeroed = sem("r_zeroed")
        stored = sem("r_stored")
        part_done, total_done, thr_done, cand_done = (sem(f"r_{n}") for n in ("part", "total", "thr", "cand"))
        delta_done = sem("r_delta")
        lo_done, tile_done, tile_used = (sem(f"r_{n}") for n in ("lo", "tile", "used"))
        block = ctx.enter_context(nc.Block())

        def wide(ap, shape):
            return ap.to_broadcast(shape)

        steps = {}

        @block.vector
        def _(dve):
            n = [0]

            def do(ins, name=None):
                n[0] += 1
                ins.then_inc(vec, 1)
                dve.wait_ge(vec, n[0])
                if name:
                    assert steps.setdefault(name, n[0]) == n[0]

            full = [P, NT, 8]
            v = nc.vector
            do(v.tensor_tensor(u[:, :, :], t.dt[:, :, :], wide(t.rows[:, 1:2, :], full), ALU.add), "u")
            dve.wait_ge(sca, 3)
            do(v.tensor_scalar(w1[:, :, :], e1[:, :, :], 1.0, None, ALU.add), "w1")
            do(v.tensor_scalar(q[:, :, :], w1[:, :, :], -1.0, None, ALU.add))
            do(v.scalar_tensor_tensor(z[:, :, :], q[:, :, :], 0.0, e1[:, :, :], ALU.is_equal, ALU.mult))
            do(v.tensor_scalar(gap[:, :, :], q[:, :, :], 1e-30, None, ALU.max))
            do(v.reciprocal(rec[:, :, :], gap[:, :, :]))
            do(v.tensor_tensor(q[:, :, :], rec[:, :, :], e1[:, :, :], ALU.mult))
            dve.wait_ge(sca, 4)
            do(v.tensor_tensor(rec[:, :, :], q[:, :, :], ln[:, :, :], ALU.mult))
            do(v.tensor_tensor(q[:, :, :], rec[:, :, :], z[:, :, :], ALU.add))
            do(v.scalar_tensor_tensor(t.dt[:, :, :], u[:, :, :], 0.0, q[:, :, :], ALU.max, ALU.add))
            do(v.scalar_tensor_tensor(dta[:, :, :], t.dt[:, :, :], -1.0, wide(a_pos[:, :, :], full), ALU.mult,
                                      ALU.mult), "dta")
            dve.wait_ge(ten, 2)
            psc = [ps[i][:, 0:NT * H].rearrange("p (t h) -> p t h", h=H) for i in range(2)]
            do(v.tensor_copy(t.cum[:, :, :], psc[0]), "cum")
            do(v.tensor_tensor(gap[:, :, :], psc[1], t.cum[:, :, :], ALU.subtract), "gap")
            dve.wait_ge(sca, 7)
            do(v.tensor_tensor(t.wst[:, :, :], wexp[:, :, :], t.dt[:, :, :], ALU.mult))
            for a in range(2):
                half = slice(a * s.HD, (a + 1) * s.HD)
                do(v.tensor_copy(t.dec[half, :, :], dec8[half, :, a:8:2]))
            dve.wait_ge(ten, 4)
            for i in range(2):
                do(v.tensor_copy(rowsT[:, i, :, :], ps[2 + i][:, 0:GT * P].rearrange("p (g c) -> p g c", g=GT)),
                   f"rows{i}")
            do(v.tensor_tensor(lsum[:, :, :], t.logit2[:, :, 0, :], t.logit2[:, :, 1, :], ALU.add))
            do(v.tensor_tensor(u[:, :, :], lsum[:, :, :], wide(t.rows[:, 2:3, :], full), ALU.add))
            do(v.tensor_reduce(top[:, :, :], u[:, :, :], AX.X, ALU.max))
            do(v.tensor_tensor(lsum[:, :, :], u[:, :, :], wide(top[:, :, :], full), ALU.subtract), "shifted")
            dve.wait_ge(sca, 8)
            do(v.tensor_reduce(esum[:, :, :], ecum[:, :, :], AX.X, ALU.add))
            do(v.reciprocal(einv[:, :, :], esum[:, :, :]))
            do(v.tensor_tensor(t.gates[:, :, :], ecum[:, :, :], wide(einv[:, :, :], full), ALU.mult), "gates")
            do(v.tensor_copy(gates_g[:, :, :, :], t.gates[:, :, :].rearrange("p (q g) e -> p g q e", g=GT)), "gates_g")
            do(v.memset(ones_row[:, :], 1.0))
            do(v.memset(zero_b[:, :], 0.0), "zero_b")
            do(v.tensor_copy(iota_b[:, :], t.iota))
            dve.wait_ge(ten, 5)
            do(v.tensor_copy(gateT[:, :], ps[4][:, 0:SEG]))
            do(v.memset(thr[:, :], 0))
            do(v.memset(bit_f[:, :], float(1 << 29)))
            do(v.tensor_copy(bit_i[:, :], bit_f[:, :]))
            with dve.Fori(0, 30) as i:
                v.tensor_tensor(cand[:, :], thr[:, :], bit_i[:, :], ALU.bitwise_or).then_inc(cand_done, 1)
                dve.wait_ge(cand_done, i + 1)
                v.tensor_scalar(junk[:, :], gateT[:, :], cand[:, :].bitcast(F32), 0.0, ALU.is_ge, ALU.add,
                                accum_out=part[:, :]).then_inc(part_done, 1)
                dve.wait_ge(total_done, i + 1)
                v.tensor_scalar(delta[:, :], ps[5][:, 0:1], float(s.CAP), bit_f[:, :], ALU.is_ge,
                                ALU.mult).then_inc(delta_done, 1)
                dve.wait_ge(delta_done, i + 1)
                v.tensor_tensor(thr[:, :], thr[:, :], delta[:, :], ALU.bitwise_or).then_inc(thr_done, 1)
                v.tensor_scalar(bit_f[:, :], bit_f[:, :], 0.5, None, ALU.mult).then_inc(thr_done, 1)
                dve.wait_ge(thr_done, 3 * i + 2)
                v.tensor_copy(bit_i[:, :], bit_f[:, :]).then_inc(thr_done, 1)
                dve.wait_ge(thr_done, 3 * i + 3)
            tf = thr[:, :].bitcast(F32)
            do(v.tensor_scalar(sel[:, :], gateT[:, :], tf, 0.0, ALU.is_gt, ALU.add, accum_out=counts[:, 0:1]))
            do(v.tensor_scalar(eq[:, :], gateT[:, :], tf, 0.0, ALU.is_equal, ALU.add, accum_out=counts[:, 1:2]),
               "counts")
            do(v.tensor_tensor_scan(cumc[:, :], ones_row[:, :], eq[:, :], 0.0, ALU.mult, ALU.add))
            dve.wait_ge(ten, 6)
            do(v.tensor_scalar(lim[:, :], ps[6][:, 0:1], -1.0, float(s.CAP), ALU.mult, ALU.add))
            do(v.tensor_tensor(lim2[:, :], ps[6][:, 1:2], lim[:, :], ALU.subtract))
            do(v.tensor_scalar(lim[:, :], lim2[:, :], -1.0, None, ALU.mult))
            do(v.scalar_tensor_tensor(keep[:, :], cumc[:, :], lim[:, :], eq[:, :], ALU.is_le, ALU.mult))
            do(v.tensor_tensor(junk[:, :], sel[:, :], keep[:, :], ALU.add))
            do(v.tensor_tensor_scan(cumc[:, :], ones_row[:, :], junk[:, :], 0.0, ALU.mult, ALU.add))
            do(v.tensor_copy(counts[:, 2:3], cumc[:, SEG - 1:SEG]), "selected")
            dve.wait_ge(ten, 7)
            do(v.tensor_scalar(lim2[:, :], ps[6][:, 2:3], 0.0, None, ALU.add))
            do(v.scalar_tensor_tensor(keep[:, :], cumc[:, :], lim2[:, :], junk[:, :], ALU.add, ALU.mult))
            do(v.tensor_scalar(slot[:, :], keep[:, :], -1.0, None, ALU.add), "slot")
            dve.wait_ge(ten, 8)
            do(v.tensor_copy(slot_i[:, :, :].rearrange("p (q g) e -> p g q e", g=GT),
                             ps[4][:, 0:SEG].rearrange("p (g q e) -> p g q e", g=GT, e=E)))
            do(v.tensor_scalar(hi_i[:, :, :], slot_i[:, :, :], LW.bit_length() - 1, None, ALU.arith_shift_right))
            do(v.tensor_scalar(lo_i[:, :, :], slot_i[:, :, :], LW - 1, None, ALU.bitwise_and))
            do(v.tensor_copy(hi[:, :, :], hi_i[:, :, :]))
            do(v.tensor_copy(lo[:, :, :], lo_i[:, :, :]))
            dve.sem_inc(tile_used, 0 + 2)
            with dve.Fori(0, NT // 2) as j:
                for p in range(2):
                    i = 2 * j + p
                    dve.wait_ge(tile_used, i + 1)
                    v.tensor_tensor(one_lo[p][:, :, :], lo[:, bass.ds(i, 1), :].rearrange("p a e -> p e a")
                                    .to_broadcast([P, E, LW]),
                                    t.cst[:, C_LO:C_LO + LW].unsqueeze(1).to_broadcast([P, E, LW]),
                                    ALU.is_equal).then_inc(lo_done, 1)
                    for e in range(E):
                        v.tensor_scalar(one_hi[p][:, e, :], iota_b[:, :],
                                        hi[:, bass.ds(i, 1), e:e + 1].rearrange("p a e -> p (a e)"), None,
                                        ALU.is_equal)
                    dve.wait_ge(lo_done, i + 1)
                    v.tensor_scalar(val_lo[p][:, :, 0, :], one_lo[p][:, :, :], t.cst[:, bass.ds(C_TAU + i, 1)],
                                    None, ALU.mult)
                    v.tensor_scalar(val_lo[p][:, :, 1, :], one_lo[p][:, :, :], t.cst[:, C_PIDX:C_PIDX + 1],
                                    None, ALU.mult).then_inc(tile_done, 1)
            dve.wait_ge(ten, 9)
            do(v.tensor_copy(lists[:, :, :, :], ps[7][:, 0:2 * E * LW].rearrange("p (e k l) -> p e k l", e=E, k=2)))
            do(v.scalar_tensor_tensor(idx_f[:, :, :], lists[:, :, 0, :], float(P), lists[:, :, 1, :], ALU.mult,
                                      ALU.add))
            do(v.tensor_copy(t.idx[:, :, :], idx_f[:, :, :]))

        @block.scalar
        def _(act):
            nc.scalar.activation(a_pos[:, :, :], t.rows[:, 0:1, :], ACT.Exp).then_inc(sca, 1)
            act.wait_ge(vec, steps["u"])
            nc.scalar.activation(gap[:, :, :], u[:, :, :], ACT.Abs).then_inc(sca, 1)
            act.wait_ge(sca, 2)
            nc.scalar.activation(e1[:, :, :], gap[:, :, :], ACT.Exp, scale=-1.0).then_inc(sca, 1)
            act.wait_ge(vec, steps["w1"])
            nc.scalar.activation(ln[:, :, :], w1[:, :, :], ACT.Ln).then_inc(sca, 1)
            act.wait_ge(vec, steps["cum"])
            nc.scalar.activation(ecum[:, :, :], t.cum[:, :, :], ACT.Exp).then_inc(sca, 1)
            act.wait_ge(vec, steps["gap"])
            nc.scalar.activation(wexp[:, :, :], gap[:, :, :], ACT.Exp).then_inc(sca, 1)
            nc.scalar.activation(dec8[:, :, :], ps[1][:, 0:NT * H].rearrange("p (t h) -> p t h", h=H),
                                 ACT.Exp).then_inc(sca, 1)
            act.wait_ge(vec, steps["shifted"])
            act.wait_ge(ten, 4)
            nc.scalar.activation(ecum[:, :, :], lsum[:, :, :], ACT.Exp).then_inc(sca, 1)

        @block.tensor
        def _(pe):
            pe.wait_ge(vec, steps["dta"])
            flat = dta[:, :, :].rearrange("p t h -> p (t h)")
            pe.matmul(ps[0][:, 0:NT * H], t.tri, flat, start=True, stop=True).then_inc(ten, 1)
            pe.matmul(ps[1][:, 0:NT * H], t.ones, flat, start=True, stop=True).then_inc(ten, 1)
            for i, (src, ready, n) in enumerate(((t.cum, vec, steps["cum"]), (ecum, sca, 5))):
                pe.wait_ge(ready, n)
                for g in range(GT):
                    mm = pe.transpose(ps[2 + i][:, g * P:(g + 1) * P],
                                      src[:, g * s.NSEG:(g + 1) * s.NSEG, :].rearrange("p t h -> p (t h)"), t.ident)
                mm.then_inc(ten, 1)
            pe.wait_ge(vec, steps["gates_g"])
            for g in range(GT):
                mm = pe.transpose(ps[4][:, g * P:(g + 1) * P],
                                  gates_g[:, g, :, :].rearrange("p q e -> p (q e)"), t.ident)
            mm.then_inc(ten, 1)
            with pe.Fori(0, 30) as i:
                pe.wait_ge(part_done, i + 1)
                pe.matmul(ps[5][:, 0:1], t.rsum, part[:, :], start=True, stop=True).then_inc(total_done, 1)
            pe.wait_ge(vec, steps["counts"])
            pe.matmul(ps[6][:, 0:1], t.rsum, counts[:, 0:1], start=True, stop=True)
            pe.matmul(ps[6][:, 1:2], t.rtri, counts[:, 1:2], start=True, stop=True).then_inc(ten, 1)
            pe.wait_ge(vec, steps["selected"])
            pe.matmul(ps[6][:, 2:3], t.rtri, counts[:, 2:3], start=True, stop=True).then_inc(ten, 1)
            pe.wait_ge(vec, steps["slot"])
            for g in range(GT):
                mm = pe.transpose(ps[4][:, g * P:(g + 1) * P], slot[:, g * P:(g + 1) * P], t.ident)
            mm.then_inc(ten, 1)
            W = 2 * E * LW
            pe.matmul(ps[7][:, 0:W], zero_b[:, :], zero_b[:, 0:W], start=True, stop=False, skip_group_check=True)
            with pe.Fori(0, NT // 2) as j:
                for p in range(2):
                    pe.wait_ge(tile_done, 2 * j + (p + 1))
                    for e in range(E):
                        mm = pe.matmul(ps[7][:, e * 2 * LW:(e + 1) * 2 * LW], one_hi[p][:, e, :],
                                       val_lo[p][:, e, :, :].rearrange("p k l -> p (k l)"),
                                       start=False, stop=False, skip_group_check=True)
                    mm.then_inc(tile_used, 1)
            pe.matmul(ps[7][:, 0:W], zero_b[:, :], zero_b[:, 0:W], start=False, stop=True,
                      skip_group_check=True).then_inc(ten, 1)

        @block.gpsimd
        def _(pool):
            nc.gpsimd.memset(zero[:, :, :], 0.0).then_inc(zeroed, 1)

        @block.sync
        def _(sp):
            sp.wait_ge(vec, steps["rows1"])
            for i, dst in enumerate((t.cum_dram, t.ecum_dram)):
                sp.dma_start(dst.rearrange("(g t) h c -> (t h) g c", t=s.NSEG), rowsT[:, i, :, :]).then_inc(stored, 16)
            sp.wait_ge(vec, steps["gates"])
            sp.dma_start(t.rows_dram[:, s.D:s.ROW].rearrange("(t p) e -> p t e", p=P), t.gates[:, :, :]).then_inc(
                stored, 16)
            sp.wait_ge(zeroed, 1)
            for k in range(s.T // (8 * P)):
                sp.dma_start(t.ffn_dram[8 * P * k:8 * P * (k + 1), :].rearrange("(p c) d -> p c d", p=P),
                             zero[:, :, :]).then_inc(stored, 16)
            sp.wait_ge(stored, 16 * (3 + s.T // (8 * P)))


def phase_scan(nc, s, t, wb_d, wc_d):
    MT, H, HD, NB = s.MT, s.H, s.HD, s.NB
    CPRE = PRE * CH
    with ExitStack() as ctx:
        def sem(name):
            return ctx.enter_context(nc.semaphore(name))

        def sb(name, shape, dt=F32):
            return ctx.enter_context(nc.sbuf_tensor(name, shape, dt))

        w_raw = sb("b_w_raw", [P, 2, s.INNER])
        wb_hi, wb_lo, wc_hi, wc_lo = (sb(f"w{n}", [P, MT, s.INNER], F32R) for n in ("bh", "bl", "ch", "cl"))
        x2 = [sb(f"x2_{i}", [P, MT, BLK]) for i in range(2)]
        x_raw = [sb(f"x_raw{i}", [P, BLK]) for i in range(2)]
        x_hi = [sb(f"x_hi{i}", [P, MT, BLK], F32R) for i in range(2)]
        x_lo = [sb(f"x_lo{i}", [P, MT, BLK], F32R) for i in range(2)]
        bT = [sb(f"bT{i}", [P, MT, BLK]) for i in range(2)]
        cT = [sb(f"cT{i}", [P, MT, BLK]) for i in range(2)]
        cum_row = [sb(f"cum_row{i}", [P, H, P]) for i in range(2)]
        ecum_row = [sb(f"ecum_row{i}", [P, MT, P]) for i in range(2)]
        decay = sb("decay", [P, H, P])
        mix = sb("mix", [P, H, P])
        b_tok = sb("b_tok", [P, s.INNER])
        x_dt = sb("x_dt", [P, MT, 2, P])
        x_w = sb("x_w", [P, s.INNER])
        c_dec = sb("c_dec", [P, MT, P])
        state = sb("state", [P, MT, P])
        dx = sb("dx", [P, MT, BLK])
        yb = [sb(f"yb{i}", [P, MT, BLK]) for i in range(2)]
        ps_g, ps_y, ps_s, ps_x, ps_b, ps_pb, ps_pc = (t.ps[0:2], t.ps[2], t.ps[3], t.ps[4], t.ps[5], t.ps[6],
                                                      t.ps[7])

        w_loaded, w_hi, w_lo, zeroed = sem("b_w_loaded"), sem("b_w_hi"), sem("b_w_lo"), sem("b_zeroed")
        state_zeroed = sem("b_state_zeroed")
        x2_loaded = [sem(f"b_x2_loaded{i}") for i in range(2)]
        raw_loaded = [sem(f"b_raw_loaded{i}") for i in range(2)]
        cum_loaded = [sem(f"b_cum_loaded{i}") for i in range(2)]
        ecum_loaded = [sem(f"b_ecum_loaded{i}") for i in range(2)]
        y_stored = [sem(f"b_y_stored{i}") for i in range(2)]
        waited = sem("b_waited")
        dx_ready, stat_done = sem("b_dx"), sem("b_stat")
        x_hi_ready, x_lo_ready, b_ready, c_ready, b_out, c_out = (
            sem(f"b_{n}") for n in ("x_hi", "x_lo", "b_ready", "c_ready", "b_out", "c_out"))
        x_turned, b_turned, b_tok_ready, g_ready, c_dec_ready, x_dt_ready, x_w_ready = (
            sem(f"b_{n}") for n in ("xt", "bt", "btok", "g", "cdec", "xdt", "xw"))
        gap_ready, exp_ready, decay_ready, mix_ready, y_mm, s_mm, y_ready, state_scaled, state_ready = (
            sem(f"b_{n}") for n in ("gap", "exp", "decay", "mix", "ymm", "smm", "y", "sscaled", "state"))
        block = ctx.enter_context(nc.Block())

        def at(g, back=0):
            return g + (1 + CPRE - back)

        def run(eng, body):
            for bt in range(s.B):
                body_start = bt * s.BPB // 2
                body_end = (bt + 1) * s.BPB // 2 - (1 if bt == s.B - 1 else 0)
                body(bt, None, 0, False, False)
                if body_end > body_start:
                    with eng.Fori(body_start, body_end) as j:
                        for p in range(2):
                            body(bt, 2 * j + p, p, True, True)
            for p in range(2):
                body(None, NB - 2 + p, p, p == 0, False)

        def half_value(b, p, per_pair):
            return (b - p) * (8 * per_pair) + 16 * per_pair

        @block.sync
        def _(sp):
            for n, w in enumerate((wb_d, wb_d, wc_d, wc_d)):
                if n:
                    sp.wait_ge(w_lo, n)
                sp.dma_start(w_raw[:, :, :], w.rearrange("(k p) n -> p k n", p=P)[:, 2 * (n % 2):2 * (n % 2) + 2, :]
                             ).then_inc(w_loaded, 16)

            def load_raw(b, m):
                sp.wait_ge(x_lo_ready, MT * b + (m - 2 + 1 + CPRE))
                sp.dma_start(x_raw[m % 2][:, :], t.x2_dram[b][:, m, :]).then_inc(raw_loaded[m % 2], 16)

            def load_cum(g, q):
                sp.wait_ge(gap_ready, at(g, 2))
                sp.dma_start(cum_row[q][:, :, :], t.cum_dram[g].partition_broadcast(P)).then_inc(cum_loaded[q], 16)

            def load_ecum(g, q):
                sp.wait_ge(c_dec_ready, at(g, 2))
                for a in range(2):
                    sp.dma_start(ecum_row[q][a * HD:(a + 1) * HD, :, :],
                                 t.ecum_dram[g].rearrange("(m a) c -> a m c", a=2)[a].partition_broadcast(HD)
                                 ).then_inc(ecum_loaded[q], 16)

            def body(bt, b, p, nxt, nxt2):
                if b is None:
                    return
                sp.wait_ge(dx_ready, b + (PRE - 1))
                sp.wait_ge(x_turned, at(CH * b, CH + 1))
                sp.dma_start(x2[p][:, :, :], t.x2_dram[b]).then_inc(x2_loaded[p], 16)
                for c in range(CH):
                    g = CH * b + c
                    load_ecum(g, c % 2)
                    if c < CH - 1 or nxt:
                        load_cum(g + 1, (c + 1) % 2)
                    if nxt2:
                        load_raw(b + 2, c)
                sp.wait_ge(stat_done, b + (PRE + 1))
                sp.dma_start(t.y_dram[b], yb[p][:, :, :]).then_inc(y_stored[p], 16)

            for b in range(2):
                for m in range(MT):
                    load_raw(b, m)
            load_cum(0, 0)
            run(sp, body)
            for p in range(2):
                sp.wait_ge(y_stored[p], 16 * (NB // 2 + 1))

        @block.gpsimd
        def _(pool):
            pool.sem_inc(dx_ready, PRE)
            pool.sem_inc(decay_ready, CPRE)
            nc.gpsimd.memset(x_dt[:, :, :, :], 0.0).then_inc(zeroed, 1)

            def causal(g):
                pool.wait_ge(exp_ready, at(g))
                pool.sem_inc(waited, 1)
                nc.gpsimd.affine_select(out=decay[:, :, :], in_=decay[:, :, :], compare_op=ALU.is_ge, fill=0.0,
                                        base=0, pattern=[[0, H], [1, P]], channel_multiplier=-1).then_inc(
                    decay_ready, 1)

            def body(bt, b, p, nxt, nxt2):
                if b is None:
                    return
                pool.wait_ge(x2_loaded[p], half_value(b, p, 1))
                pool.wait_ge(y_ready, at(CH * b, 1))
                pool.sem_inc(waited, 1)
                for m in range(MT):
                    n = nc.gpsimd.tensor_scalar(dx[:, m, :], x2[p][:, m, :], t.dcol[:, m:m + 1], None, ALU.mult)
                n.then_inc(dx_ready, 1)
                for c in range(CH):
                    if c < CH - 1 or nxt:
                        causal(CH * b + (c + 1))

            causal(0)
            run(pool, body)

        @block.scalar
        def _(act):
            for c in (exp_ready, b_out, c_out, b_tok_ready, x_hi_ready):
                act.sem_inc(c, CPRE)
            for n, hi in enumerate((wb_hi, wb_hi, wc_hi, wc_hi)):
                act.wait_ge(w_loaded, 16 * (n + 1))
                nc.scalar.activation(hi[:, 2 * (n % 2):2 * (n % 2) + 2, :], w_raw[:, :, :], ACT.Copy).then_inc(w_hi, 1)

            def hi_part(b, p, m, loaded):
                act.wait_ge(raw_loaded[m % 2], loaded)
                act.wait_ge(c_ready, MT * b + (MT * (PRE - 1)))
                nc.scalar.activation(x_hi[p][:, m, :], x_raw[m % 2][:, :], ACT.Copy).then_inc(x_hi_ready, 1)

            def bc_part(b, p, m):
                act.wait_ge(b_ready, MT * b + (m + 1 + CPRE))
                nc.scalar.activation(bT[p][:, m, :], ps_pb[:, :], ACT.Copy).then_inc(b_out, 1)
                act.wait_ge(c_ready, MT * b + (m + 1 + CPRE))
                nc.scalar.activation(cT[p][:, m, :], ps_pc[:, :], ACT.Copy).then_inc(c_out, 1)

            def decays(g):
                act.wait_ge(gap_ready, at(g))
                nc.scalar.activation(decay[:, :, :], decay[:, :, :], ACT.Exp).then_inc(exp_ready, 1)

            def body(bt, b, p, nxt, nxt2):
                if b is None:
                    return
                for c in range(CH):
                    g = CH * b + c
                    act.wait_ge(b_turned, at(g))
                    act.wait_ge(s_mm, at(g, 1))
                    nc.scalar.activation(b_tok[:, :], ps_b[:, :], ACT.Copy).then_inc(b_tok_ready, 1)
                    if nxt:
                        bc_part(b + 1, 1 - p, c)
                    if nxt2:
                        hi_part(b + 2, p, c, b * 32 + (16 * (4 + c // 2 + 1)))
                    if c < CH - 1 or nxt:
                        decays(g + 1)

            for b in range(2):
                for m in range(MT):
                    hi_part(b, b, m, 16 * (2 * b + m // 2 + 1))
            for m in range(MT):
                bc_part(0, 0, m)
            decays(0)
            run(act, body)

        @block.vector
        def _(dve):
            v = nc.vector
            for c, n in ((x_lo_ready, CPRE), (gap_ready, CPRE), (c_dec_ready, CPRE), (x_dt_ready, CPRE),
                         (x_w_ready, CPRE), (mix_ready, 2 * CPRE), (y_ready, CPRE), (state_ready, 2 * CPRE),
                         (stat_done, PRE), (y_stored[0], 16), (y_stored[1], 16)):
                dve.sem_inc(c, n)
            for n, (hi, lo) in enumerate(((wb_hi, wb_lo), (wb_hi, wb_lo), (wc_hi, wc_lo), (wc_hi, wc_lo))):
                dve.wait_ge(w_hi, n + 1)
                k = slice(2 * (n % 2), 2 * (n % 2) + 2)
                v.tensor_tensor(lo[:, k, :], w_raw[:, :, :], hi[:, k, :].bitcast(F32), ALU.subtract).then_inc(w_lo, 1)

            def lo_part(b, p, m):
                dve.wait_ge(x_hi_ready, MT * b + (m + 1 + CPRE))
                v.tensor_tensor(x_lo[p][:, m, :], x_raw[m % 2][:, :], x_hi[p][:, m, :].bitcast(F32),
                                ALU.subtract).then_inc(x_lo_ready, 1)

            def gaps(g, q, loaded):
                dve.wait_ge(cum_loaded[q], loaded)
                dve.wait_ge(mix_ready, 2 * g + 2 * CPRE)
                for h in range(H):
                    n = v.tensor_scalar(decay[:, (h % 2) * MT + h // 2, :], cum_row[q][:, h, :],
                                        t.cum[:, bass.ds(g, 1), h:h + 1].rearrange("p a b -> p (a b)"), 0.0,
                                        ALU.subtract, ALU.min)
                n.then_inc(gap_ready, 1)

            def heads(ap, g):
                return ap[:, bass.ds(g, 1), :].rearrange("p a h -> p h a").to_broadcast([P, H, HD])

            def body(bt, b, p, nxt, nxt2):
                if b is None:
                    dve.wait_ge(s_mm, CH * bt * s.BPB + CPRE)
                    dve.wait_ge(state_ready, 2 * CH * bt * s.BPB + 2 * CPRE)
                    v.memset(state[:, :, :], 0.0).then_inc(state_zeroed, 1)
                    dve.wait_ge(state_zeroed, bt + 1)
                    return
                dve.wait_ge(y_stored[p], half_value(b, p, 1))
                for c in range(CH):
                    g = CH * b + c
                    cols = slice(c * P, (c + 1) * P)
                    dve.wait_ge(c_out, CH * b + CPRE + CH)
                    dve.wait_ge(ecum_loaded[c % 2], (b - 0) * 64 + (32 * (c // 2 + 1)))
                    dve.wait_ge(y_mm, at(g, 1))
                    v.tensor_tensor(c_dec[:, :, :], cT[p][:, :, cols], ecum_row[c % 2][:, :, :],
                                    ALU.mult).then_inc(c_dec_ready, 1)
                    dve.wait_ge(x_turned, at(g))
                    x_heads = ps_x[:, :].rearrange("p (h n) -> p h n", h=H)
                    for a in range(2):
                        n = v.tensor_tensor(x_dt[:, :, a, a * HD:(a + 1) * HD], x_heads[:, a:H:2, :],
                                            heads(t.dt, g)[:, a:H:2, :], ALU.mult)
                    n.then_inc(x_dt_ready, 1)
                    dve.wait_ge(s_mm, at(g, 1))
                    v.tensor_tensor(x_w[:, :].rearrange("p (h n) -> p h n", h=H), x_heads, heads(t.wst, g),
                                    ALU.mult).then_inc(x_w_ready, 1)
                    dve.wait_ge(decay_ready, at(g))
                    for i in range(2):
                        dve.wait_ge(g_ready, g + 1)
                        v.tensor_tensor(mix[:, 4 * i:4 * i + 4, :],
                                        ps_g[i][:, :].rearrange("p (h n) -> p h n", h=4),
                                        decay[:, 4 * i:4 * i + 4, :], ALU.mult).then_inc(mix_ready, 1)
                    if c < CH - 1 or nxt:
                        q = (c + 1) % 2
                        gaps(g + 1, q, (b - 0) * 32 + (16 * ((c + 1) // 2 + 1)))
                    if nxt2:
                        lo_part(b + 2, p, c)
                    dve.wait_ge(y_mm, at(g))
                    if c == 0:
                        dve.wait_ge(dx_ready, b + (PRE + 1))
                    v.tensor_tensor(yb[p][:, :, cols], ps_y[:, :].rearrange("p (m n) -> p m n", m=MT),
                                    dx[:, :, cols], ALU.add).then_inc(y_ready, 1)
                    dve.wait_ge(state_ready, 2 * g + 2 * CPRE)
                    v.tensor_tensor(state[:, :, :], state[:, :, :],
                                    t.dec[:, bass.ds(g, 1), :].rearrange("p a m -> p m a").to_broadcast([P, MT, P]),
                                    ALU.mult).then_inc(state_scaled, 1)
                    dve.wait_ge(state_scaled, g + 1)
                    dve.wait_ge(s_mm, at(g))
                    for a in range(2):
                        r = slice(a * HD, (a + 1) * HD)
                        v.tensor_tensor(state[r, :, r], ps_s[r, :].rearrange("p (m n) -> p m n", m=MT)[:, :, r],
                                        state[r, :, r], ALU.add).then_inc(state_ready, 1)
                dve.wait_ge(y_ready, at(CH * b, 1 - CH))
                for m in range(MT):
                    n = v.bn_stats(t.ystat[:, bass.ds(b, 1), m, :].rearrange("p a k -> p (a k)"), yb[p][:, m, :])
                n.then_inc(stat_done, 1)

            for b in range(2):
                for m in range(MT):
                    lo_part(b, b, m)
            gaps(0, 0, 16)
            run(dve, body)

        @block.tensor
        def _(pe):
            for c in (b_ready, c_ready, x_turned, b_turned, y_mm, s_mm):
                pe.sem_inc(c, CPRE)

            def project(b, p, m):
                pe.wait_ge(x_lo_ready, MT * b + (MT + CPRE))
                for w_h, w_l, ps, ready, drained in ((wb_hi, wb_lo, ps_pb, b_ready, b_out),
                                                     (wc_hi, wc_lo, ps_pc, c_ready, c_out)):
                    pe.wait_ge(drained, MT * b + (m + CPRE))
                    n = 0
                    for k in range(MT):
                        for w, x in ((w_h, x_hi[p]), (w_l, x_hi[p]), (w_h, x_lo[p])):
                            mm = pe.matmul(ps[:, :], w[:, k, m * P:(m + 1) * P], x[:, k, :],
                                           start=(n == 0), stop=(n == 3 * MT - 1))
                            n += 1
                    mm.then_inc(ready, 1)

            def body(bt, b, p, nxt, nxt2):
                if b is None:
                    return
                pe.wait_ge(x2_loaded[p], half_value(b, p, 1))
                pe.wait_ge(b_out, MT * b + (MT + CPRE))
                pe.wait_ge(c_out, MT * b + (MT + CPRE))
                for c in range(CH):
                    g = CH * b + c
                    cols = slice(c * P, (c + 1) * P)
                    pe.wait_ge(x_w_ready, at(g, 1))
                    for m in range(MT):
                        mm = pe.transpose(ps_x[:, m * P:(m + 1) * P], x2[p][:, m, cols], t.ident)
                    mm.then_inc(x_turned, 1)
                    pe.wait_ge(b_tok_ready, at(g, 1))
                    for m in range(MT):
                        mm = pe.transpose(ps_b[:, m * P:(m + 1) * P], bT[p][:, m, cols], t.ident)
                    mm.then_inc(b_turned, 1)
                    pe.wait_ge(mix_ready, 2 * g + 2 * CPRE)
                    for m in range(MT):
                        for a in range(2):
                            r = slice(a * HD, (a + 1) * HD)
                            mm = pe.matmul(ps_g[a][:, m * P:(m + 1) * P], bT[p][r, m, cols], cT[p][r, m, cols],
                                           start=True, stop=True)
                    mm.then_inc(g_ready, 1)
                    if nxt:
                        project(b + 1, 1 - p, c)
                    pe.wait_ge(y_ready, at(g, 1))
                    pe.wait_ge(x_dt_ready, at(g))
                    pe.wait_ge(c_dec_ready, at(g))
                    pe.wait_ge(mix_ready, 2 * g + (2 * CPRE + 2))
                    pe.wait_ge(state_ready, 2 * g + 2 * CPRE)
                    for m in range(MT):
                        out = ps_y[:, m * P:(m + 1) * P]
                        for a in range(2):
                            pe.matmul(out, x_dt[:, m, a, :], mix[:, a * MT + m, :], start=(a == 0), stop=False)
                        mm = pe.matmul(out, state[:, m, :], c_dec[:, m, :], start=False, stop=True)
                    mm.then_inc(y_mm, 1)
                    pe.wait_ge(x_w_ready, at(g))
                    pe.wait_ge(b_tok_ready, at(g))
                    for m in range(MT):
                        mm = pe.matmul(ps_s[:, m * P:(m + 1) * P], b_tok[:, m * P:(m + 1) * P],
                                       x_w[:, m * P:(m + 1) * P], start=True, stop=True)
                    mm.then_inc(s_mm, 1)

            pe.wait_ge(w_lo, 4)
            pe.wait_ge(zeroed, 1)
            for m in range(MT):
                project(0, 0, m)
            run(pe, body)


def phase_experts(nc, s, t, wup_d, bup_d, wdn_d):
    KT, FT, FR, F, HC, NH, E = s.KT, s.FT, s.FR, s.F, s.HC, s.NH, s.E
    HALF, GS = s.HALF, s.GS
    with ExitStack() as ctx:
        def sem(name):
            return ctx.enter_context(nc.semaphore(name))

        def sb(name, shape, dt=F32):
            return ctx.enter_context(nc.sbuf_tensor(name, shape, dt))

        up_raw = sb("up_raw", [P, KT, F])
        up_hi = [sb(f"up_hi{i}", [P, KT, F], F32R) for i in range(2)]
        up_lo = [sb(f"up_lo{i}", [P, KT, F], F32R) for i in range(2)]
        b_up = [sb(f"b_up{i}", [P, FT]) for i in range(2)]
        dn_raw = [sb(f"dn_raw{i}", [P, FT, s.D]) for i in range(2)]
        dn_hi = [sb(f"dn_hi{i}", [P, FT, s.D], F32R) for i in range(2)]
        dn_lo = [sb(f"dn_lo{i}", [P, FT, s.D], F32R) for i in range(2)]
        xg = [sb(f"xg{i}", [P, HC, s.ROW]) for i in range(2)]
        xg_hi = [sb(f"xg_hi{i}", [P, KT, HALF], F32R) for i in range(2)]
        xg_lo = [sb(f"xg_lo{i}", [P, KT, HALF], F32R) for i in range(2)]
        mid = [sb(f"mid{i}", [P, HALF]) for i in range(3)]
        mid_hi = [sb(f"mid_hi{i}", [P, FT, HALF], F32R) for i in range(2)]
        mid_lo = [sb(f"mid_lo{i}", [P, FT, HALF], F32R) for i in range(2)]
        one_rows = sb("one_rows", [P, HALF])
        gate_col = [sb(f"gate_col{i}", [P, HC, 1]) for i in range(2)]
        ob = [sb(f"ob{i}", [P, HC, s.D]) for i in range(2)]
        ps_t, ps_u, ps_d = t.ps[0:2], t.ps[2:5], t.ps[5:8]

        up_loaded, dn_loaded = [sem(f"f_up_loaded{i}") for i in range(2)], [sem(f"f_dn_loaded{i}") for i in range(2)]
        up_hi_ready, up_lo_ready, dn_hi_ready, dn_lo_ready = (sem(f"f_{n}") for n in ("uph", "upl", "dnh", "dnl"))
        gathered = [sem(f"f_gathered{i}") for i in range(2)]
        turned, xg_hi_ready, xg_lo_ready = sem("f_turned"), sem("f_xgh"), sem("f_xgl")
        up_mm, mid_ready, mid_hi_ready, mid_lo_ready, dn_mm, out_ready = (
            sem(f"f_{n}") for n in ("up_mm", "mid", "midh", "midl", "dn_mm", "out"))
        ones_ready, gate_copied = sem("f_ones"), sem("f_gate")
        added = [sem(f"f_added{i}") for i in range(2)]
        block = ctx.enter_context(nc.Block())
        passes = [(u, u // NH, u % NH) for u in range(E * NH)]

        def rows_of(f):
            return P if f < FT - 1 else FR + 1

        @block.sync
        def _(sp):
            def load_up(g):
                if g:
                    sp.wait_ge(up_lo_ready, g)
                sp.dma_start(up_raw[:, :, :], wup_d[g].rearrange("(k p) f -> p k f", p=P)).then_inc(
                    up_loaded[g % 2], 16)
                if g >= 2:
                    sp.wait_ge(mid_ready, NH * FT * GS * (g - 1))
                sp.dma_start(b_up[g % 2][:, :], bup_d[g]).then_inc(up_loaded[g % 2], 16)

            for e in range(E):
                if e % GS == 0:
                    load_up(e // GS)
                if e >= 2:
                    sp.wait_ge(dn_lo_ready, 2 * (e - 1))
                sp.dma_start(dn_raw[e % 2][:, 0:FT - 1, :],
                             wdn_d[e, 0:(FT - 1) * P, :].rearrange("(f p) d -> p f d", p=P)).then_inc(
                    dn_loaded[e % 2], 16)
                sp.dma_start(dn_raw[e % 2][0:FR + 1, FT - 1, :], wdn_d[e, (FT - 1) * P:F + 1, :]).then_inc(
                    dn_loaded[e % 2], 16)

        @block.gpsimd
        def _(pool):
            def gather(u, e, h):
                q = u % 2
                if u >= 2:
                    pool.wait_ge(turned, KT * (u - 1))
                    pool.wait_ge(gate_copied, u - 1)
                for c in range(HC):
                    pool.indirect_dma_start(
                        out=xg[q][:, c, :], out_offset=None, in_=t.rows_dram,
                        in_offset=bass.IndirectOffsetOnAxis(ap=t.idx[:, e, h * HC + c:h * HC + c + 1], axis=0),
                    ).then_inc(gathered[q], 16)

            def scatter(u, e, h):
                q = u % 2
                if h == 0 and e:
                    for k in range(2):
                        pool.wait_ge(added[k], 16 * HC * ((u + 1 - k) // 2))
                for c in range(HC):
                    pool.wait_ge(out_ready, HC * u + c + 1)
                    pool.indirect_dma_start(
                        out=t.ffn_dram, out_offset=bass.IndirectOffsetOnAxis(
                            ap=t.idx[:, e, h * HC + c:h * HC + c + 1], axis=0),
                        in_=ob[q][:, c, :], in_offset=None, compute_op=ALU.add).then_inc(added[q], 16)

            gather(*passes[0])
            for u in range(len(passes)):
                if u + 1 < len(passes):
                    gather(*passes[u + 1])
                if u:
                    scatter(*passes[u - 1])
            scatter(*passes[-1])
            for k in range(2):
                pool.wait_ge(added[k], 16 * HC * ((len(passes) + 1 - k) // 2))

        @block.scalar
        def _(act):
            def split_up(g):
                act.wait_ge(up_loaded[g % 2], 32 * (g // 2 + 1))
                if g >= 2:
                    act.wait_ge(up_mm, NH * FT * GS * (g - 1))
                nc.scalar.activation(up_hi[g % 2][:, :, :], up_raw[:, :, :], ACT.Copy).then_inc(up_hi_ready, 1)

            def split_down(e):
                act.wait_ge(dn_loaded[e % 2], 32 * (e // 2 + 1))
                if e >= 2:
                    act.wait_ge(dn_mm, HC * NH * (e - 1))
                nc.scalar.activation(dn_hi[e % 2][:, 0:FT - 1, :], dn_raw[e % 2][:, 0:FT - 1, :],
                                     ACT.Copy).then_inc(dn_hi_ready, 1)
                nc.scalar.activation(dn_hi[e % 2][0:FR + 1, FT - 1, :], dn_raw[e % 2][0:FR + 1, FT - 1, :],
                                     ACT.Copy).then_inc(dn_hi_ready, 1)

            split_up(0)
            split_down(0)
            for u, e, h in passes:
                q = u % 2
                for k in range(KT):
                    act.wait_ge(turned, KT * u + k + 1)
                    if u >= 2:
                        act.wait_ge(up_mm, FT * (u - 1))
                    nc.scalar.activation(xg_hi[q][:, k, :], t.ps[k][:, 0:HALF], ACT.Copy).then_inc(xg_hi_ready, 1)
                for f in range(FT):
                    n = u * FT + f
                    R = P if f < FT - 1 else FR
                    act.wait_ge(up_mm, n + 1)
                    if n >= 3:
                        act.wait_ge(mid_lo_ready, n - 2)
                    nc.scalar.activation(mid[n % 3][0:R, :], ps_u[n % 3][0:R, 0:HALF], ACT.Silu,
                                         bias=b_up[(e // GS) % 2][0:R, f:f + 1]).then_inc(mid_ready, 1)
                if h == NH - 1 and e + 1 < E:
                    if (e + 1) % GS == 0:
                        split_up((e + 1) // GS)
                    split_down(e + 1)

        @block.vector
        def _(dve):
            v = nc.vector
            v.memset(one_rows[:, :], 1.0).then_inc(ones_ready, 1)
            dve.wait_ge(ones_ready, 1)
            for q in range(2):
                v.tensor_copy(mid_hi[q][:, FT - 1, :], one_rows[:, :]).then_inc(ones_ready, 1)
                v.tensor_scalar(mid_lo[q][:, FT - 1, :], one_rows[:, :], 0.0, None, ALU.mult).then_inc(ones_ready, 1)
            dve.wait_ge(ones_ready, 5)

            def split_up(g):
                dve.wait_ge(up_hi_ready, g + 1)
                v.tensor_tensor(up_lo[g % 2][:, :, :], up_raw[:, :, :], up_hi[g % 2][:, :, :].bitcast(F32),
                                ALU.subtract).then_inc(up_lo_ready, 1)

            def split_down(e):
                q = e % 2
                dve.wait_ge(dn_hi_ready, 2 * e + 2)
                for rows, f in ((P, slice(0, FT - 1)), (FR + 1, slice(FT - 1, FT))):
                    v.tensor_tensor(dn_lo[q][0:rows, f, :], dn_raw[q][0:rows, f, :],
                                    dn_hi[q][0:rows, f, :].bitcast(F32), ALU.subtract).then_inc(dn_lo_ready, 1)

            def weigh(u):
                q = u % 2
                if u >= 2:
                    dve.wait_ge(added[q], 16 * HC * (u // 2))
                for c in range(HC):
                    n = u * HC + c
                    dve.wait_ge(dn_mm, n + 1)
                    v.tensor_scalar(ob[q][:, c, :], ps_d[n % 3][:, 0:s.D], gate_col[q][:, c, :], None,
                                    ALU.mult).then_inc(out_ready, 1)

            split_up(0)
            split_down(0)
            for u, e, h in passes:
                q = u % 2
                for k in range(KT):
                    dve.wait_ge(xg_hi_ready, KT * u + k + 1)
                    v.tensor_tensor(xg_lo[q][:, k, :], t.ps[k][:, 0:HALF], xg_hi[q][:, k, :].bitcast(F32),
                                    ALU.subtract).then_inc(xg_lo_ready, 1)
                if u >= 2:
                    dve.wait_ge(out_ready, HC * (u - 1))
                v.tensor_copy(gate_col[q][:, :, :], xg[q][:, :, s.D + e:s.D + e + 1]).then_inc(gate_copied, 1)
                for f in range(FT):
                    n = u * FT + f
                    R = P if f < FT - 1 else FR
                    dve.wait_ge(mid_ready, n + 1)
                    if u >= 2 and f == 0:
                        dve.wait_ge(dn_mm, HC * (u - 1))
                    v.tensor_copy(mid_hi[q][0:R, f, :], mid[n % 3][0:R, :]).then_inc(mid_hi_ready, 1)
                    dve.wait_ge(mid_hi_ready, n + 1)
                    v.tensor_tensor(mid_lo[q][0:R, f, :], mid[n % 3][0:R, :], mid_hi[q][0:R, f, :].bitcast(F32),
                                    ALU.subtract).then_inc(mid_lo_ready, 1)
                if u:
                    weigh(u - 1)
                if h == NH - 1 and e + 1 < E:
                    if (e + 1) % GS == 0:
                        split_up((e + 1) // GS)
                    split_down(e + 1)
            weigh(len(passes) - 1)

        @block.tensor
        def _(pe):
            def turn(u):
                q = u % 2
                pe.wait_ge(gathered[q], 16 * HC * (u // 2 + 1))
                for k in range(KT):
                    if u:
                        pe.wait_ge(xg_lo_ready, KT * (u - 1) + k + 1)
                    for c in range(HC):
                        mm = pe.transpose(t.ps[k][:, c * P:(c + 1) * P], xg[q][:, c, k * P:(k + 1) * P], t.ident)
                    mm.then_inc(turned, 1)

            def up(u, e):
                q, w = u % 2, (e // GS) % 2
                pe.wait_ge(xg_lo_ready, KT * (u + 1))
                pe.wait_ge(up_lo_ready, e // GS + 1)
                for f in range(FT):
                    n = u * FT + f
                    R = P if f < FT - 1 else FR
                    if n >= 3:
                        pe.wait_ge(mid_ready, n - 2)
                    i = 0
                    for k in range(KT):
                        for wgt, x in ((up_hi[w], xg_hi[q]), (up_lo[w], xg_hi[q]), (up_hi[w], xg_lo[q])):
                            mm = pe.matmul(ps_u[n % 3][0:R, 0:HALF], wgt[:, k, f * P:f * P + R], x[:, k, :],
                                           start=(i == 0), stop=(i == 3 * KT - 1))
                            i += 1
                    mm.then_inc(up_mm, 1)

            def down(u, e):
                q, w = u % 2, e % 2
                pe.wait_ge(mid_lo_ready, FT * (u + 1))
                pe.wait_ge(dn_lo_ready, 2 * e + 2)
                for c in range(HC):
                    n = u * HC + c
                    if n >= 3:
                        pe.wait_ge(out_ready, n - 2)
                    i = 0
                    for f in range(FT):
                        R = rows_of(f)
                        for x, wgt in ((mid_hi[q], dn_hi[w]), (mid_lo[q], dn_hi[w]), (mid_hi[q], dn_lo[w])):
                            mm = pe.matmul(ps_d[n % 3][:, 0:s.D], x[0:R, f, c * P:(c + 1) * P], wgt[0:R, f, :],
                                           start=(i == 0), stop=(i == 3 * FT - 1))
                            i += 1
                    mm.then_inc(dn_mm, 1)

            turn(0)
            for u, e, h in passes:
                up(u, e)
                if u + 1 < len(passes):
                    turn(u + 1)
                if u:
                    down(u - 1, passes[u - 1][1])
            down(*passes[-1][0:2])


def phase_output(nc, s, t, x_blk, out_blk, wout_d):
    MT, B, BPB, NB = s.MT, s.B, s.BPB, s.NB
    CPRE = PRE * CH
    with ExitStack() as ctx:
        def sem(name):
            return ctx.enter_context(nc.semaphore(name))

        def sb(name, shape, dt=F32):
            return ctx.enter_context(nc.sbuf_tensor(name, shape, dt))

        w_raw = sb("wo_raw", [P, MT, s.D])
        w_hi, w_lo = (sb(n, [P, MT, s.D], F32R) for n in ("wo_hi", "wo_lo"))
        n0, n1, n2, n3, n4, mean_c, var_c, shift, scale = (sb(f"n{i}", [P, B, MT]) for i in range(9))
        g0, g1, g2, g3 = (sb(f"g{i}", [P, B, MT, BPB]) for i in range(4))
        moments = sb("moments", [P, 2, B, MT])
        yc = [sb(f"yc{i}", [P, MT, BLK]) for i in range(2)]
        zc = [sb(f"zc{i}", [P, MT, BLK]) for i in range(2)]
        xc = [sb(f"xc{i}", [P, CH, s.D]) for i in range(2)]
        fc = [sb(f"fc{i}", [P, CH, s.D]) for i in range(2)]
        gh = [sb(f"gh{i}", [P, MT, BLK], F32R) for i in range(2)]
        gl = [sb(f"gl{i}", [P, MT, BLK], F32R) for i in range(2)]
        oc = [sb(f"oc{i}", [P, CH, s.D]) for i in range(2)]
        ps_m, ps_o = t.ps[0], t.ps[1:5]

        w_loaded, w_hi_ready, w_lo_ready = sem("c_w"), sem("c_wh"), sem("c_wl")
        vec, dev_ready, mom_ready = sem("c_vec"), sem("c_dev"), sem("c_mom")
        loaded = [sem(f"c_loaded{i}") for i in range(2)]
        gate_ready = sem("c_gate")
        normed, gated, hi_ready, lo_ready, mm_done, mul_done, sum_done = (
            sem(f"c_{n}") for n in ("normed", "gated", "hi", "lo", "mm", "mul", "sum"))
        out_stored = [sem(f"c_out{i}") for i in range(2)]
        steps = {}
        block = ctx.enter_context(nc.Block())

        @block.vector
        def _(dve):
            v = nc.vector
            n = [0]

            def do(ins, name=None):
                n[0] += 1
                ins.then_inc(vec, 1)
                dve.wait_ge(vec, n[0])
                if name:
                    steps[name] = n[0]

            half = [t.ystat[:, :, :, k].rearrange("p (a b) m -> p a m b", a=B) for k in (1, 2, 4, 5)]
            do(v.tensor_tensor(g0[:, :, :, :], half[0], half[2], ALU.add))
            do(v.tensor_reduce(n0[:, :, :].unsqueeze(3), g0[:, :, :, :], AX.X, ALU.add))
            do(v.tensor_scalar(mean_c[:, :, :], n0[:, :, :], 0.5 / BPB, None, ALU.mult))
            mb = mean_c[:, :, :].unsqueeze(3).to_broadcast([P, B, MT, BPB])
            do(v.tensor_tensor(g0[:, :, :, :], half[0], mb, ALU.subtract))
            do(v.tensor_tensor(g1[:, :, :, :], half[2], mb, ALU.subtract))
            do(v.tensor_tensor(g2[:, :, :, :], g0[:, :, :, :], g0[:, :, :, :], ALU.mult))
            do(v.tensor_tensor(g3[:, :, :, :], g1[:, :, :, :], g1[:, :, :, :], ALU.mult))
            do(v.tensor_tensor(g0[:, :, :, :], g2[:, :, :, :], g3[:, :, :, :], ALU.add))
            do(v.tensor_tensor(g1[:, :, :, :], half[1], half[3], ALU.add))
            do(v.scalar_tensor_tensor(g2[:, :, :, :].rearrange("p a m b -> p (a m b)"),
                                      g0[:, :, :, :].rearrange("p a m b -> p (a m b)"), float(BLK // 2),
                                      g1[:, :, :, :].rearrange("p a m b -> p (a m b)"), ALU.mult, ALU.add))
            do(v.tensor_reduce(n1[:, :, :].unsqueeze(3), g2[:, :, :, :], AX.X, ALU.add))
            do(v.tensor_scalar(var_c[:, :, :], n1[:, :, :], 1.0 / s.L, None, ALU.mult))
            do(v.tensor_copy(moments[:, 0, :, :], mean_c[:, :, :]))
            do(v.tensor_tensor(n0[:, :, :], mean_c[:, :, :], mean_c[:, :, :], ALU.mult))
            do(v.tensor_tensor(moments[:, 1, :, :], n0[:, :, :], var_c[:, :, :], ALU.add), "moments")
            dve.wait_ge(mom_ready, 1)
            do(v.tensor_copy(moments[:, :, :, :], ps_m[:, 0:2 * B * MT].rearrange("p (k a m) -> p k a m", k=2, a=B)))
            do(v.tensor_tensor(n0[:, :, :], moments[:, 0, :, :], moments[:, 0, :, :], ALU.mult))
            do(v.tensor_tensor(n1[:, :, :], moments[:, 1, :, :], n0[:, :, :], ALU.subtract))
            do(v.tensor_scalar(n2[:, :, :], n1[:, :, :], EPS, None, ALU.add), "var")
            dve.wait_ge(dev_ready, 1)
            do(v.reciprocal(n0[:, :, :], n3[:, :, :]))
            do(v.tensor_tensor(n1[:, :, :], n0[:, :, :], n0[:, :, :], ALU.mult))
            do(v.scalar_tensor_tensor(n4[:, :, :], n1[:, :, :], -0.5, n2[:, :, :], ALU.mult, ALU.mult))
            do(v.scalar_tensor_tensor(n1[:, :, :], n4[:, :, :], 1.5, n0[:, :, :], ALU.add, ALU.mult))
            wide = [w[:, :].unsqueeze(1).to_broadcast([P, B, MT]) for w in (t.gnw, t.gnb)]
            do(v.tensor_tensor(scale[:, :, :], n1[:, :, :], wide[0], ALU.mult))
            do(v.tensor_tensor(n0[:, :, :], moments[:, 0, :, :], scale[:, :, :], ALU.mult))
            do(v.tensor_tensor(shift[:, :, :], wide[1], n0[:, :, :], ALU.subtract), "affine")
            dve.wait_ge(w_hi_ready, 1)
            v.tensor_tensor(w_lo[:, :, :], w_raw[:, :, :], w_hi[:, :, :].bitcast(F32), ALU.subtract).then_inc(
                w_lo_ready, 1)
            for c, k in ((gated, MT * PRE), (lo_ready, MT * PRE), (mul_done, CPRE)):
                dve.sem_inc(c, k)
            with dve.Fori(0, NB // 2) as j:
                for p in range(2):
                    b = 2 * j + p
                    for m in range(MT):
                        dve.wait_ge(normed, MT * b + (MT * PRE + m + 1))
                        v.tensor_tensor(yc[p][:, m, :], yc[p][:, m, :], zc[p][:, m, :], ALU.mult).then_inc(gated, 1)
                    for m in range(MT):
                        dve.wait_ge(hi_ready, MT * b + (MT * PRE + m + 1))
                        v.tensor_tensor(gl[p][:, m, :], yc[p][:, m, :], gh[p][:, m, :].bitcast(F32),
                                        ALU.subtract).then_inc(lo_ready, 1)
                    dve.wait_ge(gate_ready, b + (PRE + 1))
                    dve.wait_ge(out_stored[p], 16 * j + 16)
                    for c in range(CH):
                        dve.wait_ge(mm_done, CH * b + (CPRE + c + 1))
                        v.tensor_tensor(oc[p][:, c, :], ps_o[c][:, 0:s.D], fc[p][:, c, :], ALU.mult).then_inc(
                            mul_done, 1)

        @block.scalar
        def _(act):
            act.wait_ge(w_loaded, 16)
            nc.scalar.activation(w_hi[:, :, :], w_raw[:, :, :], ACT.Copy).then_inc(w_hi_ready, 1)
            act.wait_ge(vec, steps["var"])
            nc.scalar.activation(n3[:, :, :], n2[:, :, :], ACT.Sqrt).then_inc(dev_ready, 1)
            for c, k in ((normed, MT * PRE), (hi_ready, MT * PRE), (gate_ready, PRE)):
                act.sem_inc(c, k)
            act.wait_ge(vec, steps["affine"])
            for bt in range(B):
                with act.Fori(bt * BPB // 2, (bt + 1) * BPB // 2) as j:
                    for p in range(2):
                        b = 2 * j + p
                        act.wait_ge(loaded[p], 64 * j + 64)
                        nc.scalar.activation(fc[p][:, :, :], fc[p][:, :, :], ACT.Silu).then_inc(gate_ready, 1)
                        for m in range(MT):
                            nc.scalar.activation(yc[p][:, m, :], yc[p][:, m, :], ACT.Identity,
                                                 bias=shift[:, bt, m:m + 1],
                                                 scale=scale[:, bt, m:m + 1]).then_inc(normed, 1)
                        act.wait_ge(mm_done, CH * b + (CPRE - CH))
                        for m in range(MT):
                            act.wait_ge(gated, MT * b + (MT * PRE + m + 1))
                            nc.scalar.activation(gh[p][:, m, :], yc[p][:, m, :], ACT.Copy).then_inc(hi_ready, 1)

        @block.gpsimd
        def _(pool):
            pool.sem_inc(sum_done, PRE)
            for p in range(2):
                pool.sem_inc(out_stored[p], 16)
            with pool.Fori(0, NB // 2) as j:
                for p in range(2):
                    b = 2 * j + p
                    pool.wait_ge(mul_done, CH * b + (CPRE + CH))
                    nc.gpsimd.tensor_tensor(oc[p][:, :, :], oc[p][:, :, :], xc[p][:, :, :], ALU.add).then_inc(
                        sum_done, 1)

        @block.tensor
        def _(pe):
            pe.wait_ge(vec, steps["moments"])
            pe.matmul(ps_m[:, 0:2 * B * MT], t.headavg, moments[:, :, :, :].rearrange("p k a m -> p (k a m)"),
                      start=True, stop=True).then_inc(mom_ready, 1)
            pe.wait_ge(w_lo_ready, 1)
            pe.sem_inc(mm_done, CPRE)
            with pe.Fori(0, NB // 2) as j:
                for p in range(2):
                    b = 2 * j + p
                    pe.wait_ge(lo_ready, MT * b + MT * (PRE + 1))
                    for c in range(CH):
                        pe.wait_ge(mul_done, CH * b + (CPRE - CH + c + 1))
                        n = 0
                        for k in range(MT):
                            for g, w in ((gh[p], w_hi), (gl[p], w_hi), (gh[p], w_lo)):
                                mm = pe.matmul(ps_o[c][:, 0:s.D], g[:, k, c * P:(c + 1) * P], w[:, k, :],
                                               start=(n == 0), stop=(n == 3 * MT - 1))
                                n += 1
                        mm.then_inc(mm_done, 1)

        @block.sync
        def _(sp):
            sp.dma_start(w_raw[:, :, :], wout_d.rearrange("(k p) n -> p k n", p=P)).then_inc(w_loaded, 16)

            def load(b, p):
                for dst, src in ((yc, t.y_dram[b]), (zc, t.zs_dram[b]), (xc, x_blk[b]), (fc, t.ffn_blk[b])):
                    sp.dma_start(dst[p][:, :, :], src).then_inc(loaded[p], 16)

            def store(b, p):
                sp.wait_ge(sum_done, b + (PRE + 1))
                sp.dma_start(out_blk[b], oc[p][:, :, :]).then_inc(out_stored[p], 16)

            for p in range(2):
                load(p, p)
            with sp.Fori(0, NB // 2 - 1) as j:
                for p in range(2):
                    store(2 * j + p, p)
                    sp.wait_ge(lo_ready, MT * (2 * j + p) + MT * (PRE + 1))
                    load(2 * j + (p + 2), p)
            for p in range(2):
                store(NB - 2 + p, p)
            for p in range(2):
                sp.wait_ge(out_stored[p], 16 * (NB // 2 + 1))


def build(nc, ins, outs):
    x_d = ins["x"]
    s = Shapes(x_d, ins["wx"], ins["wdt"], ins["wr"], ins["wup"])
    x_blk = x_d.rearrange("b (i c p) d -> (b i) p c d", c=CH, p=P)
    t = Tiles()

    def dram(name, shape):
        if name in outs:
            return outs[name]
        return nc.dram_tensor(name, shape, F32, kind="Internal").ap()

    t.rows_dram = dram("rows_dram", [s.T, s.ROW])
    t.x2_dram = dram("x2_dram", [s.NB, P, s.MT, BLK])
    t.zs_dram = dram("zs_dram", [s.NB, P, s.MT, BLK])
    t.y_dram = dram("y_dram", [s.NB, P, s.MT, BLK])
    t.ffn_dram = dram("ffn_dram", [s.T, s.D])
    t.cum_dram = dram("cum_dram", [s.NT, s.H, P])
    t.ecum_dram = dram("ecum_dram", [s.NT, s.H, P])
    t.ffn_blk = t.ffn_dram.rearrange("(i c p) d -> i p c d", c=CH, p=P)
    t.xn_blk = t.rows_dram[:, 0:s.D].rearrange("(i c p) d -> i p c d", c=CH, p=P)
    with ExitStack() as ctx:
        def sb(name, shape, dt=F32):
            return ctx.enter_context(nc.sbuf_tensor(name, shape, dt))

        t.ps = [ctx.enter_context(nc.psum_tensor(f"ps{i}", [P, 512], F32)) for i in range(8)]
        t.cst = sb("cst", [P, C_END])
        t.ident = t.cst[:, C_ID:C_ID + P]
        t.tri = t.cst[:, C_TRI:C_TRI + P]
        t.ones = t.cst[:, C_ONES:C_ONES + P]
        t.rsum = t.cst[:, C_RSUM:C_RSUM + P]
        t.rtri = t.cst[:, C_RTRI:C_RTRI + P]
        t.iota = t.cst[:, C_IOTA:C_IOTA + P]
        t.headavg = t.cst[:, C_HEAD:C_HEAD + P]
        t.rows = sb("rows", [P, 3, 8])
        t.dcol, t.gnw, t.gnb, t.cb = (sb(n, [P, s.MT]) for n in ("dcol", "gnw", "gnb", "cb"))
        t.cw = sb("cw", [P, s.MT, 4])
        t.norm = sb("norm", [P, 2, s.NT])
        t.dt = sb("dt", [P, s.NT, s.H])
        t.cum = sb("cum", [P, s.NT, s.H])
        t.wst = sb("wst", [P, s.NT, s.H])
        t.dec = sb("dec", [P, s.NT, s.MT])
        t.gates = sb("gates", [P, s.NT, s.E])
        t.idx = sb("idx", [P, s.E, s.LW], U32)
        t.ystat = sb("ystat", [P, s.NB, s.MT, 6])
        with ExitStack() as early:
            def sbe(name, shape, dt=F32):
                return early.enter_context(nc.sbuf_tensor(name, shape, dt))

            t.wx, t.wz = (sbe(n, [P, s.KT, s.INNER]) for n in ("wx", "wz"))
            t.wr = sbe("wr", [P, s.KT, s.E])
            t.wdt = sbe("wdt", [P, s.MT, s.H])
            t.logit2 = sbe("logit2", [P, s.NT, 2, s.E])
            consts = [(t.cst[:, :], ins["const"]), (t.rows[:, :, :], ins["rows"]), (t.dcol[:, :], ins["dcol"]),
                      (t.gnw[:, :], ins["gnw"]), (t.gnb[:, :], ins["gnb"]), (t.cb[:, :], ins["cb"]),
                      (t.cw[:, :, :], ins["cw"]),
                      (t.wx[:, :, :], ins["wx"].rearrange("(k p) n -> p k n", p=P)),
                      (t.wz[:, :, :], ins["wz"].rearrange("(k p) n -> p k n", p=P)),
                      (t.wr[:, :, :], ins["wr"].rearrange("(k p) n -> p k n", p=P)),
                      (t.wdt[:, :, :], ins["wdt"].rearrange("(k p) n -> p k n", p=P))]
            phase_stats(nc, s, t, x_blk, consts)
            phase_project(nc, s, t, x_blk)
            phase_route(nc, s, t)
        phase_scan(nc, s, t, ins["wb"], ins["wc"])
        phase_experts(nc, s, t, ins["wup"], ins["bup"], ins["wdn"])
        if "out" in outs:
            phase_output(nc, s, t, x_blk, outs["out"].rearrange("b (i c p) d -> (b i) p c d", c=CH, p=P), ins["wout"])


def shape_constants(T, E):
    import numpy as np

    i = np.arange(P)
    c = np.zeros((P, C_END), np.float32)
    c[:, C_ID:C_ID + P] = np.eye(P)
    c[:, C_TRI:C_TRI + P] = i[:, None] <= i[None, :]
    c[:, C_ONES:C_ONES + P] = 1
    same = i[:, None] % E == i[None, :] % E
    c[:, C_RSUM:C_RSUM + P] = same
    c[:, C_RTRI:C_RTRI + P] = same & (i[:, None] < i[None, :])
    c[:, C_IOTA:C_IOTA + P] = i[None, :]
    c[:, C_HEAD:C_HEAD + P] = (i[:, None] // 64 == i[None, :] // 64) / 64.0
    c[:, C_TAU:C_TAU + 64] = np.arange(64)[None, :]
    c[:, C_PIDX] = i
    c[:, C_LO:C_LO + 8] = np.arange(8)[None, :]
    return c


def lay_out(v):
    import numpy as np

    a = {k.split("_", 2)[2]: np.asarray(x) for k, x in v.items()}
    con = np.ascontiguousarray

    def column(row, width=P):
        return con(row.reshape(-1, width).T)

    d = a["d_param"]
    F = a["W_down"].shape[1]
    FT = -(-F // P)
    bup = np.zeros((a["b_up"].shape[0], FT * P), a["b_up"].dtype)
    bup[:, :F] = a["b_up"]
    x = a["input_tensor"]
    return {
        "x": con(x),
        "wx": con(a["Wx"].T), "wz": con(a["Wz"].T), "wb": con(a["Wb"].T), "wc": con(a["Wc"].T),
        "wdt": con(a["Wdt"].T), "wout": con(a["Wout"].T), "wr": con(a["Wr"]),
        "cw": con(a["conv_w"][:, 0, :].reshape(-1, P, 4).transpose(1, 0, 2)), "cb": column(a["conv_b"]),
        "rows": con(np.broadcast_to(np.stack([a["log_a"], a["b_dt"], a["br"]])[None], (P, 3, 8))),
        "dcol": column(np.repeat(d, a["gn_w"].shape[0] // d.shape[0])),
        "gnw": column(a["gn_w"]), "gnb": column(a["gn_b"]),
        "wup": con(a["W_up"]), "bup": con(bup.reshape(-1, FT, P).transpose(0, 2, 1)),
        "wdn": con(np.concatenate([a["W_down"], a["b_down"][:, None, :]], axis=1)),
        "const": shape_constants(x.shape[0] * x.shape[1], a["Wr"].shape[1]),
    }


def kernel(**inputs):
    import numpy as _np
    import concourse.bacc as _bacc
    from concourse import mybir as _mybir
    from concourse.bass_utils import run_bass_kernel_spmd as _run

    nc = _bacc.Bacc("TRN2", target_bir_lowering=False, num_devices=1)
    arrays = {f"in_{k}": v for k, v in lay_out(inputs).items()}
    ins = {k[3:]: nc.dram_tensor(k, v.shape, _mybir.dt.from_np(v.dtype), kind="ExternalInput").ap()
           for k, v in arrays.items()}
    shape = arrays["in_x"].shape
    out = nc.dram_tensor("out_dram", shape, _mybir.dt.float32, kind="ExternalOutput").ap()
    build(nc, ins, {"out": out})
    r = _run(nc, [arrays], core_ids=[0])
    return r.results[0]["out_dram"]
```

```python
from contextlib import ExitStack

import concourse.bass as bass
from concourse import mybir

F32 = mybir.dt.float32
F32R = mybir.dt.float32r
BF16 = mybir.dt.bfloat16
I32 = mybir.dt.int32
U32 = mybir.dt.uint32
ALU = mybir.AluOpType
ACT = mybir.ActivationFunctionType
AX = mybir.AxisListType

P = 128
BLK = 512
CH = BLK // P
EPS = 1e-5

PRE = 2

C_ID, C_TRI, C_ONES, C_RSUM, C_RTRI, C_IOTA, C_HEAD, C_TAU, C_PIDX, C_LO, C_BIT = (
    0, 128, 256, 384, 512, 640, 768, 896, 960, 961, 969)
BITS = 30
C_END = 1002


class Shapes:

    def __init__(self, x, wx, wdt, wr, wup):
        self.B, self.L, self.D = x.shape
        self.INNER = wx.shape[1]
        self.KT = self.D // P
        self.MT = self.INNER // P
        self.H = wdt.shape[1]
        self.HD = self.INNER // self.H
        self.E = wr.shape[1]
        self.G, _, self.F = wup.shape
        self.GS = self.E // self.G
        self.FT = -(-self.F // P)
        self.FR = self.F - (self.FT - 1) * P
        self.T = self.B * self.L
        self.NB = self.T // BLK
        self.NT = self.T // P
        self.BPB = self.L // BLK
        self.CAP = self.T // self.E
        self.LW = self.CAP // P
        self.HALF = min(BLK, self.CAP)
        self.NH = self.CAP // self.HALF
        self.HC = self.HALF // P
        self.NSEG = P // self.E
        self.GT = self.NT // self.NSEG
        self.SEG = self.GT * P
        self.ROW = self.D + self.E
        assert self.KT == 2 and self.MT == 4 and self.H == 2 * self.MT and self.HD == 64
        assert self.BPB * CH == self.NT // 2 and self.B == 2 and BITS <= self.BPB * CH <= 32
        assert self.LW & (self.LW - 1) == 0 and self.BPB % 2 == 0 and self.E == 8 and self.GS == 2


class Tiles:
    pass


def phase_stats(nc, s, t, x_blk, consts):
    with ExitStack() as ctx:
        def sem(name):
            return ctx.enter_context(nc.semaphore(name))

        xin = [ctx.enter_context(nc.sbuf_tensor(f"stat_x{i}", [P, CH, s.D], F32)) for i in range(4)]
        stat6 = ctx.enter_context(nc.sbuf_tensor("stat6", [P, s.NT, 6], F32))
        dmean, var, dev, inv, tmp = (
            ctx.enter_context(nc.sbuf_tensor(f"stat_t{i}", [P, s.NT], F32)) for i in range(5))
        const_loaded = sem("const_loaded")
        x_loaded = [sem(f"stat_x_loaded{i}") for i in range(4)]
        stat_done = sem("stat_done")
        step = sem("stat_step")
        dev_done = sem("dev_done")
        block = ctx.enter_context(nc.Block())

        @block.sync
        def _(sp):
            for i in range(4):
                sp.dma_start(xin[i][:, :, :], x_blk[i]).then_inc(x_loaded[i], 16)
            if s.NB > 4:
                with sp.Fori(1, s.NB // 4) as j:
                    for i in range(4):
                        sp.wait_ge(stat_done, 4 * j + (i - 3))
                        sp.dma_start(xin[i][:, :, :], x_blk[4 * j + i]).then_inc(x_loaded[i], 16)

        @block.gpsimd
        def _(pool):
            for dst, src in consts:
                pool.dma_start(dst, src).then_inc(const_loaded, 16)
            pool.wait_ge(const_loaded, 16 * len(consts))

        @block.vector
        def _(dve):
            with dve.Fori(0, s.NB // 4) as j:
                for i in range(4):
                    dve.wait_ge(x_loaded[i], 16 * j + 16)
                    for c in range(CH):
                        n = nc.vector.bn_stats(stat6[:, 4 * CH * j + (CH * i + c), :], xin[i][:, c, :])
                    n.then_inc(stat_done, 1)
            dve.wait_ge(stat_done, s.NB)
            half_mean = [stat6[:, :, k] for k in (1, 4)]
            half_m2 = [stat6[:, :, k] for k in (2, 5)]
            mean, rstd = t.norm[:, 0, :], t.norm[:, 1, :]
            nc.vector.tensor_tensor(tmp[:, :], half_mean[0], half_mean[1], ALU.add).then_inc(step, 1)
            nc.vector.tensor_tensor(dmean[:, :], half_mean[0], half_mean[1], ALU.subtract).then_inc(step, 1)
            nc.vector.tensor_tensor(var[:, :], half_m2[0], half_m2[1], ALU.add).then_inc(step, 1)
            dve.wait_ge(step, 3)
            nc.vector.tensor_scalar(mean, tmp[:, :], 0.5, None, ALU.mult).then_inc(step, 1)
            nc.vector.scalar_tensor_tensor(dev[:, :], dmean[:, :], 0.25, dmean[:, :], ALU.mult,
                                           ALU.mult).then_inc(step, 1)
            dve.wait_ge(step, 5)
            nc.vector.scalar_tensor_tensor(tmp[:, :], var[:, :], 1.0 / s.D, dev[:, :], ALU.mult,
                                           ALU.add).then_inc(step, 1)
            dve.wait_ge(step, 6)
            nc.vector.tensor_scalar(var[:, :], tmp[:, :], EPS, None, ALU.add).then_inc(step, 1)
            dve.wait_ge(dev_done, 1)
            nc.vector.reciprocal(inv[:, :], dev[:, :]).then_inc(step, 1)
            dve.wait_ge(step, 8)
            nc.vector.tensor_tensor(tmp[:, :], inv[:, :], inv[:, :], ALU.mult).then_inc(step, 1)
            dve.wait_ge(step, 9)
            nc.vector.scalar_tensor_tensor(dmean[:, :], tmp[:, :], -0.5, var[:, :], ALU.mult,
                                           ALU.mult).then_inc(step, 1)
            dve.wait_ge(step, 10)
            nc.vector.scalar_tensor_tensor(rstd, dmean[:, :], 1.5, inv[:, :], ALU.add,
                                           ALU.mult).then_inc(step, 1)

        @block.scalar
        def _(act):
            act.wait_ge(step, 7)
            nc.scalar.activation(dev[:, :], var[:, :], ACT.Sqrt).then_inc(dev_done, 1)


def phase_project(nc, s, t, x_blk):
    KT, MT = s.KT, s.MT
    with ExitStack() as ctx:
        def sem(name):
            return ctx.enter_context(nc.semaphore(name))

        def sb(name, shape, dt=F32):
            return ctx.enter_context(nc.sbuf_tensor(name, shape, dt))

        wx_hi, wx_lo, wz_hi, wz_lo = (sb(f"w{n}", [P, KT, s.INNER], F32R) for n in ("xh", "xl", "zh", "zl"))
        wr2 = sb("wr2", [P, KT, 2, s.E], F32R)
        xin = [sb(f"xin{i}", [P, CH, s.D]) for i in range(2)]
        xn = [sb(f"xn{i}", [P, CH, s.D]) for i in range(2)]
        norm_blk = [sb(f"norm_blk{i}", [P, 2, CH]) for i in range(2)]
        xn_hi = [sb(f"xn_hi{i}", [P, KT, BLK], F32R) for i in range(2)]
        xn_lo = [sb(f"xn_lo{i}", [P, KT, BLK], F32R) for i in range(2)]
        xpre = [sb(f"xpre{m}", [P, 3 + BLK]) for m in range(MT)]
        acc = [sb(f"acc{m}", [P, BLK]) for m in range(MT)]
        x2 = [sb(f"x2a{i}", [P, MT, BLK]) for i in range(2)]
        zs = [sb(f"zsa{i}", [P, MT, BLK]) for i in range(2)]
        ps_t, ps_x, ps_z, ps_lg, ps_dt = t.ps[0:2], t.ps[2:4], t.ps[4:6], t.ps[6], t.ps[7]

        w_hi = sem("a_w_hi")
        w_lo = sem("a_w_lo")
        x_loaded = [sem(f"a_x_loaded{i}") for i in range(2)]
        norm_copied = sem("a_norm_copied")
        xn_ready = sem("a_xn_ready")
        xn_stored = [sem(f"a_xn_stored{i}") for i in range(2)]
        xnT_ready = sem("a_xnT_ready")
        xn_hi_ready = sem("a_xn_hi_ready")
        xn_lo_ready = sem("a_xn_lo_ready")
        x_ready = sem("a_x_ready")
        z_ready = sem("a_z_ready")
        xpre_ready = sem("a_xpre_ready")
        tap0_done = sem("a_tap0_done")
        taps = sem("a_taps")
        conv_done = sem("a_conv_done")
        halo_done = sem("a_halo_done")
        halo_reset = sem("a_halo_reset")
        x2_ready = sem("a_x2_ready")
        zs_ready = sem("a_zs_ready")
        lg_ready = sem("a_lg_ready")
        dt_ready = sem("a_dt_ready")
        lg_copied = sem("a_lg_copied")
        dt_copied = sem("a_dt_copied")
        x2_stored = [sem(f"a_x2_stored{i}") for i in range(2)]
        zs_stored = [sem(f"a_zs_stored{i}") for i in range(2)]
        waited = sem("a_waited")
        block = ctx.enter_context(nc.Block())

        @block.sync
        def _(sp):
            with sp.Fori(0, s.NB // 2) as j:
                for p in range(2):
                    b = 2 * j + p
                    sp.wait_ge(xn_ready, b + (PRE - 1))
                    sp.dma_start(xin[p][:, :, :], x_blk[b]).then_inc(x_loaded[p], 16)
                    sp.wait_ge(xn_ready, b + (PRE + 1))
                    sp.dma_start(t.xn_blk[b], xn[p][:, :, :]).then_inc(xn_stored[p], 16)

        @block.gpsimd
        def _(pool):
            pool.sem_inc(xn_ready, PRE)
            pool.sem_inc(tap0_done, MT * PRE)

            def block_steps(j, p):
                    b = 2 * j + p
                    nc.gpsimd.tensor_copy(norm_blk[p][:, :, :], t.norm[:, :, bass.ds(CH * b, CH)]).then_inc(
                        norm_copied, 1)
                    pool.wait_ge(norm_copied, b + 1)
                    pool.wait_ge(x_loaded[p], 16 * j + 16)
                    pool.wait_ge(xn_stored[p], 16 * j + 16)
                    pool.wait_ge(xnT_ready, KT * b + KT * (PRE - 1))
                    pool.sem_inc(waited, 1)
                    for c in range(CH):
                        n = nc.gpsimd.tensor_scalar(xn[p][:, c, :], xin[p][:, c, :], norm_blk[p][:, 0, c:c + 1],
                                                    norm_blk[p][:, 1, c:c + 1], ALU.subtract, ALU.mult)
                    n.then_inc(xn_ready, 1)
                    for m in range(MT):
                        pool.wait_ge(xpre_ready, MT * b + (MT * PRE + m + 1))
                        pool.wait_ge(x2_ready, MT * b + (MT * (PRE - 1) + m + 1))
                        pool.sem_inc(waited, 1)
                        nc.gpsimd.tensor_scalar(acc[m][:, :], xpre[m][:, 0:BLK], t.cw[:, m, 0:1], t.cb[:, m:m + 1],
                                                ALU.mult, ALU.add).then_inc(tap0_done, 1)

            for bt in range(s.B):
                pool.wait_ge(halo_reset, MT * (bt + 1))
                with pool.Fori(bt * s.BPB // 2, (bt + 1) * s.BPB // 2) as j:
                    for p in range(2):
                        block_steps(j, p)

        @block.scalar
        def _(act):
            for c, n in ((xn_hi_ready, KT * PRE), (xpre_ready, MT * PRE), (x2_ready, MT * PRE),
                         (zs_ready, MT * PRE), (xn_stored[0], 16), (xn_stored[1], 16), (x2_stored[0], 16),
                         (x2_stored[1], 16), (zs_stored[0], 16), (zs_stored[1], 16)):
                act.sem_inc(c, n)
            nc.scalar.activation(wx_hi[:, :, :], t.wx[:, :, :], ACT.Copy).then_inc(w_hi, 1)
            nc.scalar.activation(wz_hi[:, :, :], t.wz[:, :, :], ACT.Copy).then_inc(w_hi, 1)
            nc.scalar.activation(wr2[:, :, 0, :], t.wr[:, :, :], ACT.Copy).then_inc(w_hi, 1)

            def x_out(b, m):
                act.wait_ge(x_ready, MT * b + (MT * PRE + m + 1))
                act.wait_ge(halo_done, MT * b + (MT * (PRE - 1) + m + 1))
                nc.scalar.activation(xpre[m][:, 3:3 + BLK], ps_x[m % 2][:, :], ACT.Copy).then_inc(xpre_ready, 1)

            def x_silu(b, p, m):
                act.wait_ge(conv_done, MT * b + (MT * PRE + m + 1))
                nc.scalar.activation(x2[p][:, m, :], acc[m][:, :], ACT.Silu).then_inc(x2_ready, 1)

            def z_silu(b, p, m):
                act.wait_ge(z_ready, MT * b + (MT * PRE + m + 1))
                nc.scalar.activation(zs[p][:, m, :], ps_z[m % 2][:, :], ACT.Silu).then_inc(zs_ready, 1)

            with act.Fori(0, s.NB // 2) as j:
                for p in range(2):
                    b = 2 * j + p
                    act.wait_ge(z_ready, MT * b + MT * (PRE - 1))
                    for k in range(KT):
                        act.wait_ge(xnT_ready, KT * b + (KT * PRE + k + 1))
                        nc.scalar.activation(xn_hi[p][:, k, :], ps_t[k][:, :], ACT.Copy).then_inc(xn_hi_ready, 1)
                    act.wait_ge(x2_stored[p], 16 * j + 16)
                    act.wait_ge(dt_ready, b + (PRE - 1))
                    act.wait_ge(zs_stored[p], 16 * j + 16)
                    x_out(b, 0)
                    x_out(b, 1)
                    x_out(b, 2)
                    x_silu(b, p, 0)
                    x_out(b, 3)
                    for m in range(1, MT):
                        z_silu(b, p, m - 1)
                        x_silu(b, p, m)
                    z_silu(b, p, MT - 1)
                    act.wait_ge(x2_ready, MT * b + MT * (PRE + 1))
                    act.dma_start(t.x2_dram[b], x2[p][:, :, :]).then_inc(x2_stored[p], 16)
                    act.wait_ge(zs_ready, MT * b + MT * (PRE + 1))
                    act.dma_start(t.zs_dram[b], zs[p][:, :, :]).then_inc(zs_stored[p], 16)
            for p in range(2):
                for c in (xn_stored[p], x2_stored[p], zs_stored[p]):
                    act.wait_ge(c, 16 * (s.NB // 2 + 1))

        @block.vector
        def _(dve):
            for c, n in ((xn_lo_ready, KT * PRE), (conv_done, MT * PRE), (halo_done, MT * PRE),
                         (lg_copied, PRE), (dt_copied, PRE)):
                dve.sem_inc(c, n)
            for n, (lo, raw, hi) in enumerate(((wx_lo[:, :, :], t.wx[:, :, :], wx_hi[:, :, :]),
                                               (wz_lo[:, :, :], t.wz[:, :, :], wz_hi[:, :, :]),
                                               (wr2[:, :, 1, :], t.wr[:, :, :], wr2[:, :, 0, :]))):
                dve.wait_ge(w_hi, n + 1)
                nc.vector.tensor_tensor(lo, raw, hi.bitcast(F32), ALU.subtract).then_inc(w_lo, 1)

            def conv(b, m):
                for k in range(1, 4):
                    if k == 1:
                        dve.wait_ge(tap0_done, MT * b + (MT * PRE + m + 1))
                    else:
                        dve.wait_ge(taps, 2 * MT * b + (2 * m + k - 1))
                    n = nc.vector.scalar_tensor_tensor(acc[m][:, :], xpre[m][:, k:k + BLK], t.cw[:, m, k:k + 1],
                                                       acc[m][:, :], ALU.mult, ALU.add)
                    n.then_inc(taps if k < 3 else conv_done, 1)
                dve.wait_ge(conv_done, MT * b + (MT * PRE + m + 1))
                nc.vector.tensor_copy(xpre[m][:, 0:3], xpre[m][:, BLK:BLK + 3]).then_inc(halo_done, 1)

            def block_steps(j, p):
                b = 2 * j + p
                for k in range(KT):
                    dve.wait_ge(xn_hi_ready, KT * b + (KT * PRE + k + 1))
                    nc.vector.tensor_tensor(xn_lo[p][:, k, :], ps_t[k][:, :], xn_hi[p][:, k, :].bitcast(F32),
                                            ALU.subtract).then_inc(xn_lo_ready, 1)
                for m in range(MT):
                    conv(b, m)
                dve.wait_ge(lg_ready, b + 1)
                nc.vector.tensor_copy(t.logit2[:, bass.ds(CH * b, CH), :, :],
                                      ps_lg[:, 0:CH * 2 * s.E].rearrange("p (c k e) -> p c k e", c=CH, k=2)
                                      ).then_inc(lg_copied, 1)
                dve.wait_ge(dt_ready, b + (PRE + 1))
                nc.vector.tensor_copy(t.dt[:, bass.ds(CH * b, CH), :],
                                      ps_dt[:, 0:CH * s.H].rearrange("p (c h) -> p c h", c=CH)).then_inc(dt_copied, 1)

            for bt in range(s.B):
                if bt:
                    dve.wait_ge(halo_done, MT * (bt * s.BPB + PRE))
                for m in range(MT):
                    n = nc.vector.memset(xpre[m][:, 0:3], 0.0)
                    n.then_inc(halo_reset, 1)
                dve.wait_ge(halo_reset, MT * (bt + 1))
                with dve.Fori(bt * s.BPB // 2, (bt + 1) * s.BPB // 2) as j:
                    for p in range(2):
                        block_steps(j, p)

        @block.tensor
        def _(pe):
            for c, n in ((xnT_ready, KT * PRE), (x_ready, MT * PRE), (z_ready, MT * PRE), (dt_ready, PRE)):
                pe.sem_inc(c, n)
            pe.wait_ge(w_lo, 3)

            def project(b, p, m, w, ps, ready, drained):
                pe.wait_ge(drained, MT * b + (MT * PRE + m - 2 + 1))
                n = 0
                for k in range(KT):
                    for wgt, act_in in ((w[0], xn_hi[p]), (w[1], xn_hi[p]), (w[0], xn_lo[p])):
                        if m == 0 and ready is x_ready:
                            pe.wait_ge(xn_hi_ready if act_in is xn_hi[p] else xn_lo_ready,
                                       KT * b + (KT * PRE + k + 1))
                        mm = pe.matmul(ps[m % 2][:, :], wgt[:, k, m * P:(m + 1) * P], act_in[:, k, :],
                                       start=(n == 0), stop=(n == 3 * KT - 1))
                        n += 1
                mm.then_inc(ready, 1)

            with pe.Fori(0, s.NB // 2) as j:
                for p in range(2):
                    b = 2 * j + p
                    pe.wait_ge(xn_ready, b + (PRE + 1))
                    for k in range(KT):
                        pe.wait_ge(xn_lo_ready, KT * b + (KT * (PRE - 1) + k + 1))
                        for c in range(CH):
                            mm = pe.transpose(ps_t[k][:, c * P:(c + 1) * P], xn[p][:, c, k * P:(k + 1) * P], t.ident)
                        mm.then_inc(xnT_ready, 1)
                    for m in range(MT):
                        project(b, p, m, (wx_hi, wx_lo), ps_x, x_ready, xpre_ready)
                    pe.wait_ge(lg_copied, b + PRE)
                    for c in range(CH):
                        for n, (k, half) in enumerate((k, half) for k in range(KT) for half in (xn_hi[p], xn_lo[p])):
                            mm = pe.matmul(ps_lg[:, c * 2 * s.E:(c + 1) * 2 * s.E], half[:, k, c * P:(c + 1) * P],
                                           wr2[:, k, :, :], start=(n == 0), stop=(n == 2 * KT - 1))
                    mm.then_inc(lg_ready, 1)
                    for m in range(MT):
                        project(b, p, m, (wz_hi, wz_lo), ps_z, z_ready, zs_ready)
                    pe.wait_ge(dt_copied, b + PRE)
                    pe.wait_ge(x2_ready, MT * b + MT * (PRE + 1))
                    for c in range(CH):
                        for k in range(MT):
                            mm = pe.matmul(ps_dt[:, c * s.H:(c + 1) * s.H], x2[p][:, k, c * P:(c + 1) * P],
                                           t.wdt[:, k, :], start=(k == 0), stop=(k == MT - 1))
                    mm.then_inc(dt_ready, 1)


def phase_decays(nc, s, t, wb_d, wc_d):
    NT, E, H, GT, SEG = s.NT, s.E, s.H, s.GT, s.SEG
    with ExitStack() as ctx:
        def sem(name):
            return ctx.enter_context(nc.semaphore(name))

        def sb(name, shape, dt=F32):
            return ctx.enter_context(nc.sbuf_tensor(name, shape, dt))

        u, e1, w1, ln, q, z, rec, dta, gap, ecum, wexp, dec8, lsum = (
            sb(f"r_{n}", [P, NT, 8]) for n in ("u", "e1", "w1", "ln", "q", "z", "rec", "dta", "gap", "ecum",
                                               "wexp", "dec8", "lsum"))
        a_pos = sb("r_a_pos", [P, 1, 8])
        top, esum, einv = (sb(f"r_{n}", [P, NT, 1]) for n in ("top", "esum", "einv"))
        gates_g = sb("r_gates_g", [P, GT, s.NSEG, E])
        rowsT = sb("rowsT", [P, 2, GT, P])
        w_raw = [sb(f"w_raw{i}", [P, s.MT, s.INNER]) for i in range(2)]
        zero = sb("zero", [P, 8, s.D])
        ps = t.ps

        vec, sca, ten = sem("r_vec"), sem("r_sca"), sem("r_ten")
        zeroed = sem("r_zeroed")
        stored = sem("r_stored")
        w_loaded, w_hi, w_lo = [sem(f"r_w_loaded{i}") for i in range(2)], sem("r_w_hi"), sem("r_w_lo")
        block = ctx.enter_context(nc.Block())

        def wide(ap, shape):
            return ap.to_broadcast(shape)

        steps = {}

        @block.vector
        def _(dve):
            n = [0]

            def do(ins, name=None):
                n[0] += 1
                ins.then_inc(vec, 1)
                dve.wait_ge(vec, n[0])
                if name:
                    assert steps.setdefault(name, n[0]) == n[0]

            full = [P, NT, 8]
            v = nc.vector
            do(v.tensor_tensor(u[:, :, :], t.dt[:, :, :], wide(t.rows[:, 1:2, :], full), ALU.add), "u")
            dve.wait_ge(sca, 3)
            do(v.tensor_scalar(w1[:, :, :], e1[:, :, :], 1.0, None, ALU.add), "w1")
            do(v.tensor_scalar(q[:, :, :], w1[:, :, :], -1.0, None, ALU.add))
            do(v.scalar_tensor_tensor(z[:, :, :], q[:, :, :], 0.0, e1[:, :, :], ALU.is_equal, ALU.mult))
            do(v.tensor_scalar(gap[:, :, :], q[:, :, :], 1e-30, None, ALU.max))
            do(v.reciprocal(rec[:, :, :], gap[:, :, :]))
            do(v.tensor_tensor(q[:, :, :], rec[:, :, :], e1[:, :, :], ALU.mult))
            dve.wait_ge(sca, 4)
            do(v.tensor_tensor(rec[:, :, :], q[:, :, :], ln[:, :, :], ALU.mult))
            do(v.tensor_tensor(q[:, :, :], rec[:, :, :], z[:, :, :], ALU.add))
            do(v.scalar_tensor_tensor(t.dt[:, :, :], u[:, :, :], 0.0, q[:, :, :], ALU.max, ALU.add))
            do(v.scalar_tensor_tensor(dta[:, :, :], t.dt[:, :, :], -1.0, wide(a_pos[:, :, :], full), ALU.mult,
                                      ALU.mult), "dta")
            dve.wait_ge(ten, 2)
            psc = [ps[i][:, 0:NT * H].rearrange("p (t h) -> p t h", h=H) for i in range(2)]
            do(v.tensor_copy(t.cum[:, :, :], psc[0]), "cum")
            do(v.tensor_tensor(gap[:, :, :], psc[1], t.cum[:, :, :], ALU.subtract), "gap")
            dve.wait_ge(sca, 7)
            do(v.tensor_tensor(t.wst[:, :, :], wexp[:, :, :], t.dt[:, :, :], ALU.mult))
            for a in range(2):
                half = slice(a * s.HD, (a + 1) * s.HD)
                do(v.tensor_copy(t.dec[half, :, :], dec8[half, :, a:8:2]))
            dve.wait_ge(ten, 4)
            for i in range(2):
                do(v.tensor_copy(rowsT[:, i, :, :], ps[2 + i][:, 0:GT * P].rearrange("p (g c) -> p g c", g=GT)),
                   f"rows{i}")
            do(v.tensor_tensor(lsum[:, :, :], t.logit2[:, :, 0, :], t.logit2[:, :, 1, :], ALU.add))
            do(v.tensor_tensor(u[:, :, :], lsum[:, :, :], wide(t.rows[:, 2:3, :], full), ALU.add))
            do(v.tensor_reduce(top[:, :, :], u[:, :, :], AX.X, ALU.max))
            do(v.tensor_tensor(lsum[:, :, :], u[:, :, :], wide(top[:, :, :], full), ALU.subtract), "shifted")
            dve.wait_ge(sca, 8)
            do(v.tensor_reduce(esum[:, :, :], ecum[:, :, :], AX.X, ALU.add))
            do(v.reciprocal(einv[:, :, :], esum[:, :, :]))
            do(v.tensor_tensor(t.gates[:, :, :], ecum[:, :, :], wide(einv[:, :, :], full), ALU.mult), "gates")
            do(v.tensor_copy(gates_g[:, :, :, :], t.gates[:, :, :].rearrange("p (q g) e -> p g q e", g=GT)), "gates_g")
            dve.wait_ge(ten, 5)
            do(v.tensor_copy(t.gateT[:, :], ps[4][:, 0:SEG]))

        @block.scalar
        def _(act):
            def split(n):
                act.wait_ge(w_loaded[n], 16)
                nc.scalar.activation(t.wbc_hi[n][:, :, :], w_raw[n][:, :, :], ACT.Copy).then_inc(w_hi, 1)

            nc.scalar.activation(a_pos[:, :, :], t.rows[:, 0:1, :], ACT.Exp).then_inc(sca, 1)
            act.wait_ge(vec, steps["u"])
            nc.scalar.activation(gap[:, :, :], u[:, :, :], ACT.Abs).then_inc(sca, 1)
            act.wait_ge(sca, 2)
            nc.scalar.activation(e1[:, :, :], gap[:, :, :], ACT.Exp, scale=-1.0).then_inc(sca, 1)
            act.wait_ge(vec, steps["w1"])
            nc.scalar.activation(ln[:, :, :], w1[:, :, :], ACT.Ln).then_inc(sca, 1)
            split(0)
            act.wait_ge(vec, steps["cum"])
            nc.scalar.activation(ecum[:, :, :], t.cum[:, :, :], ACT.Exp).then_inc(sca, 1)
            act.wait_ge(vec, steps["gap"])
            nc.scalar.activation(wexp[:, :, :], gap[:, :, :], ACT.Exp).then_inc(sca, 1)
            nc.scalar.activation(dec8[:, :, :], ps[1][:, 0:NT * H].rearrange("p (t h) -> p t h", h=H),
                                 ACT.Exp).then_inc(sca, 1)
            split(1)
            act.wait_ge(vec, steps["shifted"])
            act.wait_ge(ten, 4)
            nc.scalar.activation(ecum[:, :, :], lsum[:, :, :], ACT.Exp).then_inc(sca, 1)

        @block.tensor
        def _(pe):
            pe.wait_ge(vec, steps["dta"])
            flat = dta[:, :, :].rearrange("p t h -> p (t h)")
            pe.matmul(ps[0][:, 0:NT * H], t.tri, flat, start=True, stop=True).then_inc(ten, 1)
            pe.matmul(ps[1][:, 0:NT * H], t.ones, flat, start=True, stop=True).then_inc(ten, 1)
            for i, (src, ready, n) in enumerate(((t.cum, vec, steps["cum"]), (ecum, sca, 5))):
                pe.wait_ge(ready, n)
                for g in range(GT):
                    mm = pe.transpose(ps[2 + i][:, g * P:(g + 1) * P],
                                      src[:, g * s.NSEG:(g + 1) * s.NSEG, :].rearrange("p t h -> p (t h)"), t.ident)
                mm.then_inc(ten, 1)
            pe.wait_ge(vec, steps["gates_g"])
            for g in range(GT):
                mm = pe.transpose(ps[4][:, g * P:(g + 1) * P],
                                  gates_g[:, g, :, :].rearrange("p q e -> p (q e)"), t.ident)
            mm.then_inc(ten, 1)

        @block.gpsimd
        def _(pool):
            nc.gpsimd.memset(zero[:, :, :], 0.0).then_inc(zeroed, 1)
            for n in range(2):
                pool.wait_ge(w_hi, n + 1)
                nc.gpsimd.tensor_tensor(t.wbc_lo[n][:, :, :], w_raw[n][:, :, :], t.wbc_hi[n][:, :, :].bitcast(F32),
                                        ALU.subtract).then_inc(w_lo, 1)

        @block.sync
        def _(sp):
            for n, w in enumerate((wb_d, wc_d)):
                sp.dma_start(w_raw[n][:, :, :], w.rearrange("(k p) n -> p k n", p=P)).then_inc(w_loaded[n], 16)
            sp.wait_ge(zeroed, 1)
            for k in range(s.T // (8 * P)):
                sp.dma_start(t.ffn_dram[8 * P * k:8 * P * (k + 1), :].rearrange("(p c) d -> p c d", p=P),
                             zero[:, :, :]).then_inc(stored, 16)
            sp.wait_ge(vec, steps["rows1"])
            for i, dst in enumerate((t.cum_dram, t.ecum_dram)):
                sp.dma_start(dst.rearrange("(g t) h c -> (t h) g c", t=s.NSEG), rowsT[:, i, :, :]).then_inc(stored, 16)
            sp.wait_ge(vec, steps["gates"])
            sp.dma_start(t.rows_dram[:, s.D:s.ROW].rearrange("(t p) e -> p t e", p=P), t.gates[:, :, :]).then_inc(
                stored, 16)
            sp.wait_ge(stored, 16 * (3 + s.T // (8 * P)))


def phase_scan(nc, s, t):
    MT, H, HD, NB = s.MT, s.H, s.HD, s.NB
    NT, E, LW, GT, SEG, FIRST = s.NT, s.E, s.LW, s.GT, s.SEG, s.BPB * CH
    CPRE = PRE * CH
    with ExitStack() as ctx:
        def sem(name):
            return ctx.enter_context(nc.semaphore(name))

        def sb(name, shape, dt=F32):
            return ctx.enter_context(nc.sbuf_tensor(name, shape, dt))

        (wb_hi, wc_hi), (wb_lo, wc_lo) = t.wbc_hi, t.wbc_lo
        x2 = [sb(f"x2_{i}", [P, MT, BLK]) for i in range(2)]
        x_raw = [sb(f"x_raw{i}", [P, BLK]) for i in range(2)]
        x_hi = [sb(f"x_hi{i}", [P, MT, BLK], F32R) for i in range(2)]
        x_lo = [sb(f"x_lo{i}", [P, MT, BLK], F32R) for i in range(2)]
        bT = [sb(f"bT{i}", [P, MT, BLK]) for i in range(2)]
        cT = [sb(f"cT{i}", [P, MT, BLK]) for i in range(2)]
        cum_row = [sb(f"cum_row{i}", [P, H, P]) for i in range(2)]
        ecum_row = [sb(f"ecum_row{i}", [P, MT, P]) for i in range(2)]
        decay = sb("decay", [P, H, P])
        mix = sb("mix", [P, H, P])
        b_tok = sb("b_tok", [P, s.INNER])
        x_dt = sb("x_dt", [P, MT, 2, P])
        x_w = sb("x_w", [P, s.INNER])
        c_dec = sb("c_dec", [P, MT, P])
        state = sb("state", [P, MT, P])
        yb = [sb(f"yb{i}", [P, MT, BLK]) for i in range(2)]
        ps_g, ps_y, ps_s, ps_xb, ps_r, ps_pb, ps_pc = (t.ps[0:2], t.ps[2], t.ps[3], t.ps[4], t.ps[5], t.ps[6],
                                                       t.ps[7])
        spare = [mix[:, 4 * i:4 * i + 4, :].rearrange("p h n -> p (h n)") for i in range(2)]
        spare += [x_w[:, :], c_dec[:, :, :].rearrange("p m n -> p (m n)")]
        chosen = sb("chosen", [P, SEG])
        bit_i = sb("bit_i", [P, C_END - C_BIT], I32)
        thr, cand, delta = (sb(f"r_{n}", [P, 1], I32) for n in ("thr", "cand", "delta"))
        part, lim, lim2 = (sb(f"r_{n}", [P, 1]) for n in ("part", "lim", "lim2"))
        counts = sb("counts", [P, 4])
        one_hi = [sb(f"one_hi{i}", [P, E, P], BF16) for i in range(2)]
        iota_b = sb("iota_b", [P, P], BF16)
        one_lo = [sb(f"one_lo{i}", [P, E, LW]) for i in range(2)]
        val_lo = [sb(f"val_lo{i}", [P, E, 2, LW], BF16) for i in range(2)]
        zero_b = sb("zero_b", [P, P], BF16)
        lists = sb("lists", [P, E, 2, LW])
        idx_f = sb("idx_f", [P, E, LW])
        hi, lo = (a.rearrange("p (t e) -> p t e", e=E) for a in (t.gateT[:, :], chosen[:, :]))

        zeroed = sem("b_zeroed")
        sel_step, sel_mm = sem("b_sel_step"), sem("b_sel_mm")
        part_done, total_done, bit_step = sem("b_part"), sem("b_total"), sem("b_bit")
        one_lo_done, tile_done, tile_used = sem("b_one_lo"), sem("b_tile"), sem("b_tile_used")
        steps = {}
        state_zeroed = sem("b_state_zeroed")
        x2_loaded = [sem(f"b_x2_loaded{i}") for i in range(2)]
        raw_loaded = [sem(f"b_raw_loaded{i}") for i in range(2)]
        cum_loaded = [sem(f"b_cum_loaded{i}") for i in range(2)]
        ecum_loaded = [sem(f"b_ecum_loaded{i}") for i in range(2)]
        y_stored = [sem(f"b_y_stored{i}") for i in range(2)]
        sp_waited = sem("b_sp_waited")
        waited = sem("b_waited")
        dx_ready, stat_done = sem("b_dx"), sem("b_stat")
        x_hi_ready, x_lo_ready, b_ready, c_ready, b_out, c_out = (
            sem(f"b_{n}") for n in ("x_hi", "x_lo", "b_ready", "c_ready", "b_out", "c_out"))
        x_turned, b_turned, b_tok_ready, g_ready, c_dec_ready, x_dt_ready, x_w_ready = (
            sem(f"b_{n}") for n in ("xt", "bt", "btok", "g", "cdec", "xdt", "xw"))
        gap_ready, exp_ready, decay_ready, mix_ready, y_mm, s_mm, y_ready, state_scaled, state_ready = (
            sem(f"b_{n}") for n in ("gap", "exp", "decay", "mix", "ymm", "smm", "y", "sscaled", "state"))
        block = ctx.enter_context(nc.Block())

        def at(g, back=0):
            return g + (1 + CPRE - back)

        def run(eng, body):
            for bt in range(s.B):
                body_start = bt * s.BPB // 2
                body_end = (bt + 1) * s.BPB // 2 - (1 if bt == s.B - 1 else 0)
                body(bt, None, 0, False, False)
                if body_end > body_start:
                    with eng.Fori(body_start, body_end) as j:
                        for p in range(2):
                            body(bt, 2 * j + p, p, True, True)
            for p in range(2):
                body(None, NB - 2 + p, p, p == 0, False)

        def half_value(b, p, per_pair):
            return (b - p) * (8 * per_pair) + 16 * per_pair

        @block.vector
        def _(dve):
            v = nc.vector
            for c, n in ((gap_ready, CPRE), (x_dt_ready, CPRE),
                         (x_w_ready, CPRE), (mix_ready, 2 * CPRE), (y_ready, CPRE), (state_ready, 2 * CPRE),
                         (stat_done, PRE), (y_stored[0], 16), (y_stored[1], 16)):
                dve.sem_inc(c, n)

            def gaps(g, q, loaded):
                dve.wait_ge(cum_loaded[q], loaded)
                dve.wait_ge(mix_ready, 2 * g + 2 * CPRE)
                for h in range(H):
                    n = v.tensor_scalar(decay[:, (h % 2) * MT + h // 2, :], cum_row[q][:, h, :],
                                        t.cum[:, bass.ds(g, 1), h:h + 1].rearrange("p a b -> p (a b)"), 0.0,
                                        ALU.subtract, ALU.min)
                n.then_inc(gap_ready, 1)

            def heads(ap, g):
                return ap[:, bass.ds(g, 1), :].rearrange("p a h -> p h a").to_broadcast([P, H, HD])

            n = [0]

            def do(ins, name=None):
                n[0] += 1
                ins.then_inc(sel_step, 1)
                dve.wait_ge(sel_step, n[0])
                if name:
                    steps[name] = n[0]

            def count(i):
                v.tensor_tensor(cand[:, :], thr[:, :], bit_i[:, bass.ds(i, 1)], ALU.bitwise_or).then_inc(bit_step, 1)
                dve.wait_ge(bit_step, 3 * i + 1)
                v.tensor_scalar(chosen[:, :], t.gateT[:, :], cand[:, :].bitcast(F32), 0.0, ALU.is_ge, ALU.add,
                                accum_out=part[:, :]).then_inc(part_done, 1)

            def next_bit(g):
                dve.wait_ge(total_done, g + 1)
                v.tensor_scalar(delta[:, :], ps_r[:, 0:1], float(s.CAP), t.cst[:, bass.ds(C_BIT + g, 1)],
                                ALU.is_ge, ALU.mult).then_inc(bit_step, 1)
                dve.wait_ge(bit_step, 3 * g + 2)
                v.tensor_tensor(thr[:, :], thr[:, :], delta[:, :], ALU.bitwise_or).then_inc(bit_step, 1)
                dve.wait_ge(bit_step, 3 * g + 3)
                count(g + 1)

            def select():
                dve.wait_ge(y_mm, CH * s.BPB + CPRE)
                dve.wait_ge(part_done, FIRST + 1)
                slot_i, hi_i, lo_i = (a.bitcast(I32).rearrange("p (t e) -> p t e", e=E) for a in spare[1:4])
                ones_row = t.ones[:, 0:1].to_broadcast([P, SEG])
                tf = thr[:, :].bitcast(F32)
                do(v.tensor_scalar(spare[0], t.gateT[:, :], tf, 0.0, ALU.is_gt, ALU.add, accum_out=counts[:, 0:1]))
                do(v.tensor_scalar(spare[1], t.gateT[:, :], tf, 0.0, ALU.is_equal, ALU.add, accum_out=counts[:, 1:2]),
                   "counts")
                do(v.tensor_tensor_scan(spare[2], ones_row, spare[1], 0.0, ALU.mult, ALU.add))
                dve.wait_ge(sel_mm, 1)
                do(v.tensor_scalar(lim[:, :], ps_r[:, 0:1], -1.0, float(s.CAP), ALU.mult, ALU.add))
                do(v.tensor_tensor(lim2[:, :], ps_r[:, 1:2], lim[:, :], ALU.subtract))
                do(v.tensor_scalar(lim[:, :], lim2[:, :], -1.0, None, ALU.mult))
                do(v.scalar_tensor_tensor(spare[3], spare[2], lim[:, :], spare[1], ALU.is_le, ALU.mult))
                do(v.tensor_tensor(chosen[:, :], spare[0], spare[3], ALU.add))
                do(v.tensor_tensor_scan(spare[2], ones_row, chosen[:, :], 0.0, ALU.mult, ALU.add))
                do(v.tensor_copy(counts[:, 2:3], spare[2][:, SEG - 1:SEG]), "selected")
                dve.wait_ge(sel_mm, 2)
                do(v.tensor_scalar(lim2[:, :], ps_r[:, 2:3], 0.0, None, ALU.add))
                do(v.scalar_tensor_tensor(spare[3], spare[2], lim2[:, :], chosen[:, :], ALU.add, ALU.mult))
                do(v.tensor_scalar(spare[0], spare[3], -1.0, None, ALU.add), "slot")
                dve.wait_ge(sel_mm, 3)
                do(v.tensor_copy(slot_i.rearrange("p (q g) e -> p g q e", g=GT),
                                 ps_r[:, 0:SEG].rearrange("p (g q e) -> p g q e", g=GT, e=E)),
                   "slot_i")
                do(v.tensor_scalar(hi_i, slot_i, LW.bit_length() - 1, None, ALU.arith_shift_right))
                do(v.tensor_scalar(lo_i, slot_i, LW - 1, None, ALU.bitwise_and))
                do(v.tensor_copy(hi, hi_i))
                do(v.tensor_copy(lo, lo_i), "lo")

            def token_tile(g, q):
                i = 2 * g + (q - 2 * FIRST)
                dve.wait_ge(tile_used, i + 1)
                v.tensor_tensor(one_lo[q][:, :, :], lo[:, bass.ds(i, 1), :].rearrange("p a e -> p e a")
                                .to_broadcast([P, E, LW]),
                                t.cst[:, C_LO:C_LO + LW].unsqueeze(1).to_broadcast([P, E, LW]),
                                ALU.is_equal).then_inc(one_lo_done, 1)
                for e in range(E):
                    v.tensor_scalar(one_hi[q][:, e, :], iota_b[:, :],
                                    hi[:, bass.ds(i, 1), e:e + 1].rearrange("p a e -> p (a e)"), None, ALU.is_equal)
                dve.wait_ge(one_lo_done, i + 1)
                v.tensor_scalar(val_lo[q][:, :, 0, :], one_lo[q][:, :, :], t.cst[:, bass.ds(C_TAU + i, 1)],
                                None, ALU.mult)
                v.tensor_scalar(val_lo[q][:, :, 1, :], one_lo[q][:, :, :], t.cst[:, C_PIDX:C_PIDX + 1],
                                None, ALU.mult).then_inc(tile_done, 1)

            def body(bt, b, p, nxt, nxt2):
                if b is None:
                    dve.wait_ge(s_mm, CH * bt * s.BPB + CPRE)
                    dve.wait_ge(state_ready, 2 * CH * bt * s.BPB + 2 * CPRE)
                    v.memset(state[:, :, :], 0.0).then_inc(state_zeroed, 1)
                    dve.wait_ge(state_zeroed, bt + 1)
                    if bt == 1:
                        select()
                        for q in range(2):
                            token_tile(FIRST, q)
                    return
                for c in range(CH):
                    g = CH * b + c
                    cols = slice(c * P, (c + 1) * P)
                    dve.wait_ge(y_mm, at(g, 1))
                    dve.wait_ge(x_turned, at(g))
                    x_heads = ps_xb[:, :].rearrange("p (h n) -> p h n", h=H)
                    for a in range(2):
                        n = v.tensor_tensor(x_dt[:, :, a, a * HD:(a + 1) * HD], x_heads[:, a:H:2, :],
                                            heads(t.dt, g)[:, a:H:2, :], ALU.mult)
                    n.then_inc(x_dt_ready, 1)
                    dve.wait_ge(s_mm, at(g, 1))
                    v.tensor_tensor(x_w[:, :].rearrange("p (h n) -> p h n", h=H), x_heads, heads(t.wst, g),
                                    ALU.mult).then_inc(x_w_ready, 1)
                    dve.wait_ge(decay_ready, at(g))
                    for i in range(2):
                        dve.wait_ge(g_ready, g + 1)
                        v.tensor_tensor(mix[:, 4 * i:4 * i + 4, :],
                                        ps_g[i][:, :].rearrange("p (h n) -> p h n", h=4),
                                        decay[:, 4 * i:4 * i + 4, :], ALU.mult).then_inc(mix_ready, 1)
                    if c < CH - 1 or nxt:
                        q = (c + 1) % 2
                        gaps(g + 1, q, (b - 0) * 32 + (16 * ((c + 1) // 2 + 1)))
                    if bt == 0:
                        next_bit(g)
                    elif c < CH - 1 or nxt:
                        for q in range(2):
                            token_tile(g + 1, q)
                    dve.wait_ge(y_mm, at(g))
                    if c == 0:
                        dve.wait_ge(dx_ready, b + (PRE + 1))
                    v.tensor_tensor(yb[p][:, :, cols], ps_y[:, :].rearrange("p (m n) -> p m n", m=MT),
                                    yb[p][:, :, cols], ALU.add).then_inc(y_ready, 1)
                    dve.wait_ge(state_ready, 2 * g + 2 * CPRE)
                    v.tensor_tensor(state[:, :, :], state[:, :, :],
                                    t.dec[:, bass.ds(g, 1), :].rearrange("p a m -> p m a").to_broadcast([P, MT, P]),
                                    ALU.mult).then_inc(state_scaled, 1)
                    dve.wait_ge(state_scaled, g + 1)
                    dve.wait_ge(s_mm, at(g))
                    for a in range(2):
                        r = slice(a * HD, (a + 1) * HD)
                        v.tensor_tensor(state[r, :, r], ps_s[r, :].rearrange("p (m n) -> p m n", m=MT)[:, :, r],
                                        state[r, :, r], ALU.add).then_inc(state_ready, 1)
                dve.wait_ge(y_ready, at(CH * b, 1 - CH))
                for m in range(MT):
                    n = v.bn_stats(t.ystat[:, bass.ds(b, 1), m, :].rearrange("p a k -> p (a k)"), yb[p][:, m, :])
                n.then_inc(stat_done, 1)

            gaps(0, 0, 16)
            v.memset(zero_b[:, :], 0.0).then_inc(zeroed, 1)
            do(v.memset(thr[:, :], 0))
            do(v.tensor_copy(iota_b[:, :], t.iota))
            do(v.tensor_copy(bit_i[:, :], t.cst[:, C_BIT:C_END]))
            count(0)
            run(dve, body)
            dve.wait_ge(sel_mm, 4)
            do(v.tensor_copy(lists[:, :, :, :], ps_r[:, 0:2 * E * LW].rearrange("p (e k l) -> p e k l", e=E, k=2)))
            do(v.scalar_tensor_tensor(idx_f[:, :, :], lists[:, :, 0, :], float(P), lists[:, :, 1, :], ALU.mult,
                                      ALU.add))
            do(v.tensor_copy(t.idx[:, :, :], idx_f[:, :, :]))

        @block.sync
        def _(sp):
            def load_raw(b, m):
                sp.wait_ge(x_lo_ready, MT * b + (m - 2 + 1 + CPRE))
                sp.dma_start(x_raw[m % 2][:, :], t.x2_dram[b][:, m, :]).then_inc(raw_loaded[m % 2], 16)

            def load_cum(g, q):
                sp.wait_ge(gap_ready, at(g, 2))
                sp.dma_start(cum_row[q][:, :, :], t.cum_dram[g].partition_broadcast(P)).then_inc(cum_loaded[q], 16)

            def load_ecum(g, q):
                sp.wait_ge(c_dec_ready, at(g, 2))
                for a in range(2):
                    sp.dma_start(ecum_row[q][a * HD:(a + 1) * HD, :, :],
                                 t.ecum_dram[g].rearrange("(m a) c -> a m c", a=2)[a].partition_broadcast(HD)
                                 ).then_inc(ecum_loaded[q], 16)

            def load_x2(b, p):
                sp.wait_ge(dx_ready, b + (PRE - 1))
                sp.sem_inc(sp_waited, 1)
                sp.wait_ge(x_turned, at(CH * b, CH + 1))
                sp.dma_start(x2[p][:, :, :], t.x2_dram[b]).then_inc(x2_loaded[p], 16)

            def body(bt, b, p, nxt, nxt2):
                if b is None:
                    return
                if nxt:
                    load_x2(b + 1, 1 - p)
                for c in range(CH):
                    g = CH * b + c
                    if c < CH - 1 or nxt:
                        load_ecum(g + 1, (c + 1) % 2)
                        load_cum(g + 1, (c + 1) % 2)
                    if nxt2:
                        load_raw(b + 2, c)
                sp.wait_ge(stat_done, b + (PRE + 1))
                sp.dma_start(t.y_dram[b], yb[p][:, :, :]).then_inc(y_stored[p], 16)

            load_x2(0, 0)
            for b in range(2):
                for m in range(MT):
                    load_raw(b, m)
            load_cum(0, 0)
            load_ecum(0, 0)
            run(sp, body)
            for p in range(2):
                sp.wait_ge(y_stored[p], 16 * (NB // 2 + 1))

        @block.gpsimd
        def _(pool):
            pool.sem_inc(dx_ready, PRE)
            for c in (decay_ready, x_lo_ready, c_dec_ready):
                pool.sem_inc(c, CPRE)
            nc.gpsimd.memset(x_dt[:, :, :, :], 0.0).then_inc(zeroed, 1)

            def causal(g):
                pool.wait_ge(exp_ready, at(g))
                pool.sem_inc(waited, 1)
                nc.gpsimd.affine_select(out=decay[:, :, :], in_=decay[:, :, :], compare_op=ALU.is_ge, fill=0.0,
                                        base=0, pattern=[[0, H], [1, P]], channel_multiplier=-1).then_inc(
                    decay_ready, 1)

            def lo_part(b, p, m):
                pool.wait_ge(x_hi_ready, MT * b + (m + 1 + CPRE))
                nc.gpsimd.tensor_tensor(x_lo[p][:, m, :], x_raw[m % 2][:, :], x_hi[p][:, m, :].bitcast(F32),
                                        ALU.subtract).then_inc(x_lo_ready, 1)

            def decay_c(b, p, g, c):
                pool.wait_ge(c_out, CH * b + CPRE + CH)
                pool.wait_ge(ecum_loaded[c % 2], b * 64 + (32 * (c // 2 + 1)))
                pool.wait_ge(y_mm, at(g, 1))
                nc.gpsimd.tensor_tensor(c_dec[:, :, :], cT[p][:, :, c * P:(c + 1) * P], ecum_row[c % 2][:, :, :],
                                        ALU.mult).then_inc(c_dec_ready, 1)

            def scale_x(b, p, m):
                if m == 0:
                    pool.wait_ge(x2_loaded[p], half_value(b, p, 1))
                    pool.wait_ge(y_stored[p], half_value(b, p, 1))
                    pool.sem_inc(waited, 1)
                n = nc.gpsimd.tensor_scalar(yb[p][:, m, :], x2[p][:, m, :], t.dcol[:, m:m + 1], 0.0, ALU.mult,
                                            ALU.add)
                if m == MT - 1:
                    n.then_inc(dx_ready, 1)

            def body(bt, b, p, nxt, nxt2):
                if b is None:
                    if bt == 1:
                        pool.wait_ge(sel_step, steps["lo"])
                    return
                for c in range(CH):
                    g = CH * b + c
                    decay_c(b, p, g, c)
                    if c < CH - 1 or nxt:
                        causal(g + 1)
                    if nxt:
                        scale_x(b + 1, 1 - p, c)
                    if nxt2:
                        lo_part(b + 2, p, c)

            for b in range(2):
                for m in range(MT):
                    lo_part(b, b, m)
            for m in range(MT):
                scale_x(0, 0, m)
            causal(0)
            run(pool, body)

        @block.scalar
        def _(act):
            for c in (exp_ready, b_out, c_out, b_tok_ready, x_hi_ready):
                act.sem_inc(c, CPRE)

            def hi_part(b, p, m, loaded):
                act.wait_ge(raw_loaded[m % 2], loaded)
                act.wait_ge(c_ready, MT * b + (MT * (PRE - 1)))
                nc.scalar.activation(x_hi[p][:, m, :], x_raw[m % 2][:, :], ACT.Copy).then_inc(x_hi_ready, 1)

            def b_part(b, p, m):
                act.wait_ge(b_ready, MT * b + (m + 1 + CPRE))
                nc.scalar.activation(bT[p][:, m, :], ps_pb[:, :], ACT.Copy).then_inc(b_out, 1)

            def c_part(b, p, m):
                act.wait_ge(c_ready, MT * b + (m + 1 + CPRE))
                nc.scalar.activation(cT[p][:, m, :], ps_pc[:, :], ACT.Copy).then_inc(c_out, 1)

            def decays(g):
                act.wait_ge(gap_ready, at(g))
                nc.scalar.activation(decay[:, :, :], decay[:, :, :], ACT.Exp).then_inc(exp_ready, 1)

            def body(bt, b, p, nxt, nxt2):
                if b is None:
                    return
                for c in range(CH):
                    g = CH * b + c
                    if nxt:
                        b_part(b + 1, 1 - p, c)
                    act.wait_ge(b_turned, at(g))
                    act.wait_ge(s_mm, at(g, 1))
                    nc.scalar.activation(b_tok[:, :], ps_xb[:, :], ACT.Copy).then_inc(b_tok_ready, 1)
                    if c < CH - 1 or nxt:
                        decays(g + 1)
                    if nxt:
                        c_part(b + 1, 1 - p, c)
                    if nxt2:
                        hi_part(b + 2, p, c, b * 32 + (16 * (4 + c // 2 + 1)))

            for b in range(2):
                for m in range(MT):
                    hi_part(b, b, m, 16 * (2 * b + m // 2 + 1))
            for m in range(MT):
                b_part(0, 0, m)
                c_part(0, 0, m)
            decays(0)
            run(act, body)

        @block.tensor
        def _(pe):
            for c in (b_ready, c_ready, x_turned, b_turned, y_mm, s_mm):
                pe.sem_inc(c, CPRE)

            def project(b, p, m, which):
                pe.wait_ge(x_lo_ready, MT * b + (MT + CPRE))
                for w_h, w_l, ps, ready, drained in (((wb_hi, wb_lo, ps_pb, b_ready, b_out),
                                                      (wc_hi, wc_lo, ps_pc, c_ready, c_out))[which],):
                    pe.wait_ge(drained, MT * b + (m + CPRE))
                    n = 0
                    for k in range(MT):
                        for w, x in ((w_h, x_hi[p]), (w_l, x_hi[p]), (w_h, x_lo[p])):
                            mm = pe.matmul(ps[:, :], w[:, k, m * P:(m + 1) * P], x[:, k, :],
                                           start=(n == 0), stop=(n == 3 * MT - 1))
                            n += 1
                    mm.then_inc(ready, 1)

            W = 2 * E * LW

            def select():
                pe.wait_ge(sel_step, steps["counts"])
                pe.matmul(ps_r[:, 0:1], t.rsum, counts[:, 0:1], start=True, stop=True)
                pe.matmul(ps_r[:, 1:2], t.rtri, counts[:, 1:2], start=True, stop=True).then_inc(sel_mm, 1)
                pe.wait_ge(sel_step, steps["selected"])
                pe.matmul(ps_r[:, 2:3], t.rtri, counts[:, 2:3], start=True, stop=True).then_inc(sel_mm, 1)
                pe.wait_ge(sel_step, steps["slot"])
                for g in range(GT):
                    mm = pe.transpose(ps_r[:, g * P:(g + 1) * P], spare[0][:, g * P:(g + 1) * P], t.ident)
                mm.then_inc(sel_mm, 1)
                pe.wait_ge(sel_step, steps["slot_i"])
                pe.matmul(ps_r[:, 0:W], zero_b[:, :], zero_b[:, 0:W], start=True, stop=False, skip_group_check=True)

            def list_tile(g, q):
                i = 2 * g + (q - 2 * FIRST)
                pe.wait_ge(tile_done, i + 1)
                for e in range(E):
                    mm = pe.matmul(ps_r[:, e * 2 * LW:(e + 1) * 2 * LW], one_hi[q][:, e, :],
                                   val_lo[q][:, e, :, :].rearrange("p k l -> p (k l)"),
                                   start=False, stop=False, skip_group_check=True)
                mm.then_inc(tile_used, 1)

            def body(bt, b, p, nxt, nxt2):
                if b is None:
                    if bt == 1:
                        select()
                    return
                pe.wait_ge(x2_loaded[p], half_value(b, p, 1))
                pe.wait_ge(b_out, MT * b + (MT + CPRE))
                pe.wait_ge(c_out, MT * b + (MT + CPRE))
                for c in range(CH):
                    g = CH * b + c
                    cols = slice(c * P, (c + 1) * P)
                    pe.wait_ge(b_tok_ready, at(g, 1))
                    for m in range(MT):
                        mm = pe.transpose(ps_xb[:, m * P:(m + 1) * P], x2[p][:, m, cols], t.ident)
                    mm.then_inc(x_turned, 1)
                    pe.wait_ge(mix_ready, 2 * g + 2 * CPRE)
                    for m in range(MT):
                        for a in range(2):
                            r = slice(a * HD, (a + 1) * HD)
                            mm = pe.matmul(ps_g[a][:, m * P:(m + 1) * P], bT[p][r, m, cols], cT[p][r, m, cols],
                                           start=True, stop=True)
                    mm.then_inc(g_ready, 1)
                    if bt == 0:
                        pe.wait_ge(part_done, g + 1)
                        pe.matmul(ps_r[:, 0:1], t.rsum, part[:, :], start=True, stop=True).then_inc(total_done, 1)
                    else:
                        for q in range(2):
                            list_tile(g, q)
                    if nxt:
                        project(b + 1, 1 - p, c, 0)
                    pe.wait_ge(x_w_ready, at(g))
                    pe.wait_ge(x_dt_ready, at(g))
                    for m in range(MT):
                        mm = pe.transpose(ps_xb[:, m * P:(m + 1) * P], bT[p][:, m, cols], t.ident)
                    mm.then_inc(b_turned, 1)
                    if nxt:
                        project(b + 1, 1 - p, c, 1)
                    pe.wait_ge(y_ready, at(g, 1))
                    pe.wait_ge(x_dt_ready, at(g))
                    pe.wait_ge(c_dec_ready, at(g))
                    pe.wait_ge(mix_ready, 2 * g + (2 * CPRE + 2))
                    pe.wait_ge(state_ready, 2 * g + 2 * CPRE)
                    for m in range(MT):
                        out = ps_y[:, m * P:(m + 1) * P]
                        for a in range(2):
                            pe.matmul(out, x_dt[:, m, a, :], mix[:, a * MT + m, :], start=(a == 0), stop=False)
                        mm = pe.matmul(out, state[:, m, :], c_dec[:, m, :], start=False, stop=True)
                    mm.then_inc(y_mm, 1)
                    pe.wait_ge(x_w_ready, at(g))
                    pe.wait_ge(b_tok_ready, at(g))
                    for m in range(MT):
                        mm = pe.matmul(ps_s[:, m * P:(m + 1) * P], b_tok[:, m * P:(m + 1) * P],
                                       x_w[:, m * P:(m + 1) * P], start=True, stop=True)
                    mm.then_inc(s_mm, 1)

            pe.wait_ge(zeroed, 2)
            pe.sem_inc(tile_used, 2)
            for m in range(MT):
                project(0, 0, m, 0)
                project(0, 0, m, 1)
            run(pe, body)
            pe.matmul(ps_r[:, 0:W], zero_b[:, :], zero_b[:, 0:W], start=False, stop=True,
                      skip_group_check=True).then_inc(sel_mm, 1)


def phase_experts(nc, s, t, wup_d, bup_d, wdn_d):
    KT, FT, FR, F, HC, NH, E = s.KT, s.FT, s.FR, s.F, s.HC, s.NH, s.E
    HALF, GS = s.HALF, s.GS
    with ExitStack() as ctx:
        def sem(name):
            return ctx.enter_context(nc.semaphore(name))

        def sb(name, shape, dt=F32):
            return ctx.enter_context(nc.sbuf_tensor(name, shape, dt))

        up_raw = sb("up_raw", [P, KT, F])
        up_hi = [sb(f"up_hi{i}", [P, KT, F], F32R) for i in range(2)]
        up_lo = [sb(f"up_lo{i}", [P, KT, F], F32R) for i in range(2)]
        b_up = [sb(f"b_up{i}", [P, FT]) for i in range(2)]
        dn_raw = [sb(f"dn_raw{i}", [P, FT, s.D]) for i in range(2)]
        dn_hi = [sb(f"dn_hi{i}", [P, FT, s.D], F32R) for i in range(2)]
        dn_lo = [sb(f"dn_lo{i}", [P, FT, s.D], F32R) for i in range(2)]
        xg = [sb(f"xg{i}", [P, HC, s.ROW]) for i in range(2)]
        xg_hi = [sb(f"xg_hi{i}", [P, KT, HALF], F32R) for i in range(2)]
        xg_lo = [sb(f"xg_lo{i}", [P, KT, HALF], F32R) for i in range(2)]
        mid = [sb(f"mid{i}", [P, HALF]) for i in range(3)]
        mid_hi = [sb(f"mid_hi{i}", [P, FT, HALF], F32R) for i in range(2)]
        mid_lo = [sb(f"mid_lo{i}", [P, FT, HALF], F32R) for i in range(2)]
        one_rows = sb("one_rows", [P, HALF])
        gate_col = [sb(f"gate_col{i}", [P, HC, 1]) for i in range(2)]
        ob = [sb(f"ob{i}", [P, HC, s.D]) for i in range(2)]
        ps_t, ps_u, ps_d = t.ps[0:2], t.ps[2:5], t.ps[5:8]

        up_loaded, dn_loaded = [sem(f"f_up_loaded{i}") for i in range(2)], [sem(f"f_dn_loaded{i}") for i in range(2)]
        up_hi_ready, up_lo_ready, dn_hi_ready, dn_lo_ready = (sem(f"f_{n}") for n in ("uph", "upl", "dnh", "dnl"))
        gathered = [sem(f"f_gathered{i}") for i in range(2)]
        turned, xg_hi_ready, xg_lo_ready = sem("f_turned"), sem("f_xgh"), sem("f_xgl")
        up_mm, mid_ready, mid_hi_ready, mid_lo_ready, dn_mm, out_ready = (
            sem(f"f_{n}") for n in ("up_mm", "mid", "midh", "midl", "dn_mm", "out"))
        ones_ready, gate_copied = sem("f_ones"), sem("f_gate")
        added = [sem(f"f_added{i}") for i in range(2)]
        block = ctx.enter_context(nc.Block())
        passes = [(u, u // NH, u % NH) for u in range(E * NH)]

        def rows_of(f):
            return P if f < FT - 1 else FR + 1

        @block.sync
        def _(sp):
            def load_up(g):
                if g:
                    sp.wait_ge(up_lo_ready, g)
                sp.dma_start(up_raw[:, :, :], wup_d[g].rearrange("(k p) f -> p k f", p=P)).then_inc(
                    up_loaded[g % 2], 16)
                if g >= 2:
                    sp.wait_ge(mid_ready, NH * FT * GS * (g - 1))
                sp.dma_start(b_up[g % 2][:, :], bup_d[g]).then_inc(up_loaded[g % 2], 16)

            for e in range(E):
                if e % GS == 0:
                    load_up(e // GS)
                if e >= 2:
                    sp.wait_ge(dn_lo_ready, 2 * (e - 1))
                sp.dma_start(dn_raw[e % 2][:, 0:FT - 1, :],
                             wdn_d[e, 0:(FT - 1) * P, :].rearrange("(f p) d -> p f d", p=P)).then_inc(
                    dn_loaded[e % 2], 16)
                sp.dma_start(dn_raw[e % 2][0:FR + 1, FT - 1, :], wdn_d[e, (FT - 1) * P:F + 1, :]).then_inc(
                    dn_loaded[e % 2], 16)

        @block.gpsimd
        def _(pool):
            def gather(u, e, h):
                q = u % 2
                if u >= 2:
                    pool.wait_ge(turned, KT * (u - 1))
                    pool.wait_ge(gate_copied, u - 1)
                for c in range(HC):
                    pool.indirect_dma_start(
                        out=xg[q][:, c, :], out_offset=None, in_=t.rows_dram,
                        in_offset=bass.IndirectOffsetOnAxis(ap=t.idx[:, e, h * HC + c:h * HC + c + 1], axis=0),
                    ).then_inc(gathered[q], 16)

            def scatter(u, e, h):
                q = u % 2
                if h == 0 and e:
                    for k in range(2):
                        pool.wait_ge(added[k], 16 * HC * ((u + 1 - k) // 2))
                for c in range(HC):
                    pool.wait_ge(out_ready, HC * u + c + 1)
                    pool.indirect_dma_start(
                        out=t.ffn_dram, out_offset=bass.IndirectOffsetOnAxis(
                            ap=t.idx[:, e, h * HC + c:h * HC + c + 1], axis=0),
                        in_=ob[q][:, c, :], in_offset=None, compute_op=ALU.add).then_inc(added[q], 16)

            gather(*passes[0])
            for u in range(len(passes)):
                if u + 1 < len(passes):
                    gather(*passes[u + 1])
                if u:
                    scatter(*passes[u - 1])
            scatter(*passes[-1])
            for k in range(2):
                pool.wait_ge(added[k], 16 * HC * ((len(passes) + 1 - k) // 2))

        @block.scalar
        def _(act):
            def split_up(g):
                act.wait_ge(up_loaded[g % 2], 32 * (g // 2 + 1))
                if g >= 2:
                    act.wait_ge(up_mm, NH * FT * GS * (g - 1))
                nc.scalar.activation(up_hi[g % 2][:, :, :], up_raw[:, :, :], ACT.Copy).then_inc(up_hi_ready, 1)

            def split_down(e):
                act.wait_ge(dn_loaded[e % 2], 32 * (e // 2 + 1))
                if e >= 2:
                    act.wait_ge(dn_mm, HC * NH * (e - 1))
                nc.scalar.activation(dn_hi[e % 2][:, 0:FT - 1, :], dn_raw[e % 2][:, 0:FT - 1, :],
                                     ACT.Copy).then_inc(dn_hi_ready, 1)
                nc.scalar.activation(dn_hi[e % 2][0:FR + 1, FT - 1, :], dn_raw[e % 2][0:FR + 1, FT - 1, :],
                                     ACT.Copy).then_inc(dn_hi_ready, 1)

            split_up(0)
            split_down(0)
            for u, e, h in passes:
                q = u % 2
                for k in range(KT):
                    act.wait_ge(turned, KT * u + k + 1)
                    if u >= 2:
                        act.wait_ge(up_mm, FT * (u - 1))
                    nc.scalar.activation(xg_hi[q][:, k, :], t.ps[k][:, 0:HALF], ACT.Copy).then_inc(xg_hi_ready, 1)
                for f in range(FT):
                    n = u * FT + f
                    R = P if f < FT - 1 else FR
                    act.wait_ge(up_mm, n + 1)
                    if n >= 3:
                        act.wait_ge(mid_lo_ready, n - 2)
                    nc.scalar.activation(mid[n % 3][0:R, :], ps_u[n % 3][0:R, 0:HALF], ACT.Silu,
                                         bias=b_up[(e // GS) % 2][0:R, f:f + 1]).then_inc(mid_ready, 1)
                if h == NH - 1 and e + 1 < E:
                    if (e + 1) % GS == 0:
                        split_up((e + 1) // GS)
                    split_down(e + 1)

        @block.vector
        def _(dve):
            v = nc.vector
            v.memset(one_rows[:, :], 1.0).then_inc(ones_ready, 1)
            dve.wait_ge(ones_ready, 1)
            for q in range(2):
                v.tensor_copy(mid_hi[q][:, FT - 1, :], one_rows[:, :]).then_inc(ones_ready, 1)
                v.tensor_scalar(mid_lo[q][:, FT - 1, :], one_rows[:, :], 0.0, None, ALU.mult).then_inc(ones_ready, 1)
            dve.wait_ge(ones_ready, 5)

            def split_up(g):
                dve.wait_ge(up_hi_ready, g + 1)
                v.tensor_tensor(up_lo[g % 2][:, :, :], up_raw[:, :, :], up_hi[g % 2][:, :, :].bitcast(F32),
                                ALU.subtract).then_inc(up_lo_ready, 1)

            def split_down(e):
                q = e % 2
                dve.wait_ge(dn_hi_ready, 2 * e + 2)
                for rows, f in ((P, slice(0, FT - 1)), (FR + 1, slice(FT - 1, FT))):
                    v.tensor_tensor(dn_lo[q][0:rows, f, :], dn_raw[q][0:rows, f, :],
                                    dn_hi[q][0:rows, f, :].bitcast(F32), ALU.subtract).then_inc(dn_lo_ready, 1)

            def weigh(u):
                q = u % 2
                if u >= 2:
                    dve.wait_ge(added[q], 16 * HC * (u // 2))
                for c in range(HC):
                    n = u * HC + c
                    dve.wait_ge(dn_mm, n + 1)
                    v.tensor_scalar(ob[q][:, c, :], ps_d[n % 3][:, 0:s.D], gate_col[q][:, c, :], None,
                                    ALU.mult).then_inc(out_ready, 1)

            split_up(0)
            split_down(0)
            for u, e, h in passes:
                q = u % 2
                for k in range(KT):
                    dve.wait_ge(xg_hi_ready, KT * u + k + 1)
                    v.tensor_tensor(xg_lo[q][:, k, :], t.ps[k][:, 0:HALF], xg_hi[q][:, k, :].bitcast(F32),
                                    ALU.subtract).then_inc(xg_lo_ready, 1)
                if u >= 2:
                    dve.wait_ge(out_ready, HC * (u - 1))
                v.tensor_copy(gate_col[q][:, :, :], xg[q][:, :, s.D + e:s.D + e + 1]).then_inc(gate_copied, 1)
                for f in range(FT):
                    n = u * FT + f
                    R = P if f < FT - 1 else FR
                    dve.wait_ge(mid_ready, n + 1)
                    if u >= 2 and f == 0:
                        dve.wait_ge(dn_mm, HC * (u - 1))
                    v.tensor_copy(mid_hi[q][0:R, f, :], mid[n % 3][0:R, :]).then_inc(mid_hi_ready, 1)
                    dve.wait_ge(mid_hi_ready, n + 1)
                    v.tensor_tensor(mid_lo[q][0:R, f, :], mid[n % 3][0:R, :], mid_hi[q][0:R, f, :].bitcast(F32),
                                    ALU.subtract).then_inc(mid_lo_ready, 1)
                if u:
                    weigh(u - 1)
                if h == NH - 1 and e + 1 < E:
                    if (e + 1) % GS == 0:
                        split_up((e + 1) // GS)
                    split_down(e + 1)
            weigh(len(passes) - 1)

        @block.tensor
        def _(pe):
            def turn(u):
                q = u % 2
                pe.wait_ge(gathered[q], 16 * HC * (u // 2 + 1))
                for k in range(KT):
                    if u:
                        pe.wait_ge(xg_lo_ready, KT * (u - 1) + k + 1)
                    for c in range(HC):
                        mm = pe.transpose(t.ps[k][:, c * P:(c + 1) * P], xg[q][:, c, k * P:(k + 1) * P], t.ident)
                    mm.then_inc(turned, 1)

            def up(u, e):
                q, w = u % 2, (e // GS) % 2
                pe.wait_ge(xg_lo_ready, KT * (u + 1))
                pe.wait_ge(up_lo_ready, e // GS + 1)
                for f in range(FT):
                    n = u * FT + f
                    R = P if f < FT - 1 else FR
                    if n >= 3:
                        pe.wait_ge(mid_ready, n - 2)
                    i = 0
                    for k in range(KT):
                        for wgt, x in ((up_hi[w], xg_hi[q]), (up_lo[w], xg_hi[q]), (up_hi[w], xg_lo[q])):
                            mm = pe.matmul(ps_u[n % 3][0:R, 0:HALF], wgt[:, k, f * P:f * P + R], x[:, k, :],
                                           start=(i == 0), stop=(i == 3 * KT - 1))
                            i += 1
                    mm.then_inc(up_mm, 1)

            def down(u, e):
                q, w = u % 2, e % 2
                pe.wait_ge(mid_lo_ready, FT * (u + 1))
                pe.wait_ge(dn_lo_ready, 2 * e + 2)
                for c in range(HC):
                    n = u * HC + c
                    if n >= 3:
                        pe.wait_ge(out_ready, n - 2)
                    i = 0
                    for f in range(FT):
                        R = rows_of(f)
                        for x, wgt in ((mid_hi[q], dn_hi[w]), (mid_lo[q], dn_hi[w]), (mid_hi[q], dn_lo[w])):
                            mm = pe.matmul(ps_d[n % 3][:, 0:s.D], x[0:R, f, c * P:(c + 1) * P], wgt[0:R, f, :],
                                           start=(i == 0), stop=(i == 3 * FT - 1))
                            i += 1
                    mm.then_inc(dn_mm, 1)

            turn(0)
            for u, e, h in passes:
                up(u, e)
                if u + 1 < len(passes):
                    turn(u + 1)
                if u:
                    down(u - 1, passes[u - 1][1])
            down(*passes[-1][0:2])


def phase_output(nc, s, t, x_blk, out_blk, wout_d):
    MT, B, BPB, NB = s.MT, s.B, s.BPB, s.NB
    CPRE = PRE * CH
    with ExitStack() as ctx:
        def sem(name):
            return ctx.enter_context(nc.semaphore(name))

        def sb(name, shape, dt=F32):
            return ctx.enter_context(nc.sbuf_tensor(name, shape, dt))

        w_raw = sb("wo_raw", [P, MT, s.D])
        w_hi, w_lo = (sb(n, [P, MT, s.D], F32R) for n in ("wo_hi", "wo_lo"))
        n0, n1, n2, n3, n4, mean_c, var_c, shift, scale = (sb(f"n{i}", [P, B, MT]) for i in range(9))
        g0, g1, g2, g3 = (sb(f"g{i}", [P, B, MT, BPB]) for i in range(4))
        moments = sb("moments", [P, 2, B, MT])
        yc = [sb(f"yc{i}", [P, MT, BLK]) for i in range(2)]
        zc = [sb(f"zc{i}", [P, MT, BLK]) for i in range(2)]
        xc = [sb(f"xc{i}", [P, CH, s.D]) for i in range(2)]
        fc = [sb(f"fc{i}", [P, CH, s.D]) for i in range(2)]
        gh = [sb(f"gh{i}", [P, MT, BLK], F32R) for i in range(2)]
        gl = [sb(f"gl{i}", [P, MT, BLK], F32R) for i in range(2)]
        oc = [sb(f"oc{i}", [P, CH, s.D]) for i in range(2)]
        ps_m, ps_o = t.ps[0], t.ps[1:5]

        w_loaded, w_hi_ready, w_lo_ready = sem("c_w"), sem("c_wh"), sem("c_wl")
        vec, dev_ready, mom_ready = sem("c_vec"), sem("c_dev"), sem("c_mom")
        loaded = [sem(f"c_loaded{i}") for i in range(2)]
        gate_ready = sem("c_gate")
        normed, gated, hi_ready, lo_ready, mm_done, mul_done, sum_done = (
            sem(f"c_{n}") for n in ("normed", "gated", "hi", "lo", "mm", "mul", "sum"))
        out_stored = [sem(f"c_out{i}") for i in range(2)]
        steps = {}
        block = ctx.enter_context(nc.Block())

        @block.vector
        def _(dve):
            v = nc.vector
            n = [0]

            def do(ins, name=None):
                n[0] += 1
                ins.then_inc(vec, 1)
                dve.wait_ge(vec, n[0])
                if name:
                    steps[name] = n[0]

            half = [t.ystat[:, :, :, k].rearrange("p (a b) m -> p a m b", a=B) for k in (1, 2, 4, 5)]
            do(v.tensor_tensor(g0[:, :, :, :], half[0], half[2], ALU.add))
            do(v.tensor_reduce(n0[:, :, :].unsqueeze(3), g0[:, :, :, :], AX.X, ALU.add))
            do(v.tensor_scalar(mean_c[:, :, :], n0[:, :, :], 0.5 / BPB, None, ALU.mult))
            mb = mean_c[:, :, :].unsqueeze(3).to_broadcast([P, B, MT, BPB])
            do(v.tensor_tensor(g0[:, :, :, :], half[0], mb, ALU.subtract))
            do(v.tensor_tensor(g1[:, :, :, :], half[2], mb, ALU.subtract))
            do(v.tensor_tensor(g2[:, :, :, :], g0[:, :, :, :], g0[:, :, :, :], ALU.mult))
            do(v.tensor_tensor(g3[:, :, :, :], g1[:, :, :, :], g1[:, :, :, :], ALU.mult))
            do(v.tensor_tensor(g0[:, :, :, :], g2[:, :, :, :], g3[:, :, :, :], ALU.add))
            do(v.tensor_tensor(g1[:, :, :, :], half[1], half[3], ALU.add))
            do(v.scalar_tensor_tensor(g2[:, :, :, :].rearrange("p a m b -> p (a m b)"),
                                      g0[:, :, :, :].rearrange("p a m b -> p (a m b)"), float(BLK // 2),
                                      g1[:, :, :, :].rearrange("p a m b -> p (a m b)"), ALU.mult, ALU.add))
            do(v.tensor_reduce(n1[:, :, :].unsqueeze(3), g2[:, :, :, :], AX.X, ALU.add))
            do(v.tensor_scalar(var_c[:, :, :], n1[:, :, :], 1.0 / s.L, None, ALU.mult))
            do(v.tensor_copy(moments[:, 0, :, :], mean_c[:, :, :]))
            do(v.tensor_tensor(n0[:, :, :], mean_c[:, :, :], mean_c[:, :, :], ALU.mult))
            do(v.tensor_tensor(moments[:, 1, :, :], n0[:, :, :], var_c[:, :, :], ALU.add), "moments")
            dve.wait_ge(mom_ready, 1)
            do(v.tensor_copy(moments[:, :, :, :], ps_m[:, 0:2 * B * MT].rearrange("p (k a m) -> p k a m", k=2, a=B)))
            do(v.tensor_tensor(n0[:, :, :], moments[:, 0, :, :], moments[:, 0, :, :], ALU.mult))
            do(v.tensor_tensor(n1[:, :, :], moments[:, 1, :, :], n0[:, :, :], ALU.subtract))
            do(v.tensor_scalar(n2[:, :, :], n1[:, :, :], EPS, None, ALU.add), "var")
            dve.wait_ge(dev_ready, 1)
            do(v.reciprocal(n0[:, :, :], n3[:, :, :]))
            do(v.tensor_tensor(n1[:, :, :], n0[:, :, :], n0[:, :, :], ALU.mult))
            do(v.scalar_tensor_tensor(n4[:, :, :], n1[:, :, :], -0.5, n2[:, :, :], ALU.mult, ALU.mult))
            do(v.scalar_tensor_tensor(n1[:, :, :], n4[:, :, :], 1.5, n0[:, :, :], ALU.add, ALU.mult))
            wide = [w[:, :].unsqueeze(1).to_broadcast([P, B, MT]) for w in (t.gnw, t.gnb)]
            do(v.tensor_tensor(scale[:, :, :], n1[:, :, :], wide[0], ALU.mult))
            do(v.tensor_tensor(n0[:, :, :], moments[:, 0, :, :], scale[:, :, :], ALU.mult))
            do(v.tensor_tensor(shift[:, :, :], wide[1], n0[:, :, :], ALU.subtract), "affine")
            dve.wait_ge(w_hi_ready, 1)
            v.tensor_tensor(w_lo[:, :, :], w_raw[:, :, :], w_hi[:, :, :].bitcast(F32), ALU.subtract).then_inc(
                w_lo_ready, 1)
            for c, k in ((gated, MT * PRE), (lo_ready, MT * PRE), (mul_done, CPRE)):
                dve.sem_inc(c, k)
            with dve.Fori(0, NB // 2) as j:
                for p in range(2):
                    b = 2 * j + p
                    for m in range(MT):
                        dve.wait_ge(normed, MT * b + (MT * PRE + m + 1))
                        v.tensor_tensor(yc[p][:, m, :], yc[p][:, m, :], zc[p][:, m, :], ALU.mult).then_inc(gated, 1)
                    for m in range(MT):
                        dve.wait_ge(hi_ready, MT * b + (MT * PRE + m + 1))
                        v.tensor_tensor(gl[p][:, m, :], yc[p][:, m, :], gh[p][:, m, :].bitcast(F32),
                                        ALU.subtract).then_inc(lo_ready, 1)
                    dve.wait_ge(gate_ready, b + (PRE + 1))
                    dve.wait_ge(out_stored[p], 16 * j + 16)
                    for c in range(CH):
                        dve.wait_ge(mm_done, CH * b + (CPRE + c + 1))
                        v.tensor_tensor(oc[p][:, c, :], ps_o[c][:, 0:s.D], fc[p][:, c, :], ALU.mult).then_inc(
                            mul_done, 1)

        @block.scalar
        def _(act):
            act.wait_ge(w_loaded, 16)
            nc.scalar.activation(w_hi[:, :, :], w_raw[:, :, :], ACT.Copy).then_inc(w_hi_ready, 1)
            act.wait_ge(vec, steps["var"])
            nc.scalar.activation(n3[:, :, :], n2[:, :, :], ACT.Sqrt).then_inc(dev_ready, 1)
            for c, k in ((normed, MT * PRE), (hi_ready, MT * PRE), (gate_ready, PRE)):
                act.sem_inc(c, k)
            act.wait_ge(vec, steps["affine"])
            for bt in range(B):
                with act.Fori(bt * BPB // 2, (bt + 1) * BPB // 2) as j:
                    for p in range(2):
                        b = 2 * j + p
                        act.wait_ge(loaded[p], 64 * j + 64)
                        nc.scalar.activation(fc[p][:, :, :], fc[p][:, :, :], ACT.Silu).then_inc(gate_ready, 1)
                        for m in range(MT):
                            nc.scalar.activation(yc[p][:, m, :], yc[p][:, m, :], ACT.Identity,
                                                 bias=shift[:, bt, m:m + 1],
                                                 scale=scale[:, bt, m:m + 1]).then_inc(normed, 1)
                        act.wait_ge(mm_done, CH * b + (CPRE - CH))
                        for m in range(MT):
                            act.wait_ge(gated, MT * b + (MT * PRE + m + 1))
                            nc.scalar.activation(gh[p][:, m, :], yc[p][:, m, :], ACT.Copy).then_inc(hi_ready, 1)

        @block.gpsimd
        def _(pool):
            pool.sem_inc(sum_done, PRE)
            for p in range(2):
                pool.sem_inc(out_stored[p], 16)
            with pool.Fori(0, NB // 2) as j:
                for p in range(2):
                    b = 2 * j + p
                    pool.wait_ge(mul_done, CH * b + (CPRE + CH))
                    nc.gpsimd.tensor_tensor(oc[p][:, :, :], oc[p][:, :, :], xc[p][:, :, :], ALU.add).then_inc(
                        sum_done, 1)

        @block.tensor
        def _(pe):
            pe.wait_ge(vec, steps["moments"])
            pe.matmul(ps_m[:, 0:2 * B * MT], t.headavg, moments[:, :, :, :].rearrange("p k a m -> p (k a m)"),
                      start=True, stop=True).then_inc(mom_ready, 1)
            pe.wait_ge(w_lo_ready, 1)
            pe.sem_inc(mm_done, CPRE)
            with pe.Fori(0, NB // 2) as j:
                for p in range(2):
                    b = 2 * j + p
                    pe.wait_ge(lo_ready, MT * b + MT * (PRE + 1))
                    for c in range(CH):
                        pe.wait_ge(mul_done, CH * b + (CPRE - CH + c + 1))
                        n = 0
                        for k in range(MT):
                            for g, w in ((gh[p], w_hi), (gl[p], w_hi), (gh[p], w_lo)):
                                mm = pe.matmul(ps_o[c][:, 0:s.D], g[:, k, c * P:(c + 1) * P], w[:, k, :],
                                               start=(n == 0), stop=(n == 3 * MT - 1))
                                n += 1
                        mm.then_inc(mm_done, 1)

        @block.sync
        def _(sp):
            sp.dma_start(w_raw[:, :, :], wout_d.rearrange("(k p) n -> p k n", p=P)).then_inc(w_loaded, 16)

            def load(b, p):
                for dst, src in ((yc, t.y_dram[b]), (zc, t.zs_dram[b]), (xc, x_blk[b]), (fc, t.ffn_blk[b])):
                    sp.dma_start(dst[p][:, :, :], src).then_inc(loaded[p], 16)

            def store(b, p):
                sp.wait_ge(sum_done, b + (PRE + 1))
                sp.dma_start(out_blk[b], oc[p][:, :, :]).then_inc(out_stored[p], 16)

            for p in range(2):
                load(p, p)
            with sp.Fori(0, NB // 2 - 1) as j:
                for p in range(2):
                    store(2 * j + p, p)
                    sp.wait_ge(lo_ready, MT * (2 * j + p) + MT * (PRE + 1))
                    load(2 * j + (p + 2), p)
            for p in range(2):
                store(NB - 2 + p, p)
            for p in range(2):
                sp.wait_ge(out_stored[p], 16 * (NB // 2 + 1))


def build(nc, ins, outs):
    x_d = ins["x"]
    s = Shapes(x_d, ins["wx"], ins["wdt"], ins["wr"], ins["wup"])
    x_blk = x_d.rearrange("b (i c p) d -> (b i) p c d", c=CH, p=P)
    t = Tiles()

    def dram(name, shape):
        if name in outs:
            return outs[name]
        return nc.dram_tensor(name, shape, F32, kind="Internal").ap()

    t.rows_dram = dram("rows_dram", [s.T, s.ROW])
    t.x2_dram = dram("x2_dram", [s.NB, P, s.MT, BLK])
    t.zs_dram = dram("zs_dram", [s.NB, P, s.MT, BLK])
    t.y_dram = dram("y_dram", [s.NB, P, s.MT, BLK])
    t.ffn_dram = dram("ffn_dram", [s.T, s.D])
    t.cum_dram = dram("cum_dram", [s.NT, s.H, P])
    t.ecum_dram = dram("ecum_dram", [s.NT, s.H, P])
    t.ffn_blk = t.ffn_dram.rearrange("(i c p) d -> i p c d", c=CH, p=P)
    t.xn_blk = t.rows_dram[:, 0:s.D].rearrange("(i c p) d -> i p c d", c=CH, p=P)
    with ExitStack() as ctx:
        def sb(name, shape, dt=F32):
            return ctx.enter_context(nc.sbuf_tensor(name, shape, dt))

        t.ps = [ctx.enter_context(nc.psum_tensor(f"ps{i}", [P, 512], F32)) for i in range(8)]
        t.cst = sb("cst", [P, C_END])
        t.ident = t.cst[:, C_ID:C_ID + P]
        t.tri = t.cst[:, C_TRI:C_TRI + P]
        t.ones = t.cst[:, C_ONES:C_ONES + P]
        t.rsum = t.cst[:, C_RSUM:C_RSUM + P]
        t.rtri = t.cst[:, C_RTRI:C_RTRI + P]
        t.iota = t.cst[:, C_IOTA:C_IOTA + P]
        t.headavg = t.cst[:, C_HEAD:C_HEAD + P]
        t.rows = sb("rows", [P, 3, 8])
        t.dcol, t.gnw, t.gnb, t.cb = (sb(n, [P, s.MT]) for n in ("dcol", "gnw", "gnb", "cb"))
        t.cw = sb("cw", [P, s.MT, 4])
        t.norm = sb("norm", [P, 2, s.NT])
        t.dt = sb("dt", [P, s.NT, s.H])
        t.cum = sb("cum", [P, s.NT, s.H])
        t.wst = sb("wst", [P, s.NT, s.H])
        t.dec = sb("dec", [P, s.NT, s.MT])
        t.gates = sb("gates", [P, s.NT, s.E])
        t.idx = sb("idx", [P, s.E, s.LW], U32)
        t.ystat = sb("ystat", [P, s.NB, s.MT, 6])
        with ExitStack() as mid:
            t.wbc_hi = [mid.enter_context(nc.sbuf_tensor(f"w_hi_{n}", [P, s.MT, s.INNER], F32R)) for n in "bc"]
            t.wbc_lo = [mid.enter_context(nc.sbuf_tensor(f"w_lo_{n}", [P, s.MT, s.INNER], F32R)) for n in "bc"]
            t.gateT = mid.enter_context(nc.sbuf_tensor("gateT", [P, s.SEG], F32))
            with ExitStack() as early:
                def sbe(name, shape, dt=F32):
                    return early.enter_context(nc.sbuf_tensor(name, shape, dt))

                t.wx, t.wz = (sbe(n, [P, s.KT, s.INNER]) for n in ("wx", "wz"))
                t.wr = sbe("wr", [P, s.KT, s.E])
                t.wdt = sbe("wdt", [P, s.MT, s.H])
                t.logit2 = sbe("logit2", [P, s.NT, 2, s.E])
                consts = [(t.cst[:, :], ins["const"]), (t.rows[:, :, :], ins["rows"]), (t.dcol[:, :], ins["dcol"]),
                          (t.gnw[:, :], ins["gnw"]), (t.gnb[:, :], ins["gnb"]), (t.cb[:, :], ins["cb"]),
                          (t.cw[:, :, :], ins["cw"]),
                          (t.wx[:, :, :], ins["wx"].rearrange("(k p) n -> p k n", p=P)),
                          (t.wz[:, :, :], ins["wz"].rearrange("(k p) n -> p k n", p=P)),
                          (t.wr[:, :, :], ins["wr"].rearrange("(k p) n -> p k n", p=P)),
                          (t.wdt[:, :, :], ins["wdt"].rearrange("(k p) n -> p k n", p=P))]
                phase_stats(nc, s, t, x_blk, consts)
                phase_project(nc, s, t, x_blk)
                phase_decays(nc, s, t, ins["wb"], ins["wc"])
            phase_scan(nc, s, t)
        phase_experts(nc, s, t, ins["wup"], ins["bup"], ins["wdn"])
        if "out" in outs:
            phase_output(nc, s, t, x_blk, outs["out"].rearrange("b (i c p) d -> (b i) p c d", c=CH, p=P), ins["wout"])


def shape_constants(T, E):
    import numpy as np

    i = np.arange(P)
    c = np.zeros((P, C_END), np.float32)
    c[:, C_ID:C_ID + P] = np.eye(P)
    c[:, C_TRI:C_TRI + P] = i[:, None] <= i[None, :]
    c[:, C_ONES:C_ONES + P] = 1
    same = i[:, None] % E == i[None, :] % E
    c[:, C_RSUM:C_RSUM + P] = same
    c[:, C_RTRI:C_RTRI + P] = same & (i[:, None] < i[None, :])
    c[:, C_IOTA:C_IOTA + P] = i[None, :]
    c[:, C_HEAD:C_HEAD + P] = (i[:, None] // 64 == i[None, :] // 64) / 64.0
    c[:, C_TAU:C_TAU + 64] = np.arange(64)[None, :]
    c[:, C_PIDX] = i
    c[:, C_LO:C_LO + 8] = np.arange(8)[None, :]
    c[:, C_BIT:C_BIT + BITS] = 2.0 ** np.arange(BITS - 1, -1, -1)[None, :]
    return c


def lay_out(v):
    import numpy as np

    a = {k.split("_", 2)[2]: np.asarray(x) for k, x in v.items()}
    con = np.ascontiguousarray

    def column(row, width=P):
        return con(row.reshape(-1, width).T)

    d = a["d_param"]
    F = a["W_down"].shape[1]
    FT = -(-F // P)
    bup = np.zeros((a["b_up"].shape[0], FT * P), a["b_up"].dtype)
    bup[:, :F] = a["b_up"]
    x = a["input_tensor"]
    return {
        "x": con(x),
        "wx": con(a["Wx"].T), "wz": con(a["Wz"].T), "wb": con(a["Wb"].T), "wc": con(a["Wc"].T),
        "wdt": con(a["Wdt"].T), "wout": con(a["Wout"].T), "wr": con(a["Wr"]),
        "cw": con(a["conv_w"][:, 0, :].reshape(-1, P, 4).transpose(1, 0, 2)), "cb": column(a["conv_b"]),
        "rows": con(np.broadcast_to(np.stack([a["log_a"], a["b_dt"], a["br"]])[None], (P, 3, 8))),
        "dcol": column(np.repeat(d, a["gn_w"].shape[0] // d.shape[0])),
        "gnw": column(a["gn_w"]), "gnb": column(a["gn_b"]),
        "wup": con(a["W_up"]), "bup": con(bup.reshape(-1, FT, P).transpose(0, 2, 1)),
        "wdn": con(np.concatenate([a["W_down"], a["b_down"][:, None, :]], axis=1)),
        "const": shape_constants(x.shape[0] * x.shape[1], a["Wr"].shape[1]),
    }


def kernel(**inputs):
    import numpy as _np
    import concourse.bacc as _bacc
    from concourse import mybir as _mybir
    from concourse.bass_utils import run_bass_kernel_spmd as _run

    nc = _bacc.Bacc("TRN2", target_bir_lowering=False, num_devices=1)
    arrays = {f"in_{k}": v for k, v in lay_out(inputs).items()}
    ins = {k[3:]: nc.dram_tensor(k, v.shape, _mybir.dt.from_np(v.dtype), kind="ExternalInput").ap()
           for k, v in arrays.items()}
    shape = arrays["in_x"].shape
    out = nc.dram_tensor("out_dram", shape, _mybir.dt.float32, kind="ExternalOutput").ap()
    build(nc, ins, {"out": out})
    r = _run(nc, [arrays], core_ids=[0])
    return r.results[0]["out_dram"]
```

```python
from contextlib import ExitStack

import concourse.bass as bass
from concourse import mybir

F32 = mybir.dt.float32
F32R = mybir.dt.float32r
BF16 = mybir.dt.bfloat16
I32 = mybir.dt.int32
U32 = mybir.dt.uint32
ALU = mybir.AluOpType
ACT = mybir.ActivationFunctionType
AX = mybir.AxisListType

P = 128
BLK = 512
CH = BLK // P
EPS = 1e-5

PRE = 2

C_ID, C_TRI, C_ONES, C_RSUM, C_RTRI, C_IOTA, C_HEAD, C_TAU, C_PIDX, C_LO, C_BIT = (
    0, 128, 256, 384, 512, 640, 768, 896, 960, 961, 969)
BITS = 30
C_END = 1002


class Shapes:

    def __init__(self, x, wx, wdt, wr, wup):
        self.B, self.L, self.D = x.shape
        self.INNER = wx.shape[1]
        self.KT = self.D // P
        self.MT = self.INNER // P
        self.H = wdt.shape[1]
        self.HD = self.INNER // self.H
        self.E = wr.shape[1]
        self.G, _, self.F = wup.shape
        self.GS = self.E // self.G
        self.FT = -(-self.F // P)
        self.FR = self.F - (self.FT - 1) * P
        self.T = self.B * self.L
        self.NB = self.T // BLK
        self.NT = self.T // P
        self.BPB = self.L // BLK
        self.CAP = self.T // self.E
        self.LW = self.CAP // P
        self.HALF = min(BLK, self.CAP)
        self.NH = self.CAP // self.HALF
        self.HC = self.HALF // P
        self.NSEG = P // self.E
        self.GT = self.NT // self.NSEG
        self.SEG = self.GT * P
        self.ROW = self.D + self.E
        assert self.KT == 2 and self.MT == 4 and self.H == 2 * self.MT and self.HD == 64
        assert self.BPB * CH == self.NT // 2 and self.B == 2 and BITS <= self.BPB * CH <= 32
        assert self.LW & (self.LW - 1) == 0 and self.BPB % 2 == 0 and self.E == 8 and self.GS == 2


class Tiles:
    pass


def phase_stats(nc, s, t, x_blk, consts):
    with ExitStack() as ctx:
        def sem(name):
            return ctx.enter_context(nc.semaphore(name))

        xin = [ctx.enter_context(nc.sbuf_tensor(f"stat_x{i}", [P, CH, s.D], F32)) for i in range(4)]
        stat6 = ctx.enter_context(nc.sbuf_tensor("stat6", [P, s.NT, 6], F32))
        mean, dmean, var, dev, inv, tmp = (
            ctx.enter_context(nc.sbuf_tensor(f"stat_t{i}", [P, s.NT], F32)) for i in range(6))
        const_loaded = sem("const_loaded")
        x_loaded = [sem(f"stat_x_loaded{i}") for i in range(4)]
        stat_done = sem("stat_done")
        step = sem("stat_step")
        dev_done = sem("dev_done")
        w_hi, w_lo = sem("stat_w_hi"), sem("stat_w_lo")
        block = ctx.enter_context(nc.Block())

        @block.sync
        def _(sp):
            for i in range(4):
                sp.dma_start(xin[i][:, :, :], x_blk[i]).then_inc(x_loaded[i], 16)
            if s.NB > 4:
                with sp.Fori(1, s.NB // 4) as j:
                    for i in range(4):
                        sp.wait_ge(stat_done, 4 * j + (i - 3))
                        sp.dma_start(xin[i][:, :, :], x_blk[4 * j + i]).then_inc(x_loaded[i], 16)

        @block.gpsimd
        def _(pool):
            for dst, src in consts:
                pool.dma_start(dst, src).then_inc(const_loaded, 16)
            pool.wait_ge(const_loaded, 16 * len(consts))

        @block.vector
        def _(dve):
            with dve.Fori(0, s.NB // 4) as j:
                for i in range(4):
                    dve.wait_ge(x_loaded[i], 16 * j + 16)
                    for c in range(CH):
                        n = nc.vector.bn_stats(stat6[:, 4 * CH * j + (CH * i + c), :], xin[i][:, c, :])
                    n.then_inc(stat_done, 1)
            for n, (lo, raw, hi) in enumerate(((t.wx_lo[:, :, :], t.wx[:, :, :], t.wx_hi[:, :, :]),
                                               (t.wr2[:, :, 1, :], t.wr[:, :, :], t.wr2[:, :, 0, :]))):
                dve.wait_ge(w_hi, n + 1)
                nc.vector.tensor_tensor(lo, raw, hi.bitcast(F32), ALU.subtract).then_inc(w_lo, 1)
            dve.wait_ge(stat_done, s.NB)
            half_mean = [stat6[:, :, k] for k in (1, 4)]
            half_m2 = [stat6[:, :, k] for k in (2, 5)]
            rstd = t.norm[:, 1, :]
            nc.vector.tensor_tensor(tmp[:, :], half_mean[0], half_mean[1], ALU.add).then_inc(step, 1)
            nc.vector.tensor_tensor(dmean[:, :], half_mean[0], half_mean[1], ALU.subtract).then_inc(step, 1)
            nc.vector.tensor_tensor(var[:, :], half_m2[0], half_m2[1], ALU.add).then_inc(step, 1)
            dve.wait_ge(step, 3)
            nc.vector.tensor_scalar(mean[:, :], tmp[:, :], 0.5, None, ALU.mult).then_inc(step, 1)
            nc.vector.scalar_tensor_tensor(dev[:, :], dmean[:, :], 0.25, dmean[:, :], ALU.mult,
                                           ALU.mult).then_inc(step, 1)
            dve.wait_ge(step, 5)
            nc.vector.scalar_tensor_tensor(tmp[:, :], var[:, :], 1.0 / s.D, dev[:, :], ALU.mult,
                                           ALU.add).then_inc(step, 1)
            dve.wait_ge(step, 6)
            nc.vector.tensor_scalar(var[:, :], tmp[:, :], EPS, None, ALU.add).then_inc(step, 1)
            dve.wait_ge(dev_done, 1)
            nc.vector.reciprocal(inv[:, :], dev[:, :]).then_inc(step, 1)
            dve.wait_ge(step, 8)
            nc.vector.tensor_tensor(tmp[:, :], inv[:, :], inv[:, :], ALU.mult).then_inc(step, 1)
            dve.wait_ge(step, 9)
            nc.vector.scalar_tensor_tensor(dmean[:, :], tmp[:, :], -0.5, var[:, :], ALU.mult,
                                           ALU.mult).then_inc(step, 1)
            dve.wait_ge(step, 10)
            nc.vector.scalar_tensor_tensor(rstd, dmean[:, :], 1.5, inv[:, :], ALU.add,
                                           ALU.mult).then_inc(step, 1)
            dve.wait_ge(step, 11)
            nc.vector.scalar_tensor_tensor(t.norm[:, 0, :], mean[:, :], -1.0, rstd, ALU.mult,
                                           ALU.mult).then_inc(step, 1)

        @block.scalar
        def _(act):
            act.wait_ge(const_loaded, 16 * len(consts))
            nc.scalar.activation(t.wx_hi[:, :, :], t.wx[:, :, :], ACT.Copy).then_inc(w_hi, 1)
            nc.scalar.activation(t.wr2[:, :, 0, :], t.wr[:, :, :], ACT.Copy).then_inc(w_hi, 1)
            act.wait_ge(step, 7)
            nc.scalar.activation(dev[:, :], var[:, :], ACT.Sqrt).then_inc(dev_done, 1)


def phase_project(nc, s, t, x_blk):
    KT, MT = s.KT, s.MT
    with ExitStack() as ctx:
        def sem(name):
            return ctx.enter_context(nc.semaphore(name))

        def sb(name, shape, dt=F32):
            return ctx.enter_context(nc.sbuf_tensor(name, shape, dt))

        wx_hi, wx_lo, wr2 = t.wx_hi, t.wx_lo, t.wr2
        xin = [sb(f"xin{i}", [P, CH, s.D]) for i in range(2)]
        xn = [sb(f"xn{i}", [P, CH, s.D]) for i in range(2)]
        norm_blk = [sb(f"norm_blk{i}", [P, 2, CH]) for i in range(2)]
        xn_hi = [sb(f"xn_hi{i}", [P, KT, BLK], F32R) for i in range(2)]
        xn_lo = [sb(f"xn_lo{i}", [P, KT, BLK], F32R) for i in range(2)]
        xpre = [sb(f"xpre{m}", [P, 3 + BLK]) for m in range(MT)]
        acc = [sb(f"acc{m}", [P, BLK]) for m in range(MT)]
        x2 = [sb(f"x2a{i}", [P, MT, BLK]) for i in range(2)]
        dt_row = sb("dt_row", [s.H, BLK])
        ps_t, ps_x, ps_lg, ps_dt = t.ps[0:2], t.ps[2:6], t.ps[6], t.ps[7]

        dt_zeroed = sem("a_dt_zeroed")
        x_loaded = [sem(f"a_x_loaded{i}") for i in range(2)]
        norm_copied = sem("a_norm_copied")
        xn_ready = sem("a_xn_ready")
        xn_stored = [sem(f"a_xn_stored{i}") for i in range(2)]
        xnT_ready = sem("a_xnT_ready")
        xn_hi_ready = sem("a_xn_hi_ready")
        xn_lo_ready = sem("a_xn_lo_ready")
        x_ready = sem("a_x_ready")
        xpre_ready = sem("a_xpre_ready")
        tap0_done = sem("a_tap0_done")
        taps = sem("a_taps")
        conv_done = sem("a_conv_done")
        halo_done = sem("a_halo_done")
        halo_reset = sem("a_halo_reset")
        x2_ready = sem("a_x2_ready")
        lg_ready = sem("a_lg_ready")
        dt_ready = sem("a_dt_ready")
        dt_rows = sem("a_dt_rows")
        dt_turned = sem("a_dt_turned")
        lg_copied = sem("a_lg_copied")
        dt_copied = sem("a_dt_copied")
        x2_stored = [sem(f"a_x2_stored{i}") for i in range(2)]
        pe_waited = sem("a_pe_waited")
        waited = sem("a_waited")
        block = ctx.enter_context(nc.Block())

        def run(eng, body, first=None):
            for bt in range(s.B):
                if first:
                    first(bt)
                last = bt == s.B - 1
                with eng.Fori(bt * s.BPB // 2, (bt + 1) * s.BPB // 2 - (1 if last else 0)) as j:
                    for p in range(2):
                        body(2 * j + p, p, True, True, j)
            for p in range(2):
                body(s.NB - 2 + p, p, p == 0, False, s.NB // 2 - 1)

        @block.sync
        def _(sp):
            with sp.Fori(0, s.NB // 2) as j:
                for p in range(2):
                    b = 2 * j + p
                    sp.wait_ge(xn_ready, b + (PRE - 1))
                    sp.dma_start(xin[p][:, :, :], x_blk[b]).then_inc(x_loaded[p], 16)
                    sp.wait_ge(xn_ready, b + (PRE + 1))
                    sp.dma_start(t.xn_blk[b], xn[p][:, :, :]).then_inc(xn_stored[p], 16)

        @block.gpsimd
        def _(pool):
            pool.sem_inc(xn_ready, PRE)
            pool.sem_inc(tap0_done, MT * PRE)

            def layer_norm(b, p, pair):
                nc.gpsimd.tensor_copy(norm_blk[p][:, :, :], t.norm[:, :, bass.ds(CH * b, CH)]).then_inc(
                    norm_copied, 1)
                pool.wait_ge(norm_copied, b + 1)
                pool.wait_ge(x_loaded[p], 16 * pair + 16)
                pool.wait_ge(xn_stored[p], 16 * pair + 16)
                pool.wait_ge(xnT_ready, KT * b + KT * (PRE - 1))
                pool.sem_inc(waited, 1)
                for c in range(CH):
                    n = nc.gpsimd.tensor_scalar(xn[p][:, c, :], xin[p][:, c, :], norm_blk[p][:, 1, c:c + 1],
                                                norm_blk[p][:, 0, c:c + 1], ALU.mult, ALU.add)
                n.then_inc(xn_ready, 1)

            def body(b, p, nxt, nxt2, j):
                if nxt2:
                    layer_norm(b + 2, p, j + 1)
                for m in range(MT):
                    pool.wait_ge(xpre_ready, MT * b + (MT * PRE + m + 1))
                    pool.wait_ge(x2_ready, MT * b + (MT * (PRE - 1) + m + 1))
                    pool.sem_inc(waited, 1)
                    nc.gpsimd.tensor_scalar(acc[m][:, :], xpre[m][:, 0:BLK], t.cw[:, m, 0:1], t.cb[:, m:m + 1],
                                            ALU.mult, ALU.add).then_inc(tap0_done, 1)

            for p in range(2):
                layer_norm(p, p, 0)
            run(pool, body, lambda bt: pool.wait_ge(halo_reset, MT * (bt + 1)))

        @block.scalar
        def _(act):
            for c, n in ((xn_hi_ready, KT * PRE), (xpre_ready, MT * PRE), (x2_ready, MT * PRE), (dt_rows, PRE),
                         (xn_stored[0], 16), (xn_stored[1], 16), (x2_stored[0], 16), (x2_stored[1], 16)):
                act.sem_inc(c, n)

            def x_out(b, m):
                act.wait_ge(x_ready, MT * b + (MT * PRE + m + 1))
                act.wait_ge(halo_done, MT * b + (MT * (PRE - 1) + m + 1))
                nc.scalar.activation(xpre[m][:, 3:3 + BLK], ps_x[m][:, :], ACT.Copy).then_inc(xpre_ready, 1)

            def x_silu(b, p, m):
                act.wait_ge(conv_done, MT * b + (MT * PRE + m + 1))
                nc.scalar.activation(x2[p][:, m, :], acc[m][:, :], ACT.Silu).then_inc(x2_ready, 1)

            def hi_parts(b, p):
                act.wait_ge(lg_ready, b + (PRE - 1))
                for k in range(KT):
                    act.wait_ge(xnT_ready, KT * b + (KT * PRE + k + 1))
                    nc.scalar.activation(xn_hi[p][:, k, :], ps_t[k][:, :], ACT.Copy).then_inc(xn_hi_ready, 1)

            def body(b, p, nxt, nxt2, j):
                act.wait_ge(x2_stored[p], 16 * j + 16)
                act.wait_ge(dt_ready, b + (PRE - 1))
                for m in range(MT):
                    x_silu(b, p, m)
                    if nxt:
                        x_out(b + 1, m)
                act.wait_ge(x2_ready, MT * b + MT * (PRE + 1))
                act.dma_start(t.x2_dram[b], x2[p][:, :, :]).then_inc(x2_stored[p], 16)
                if nxt2:
                    hi_parts(b + 2, p)
                act.wait_ge(dt_ready, b + (PRE + 1))
                act.wait_ge(dt_turned, b + (PRE + 1))
                nc.scalar.activation(dt_row[:, :], ps_dt[0:s.H, :], ACT.Copy).then_inc(dt_rows, 1)

            hi_parts(0, 0)
            for m in range(MT):
                x_out(0, m)
            hi_parts(1, 1)
            run(act, body)
            for p in range(2):
                for c in (xn_stored[p], x2_stored[p]):
                    act.wait_ge(c, 16 * (s.NB // 2 + 1))

        @block.vector
        def _(dve):
            for c, n in ((xn_lo_ready, KT * PRE), (conv_done, MT * PRE), (halo_done, MT * PRE),
                         (lg_copied, PRE), (dt_copied, PRE)):
                dve.sem_inc(c, n)
            nc.vector.memset(dt_row[:, :], 0.0).then_inc(dt_zeroed, 1)

            def conv(b, pair):
                for k in range(1, 4):
                    for m in pair:
                        if k == 1:
                            dve.wait_ge(tap0_done, MT * b + (MT * PRE + m + 1))
                        else:
                            dve.wait_ge(taps, 2 * MT * b + (2 * pair[0] + 2 * (k - 2) + m - pair[0] + 1))
                        n = nc.vector.scalar_tensor_tensor(acc[m][:, :], xpre[m][:, k:k + BLK], t.cw[:, m, k:k + 1],
                                                           acc[m][:, :], ALU.mult, ALU.add)
                        n.then_inc(taps if k < 3 else conv_done, 1)
                for m in pair:
                    dve.wait_ge(conv_done, MT * b + (MT * PRE + m + 1))
                    nc.vector.tensor_copy(xpre[m][:, 0:3], xpre[m][:, BLK:BLK + 3]).then_inc(halo_done, 1)

            def lo_parts(b, p):
                for k in range(KT):
                    dve.wait_ge(xn_hi_ready, KT * b + (KT * PRE + k + 1))
                    nc.vector.tensor_tensor(xn_lo[p][:, k, :], ps_t[k][:, :], xn_hi[p][:, k, :].bitcast(F32),
                                            ALU.subtract).then_inc(xn_lo_ready, 1)

            def step_sizes(b):
                dve.wait_ge(dt_turned, b + (PRE + 2))
                nc.vector.tensor_copy(t.dt_all[:, bass.ds(CH * b + CH, CH), :],
                                      ps_lg[:, P:P + CH * s.H].rearrange("p (c h) -> p c h", c=CH)).then_inc(
                    dt_copied, 1)

            def body(b, p, nxt, nxt2, j):
                conv(b, (0, 1))
                step_sizes(b - 1)
                conv(b, (2, 3))
                if nxt2:
                    lo_parts(b + 2, p)
                dve.wait_ge(lg_ready, b + (PRE + 1))
                nc.vector.tensor_copy(t.logit2[:, bass.ds(CH * b, CH), :, :],
                                      ps_lg[:, 0:CH * 2 * s.E].rearrange("p (c k e) -> p c k e", c=CH, k=2)
                                      ).then_inc(lg_copied, 1)

            def first(bt):
                if bt:
                    dve.wait_ge(halo_done, MT * (bt * s.BPB + PRE))
                for m in range(MT):
                    n = nc.vector.memset(xpre[m][:, 0:3], 0.0)
                    n.then_inc(halo_reset, 1)
                dve.wait_ge(halo_reset, MT * (bt + 1))

            for p in range(2):
                lo_parts(p, p)
            run(dve, body, first)
            step_sizes(s.NB - 1)

        @block.tensor
        def _(pe):
            for c, n in ((xnT_ready, KT * PRE), (x_ready, MT * PRE), (lg_ready, PRE),
                         (dt_ready, PRE), (dt_turned, PRE)):
                pe.sem_inc(c, n)
            pe.wait_ge(dt_zeroed, 1)

            def turn(b, p):
                pe.wait_ge(xn_ready, b + (PRE + 1))
                for k in range(KT):
                    pe.wait_ge(xn_lo_ready, KT * b + (KT * (PRE - 1) + k + 1))
                    for c in range(CH):
                        mm = pe.transpose(ps_t[k][:, c * P:(c + 1) * P], xn[p][:, c, k * P:(k + 1) * P], t.ident)
                    mm.then_inc(xnT_ready, 1)

            def project(b, p):
                for m in range(MT):
                    pe.wait_ge(xpre_ready, MT * b + (MT * (PRE - 1) + m + 1))
                    n = 0
                    for k in range(KT):
                        for wgt, act_in in ((wx_hi, xn_hi[p]), (wx_lo, xn_hi[p]), (wx_hi, xn_lo[p])):
                            if m == 0:
                                pe.wait_ge(xn_hi_ready if act_in is xn_hi[p] else xn_lo_ready,
                                           KT * b + (KT * PRE + k + 1))
                            mm = pe.matmul(ps_x[m][:, :], wgt[:, k, m * P:(m + 1) * P], act_in[:, k, :],
                                           start=(n == 0), stop=(n == 3 * KT - 1))
                            n += 1
                    mm.then_inc(x_ready, 1)

            def turn_steps(b):
                pe.wait_ge(dt_rows, b + (PRE + 1))
                pe.wait_ge(lg_copied, b + (PRE + 1))
                pe.wait_ge(dt_copied, b + (PRE + 1))
                pe.sem_inc(pe_waited, 1)
                for c in range(CH):
                    mm = pe.transpose(ps_lg[:, P + c * s.H:P + (c + 1) * s.H], dt_row[:, c * P:(c + 1) * P],
                                      t.cst[0:s.H, C_ID:C_ID + s.H])
                mm.then_inc(dt_turned, 1)

            def body(b, p, nxt, nxt2, j):
                if nxt:
                    project(b + 1, 1 - p)
                turn_steps(b - 1)
                if nxt2:
                    turn(b + 2, p)
                pe.wait_ge(lg_copied, b + PRE)
                pe.wait_ge(dt_copied, b + (PRE + 1))
                for c in range(CH):
                    for n, (k, half) in enumerate((k, half) for k in range(KT) for half in (xn_hi[p], xn_lo[p])):
                        mm = pe.matmul(ps_lg[:, c * 2 * s.E:(c + 1) * 2 * s.E], half[:, k, c * P:(c + 1) * P],
                                       wr2[:, k, :, :], start=(n == 0), stop=(n == 2 * KT - 1))
                mm.then_inc(lg_ready, 1)
                for k in range(MT):
                    pe.wait_ge(x2_ready, MT * b + (MT * PRE + k + 1))
                    pe.wait_ge(dt_rows, b + PRE)
                    mm = pe.matmul(ps_dt[0:s.H, :], t.wdt[:, k, :], x2[p][:, k, :], start=(k == 0),
                                   stop=(k == MT - 1))
                mm.then_inc(dt_ready, 1)

            turn(0, 0)
            project(0, 0)
            turn(1, 1)
            run(pe, body)
            turn_steps(s.NB - 1)


def phase_decays(nc, s, t, wb_d, wc_d):
    NT, E, H, GT, SEG = s.NT, s.E, s.H, s.GT, s.SEG
    with ExitStack() as ctx:
        def sem(name):
            return ctx.enter_context(nc.semaphore(name))

        def sb(name, shape, dt=F32):
            return ctx.enter_context(nc.sbuf_tensor(name, shape, dt))

        u, e1, w1, ln, q, z, rec, dta, gap, ecum, wexp, dec8, lsum = (
            sb(f"r_{n}", [P, NT, 8]) for n in ("u", "e1", "w1", "ln", "q", "z", "rec", "dta", "gap", "ecum",
                                               "wexp", "dec8", "lsum"))
        a_pos = sb("r_a_pos", [P, 1, 8])
        top, esum, einv = (sb(f"r_{n}", [P, NT, 1]) for n in ("top", "esum", "einv"))
        gates_g = sb("r_gates_g", [P, GT, s.NSEG, E])
        rowsT = sb("rowsT", [P, 2, GT, P])
        w_raw = [sb(f"w_raw{i}", [P, s.MT, s.INNER]) for i in range(2)]
        ps = t.ps

        vec, sca, ten = sem("r_vec"), sem("r_sca"), sem("r_ten")
        x2_loaded, x_hi, x_lo = [sem(f"r_x2_loaded{i}") for i in range(2)], sem("r_x_hi"), sem("r_x_lo")
        tile_mm, tile_out = sem("r_tile_mm"), sem("r_tile_out")
        stored = sem("r_stored")
        w_loaded, w_hi, w_lo = [sem(f"r_w_loaded{i}") for i in range(2)], sem("r_w_hi"), sem("r_w_lo")
        block = ctx.enter_context(nc.Block())

        def wide(ap, shape):
            return ap.to_broadcast(shape)

        steps = {}

        @block.vector
        def _(dve):
            n = [0]

            def do(ins, name=None):
                n[0] += 1
                ins.then_inc(vec, 1)
                dve.wait_ge(vec, n[0])
                if name:
                    assert steps.setdefault(name, n[0]) == n[0]

            full = [P, NT, 8]
            v = nc.vector
            do(v.tensor_tensor(u[:, :, :], t.dt[:, :, :], wide(t.rows[:, 1:2, :], full), ALU.add), "u")
            dve.wait_ge(sca, 3)
            do(v.tensor_scalar(w1[:, :, :], e1[:, :, :], 1.0, None, ALU.add), "w1")
            do(v.tensor_scalar(q[:, :, :], w1[:, :, :], -1.0, None, ALU.add))
            do(v.scalar_tensor_tensor(z[:, :, :], q[:, :, :], 0.0, e1[:, :, :], ALU.is_equal, ALU.mult))
            do(v.tensor_scalar(gap[:, :, :], q[:, :, :], 1e-30, None, ALU.max))
            do(v.reciprocal(rec[:, :, :], gap[:, :, :]))
            do(v.tensor_tensor(q[:, :, :], rec[:, :, :], e1[:, :, :], ALU.mult))
            dve.wait_ge(sca, 4)
            do(v.tensor_tensor(rec[:, :, :], q[:, :, :], ln[:, :, :], ALU.mult))
            do(v.tensor_tensor(q[:, :, :], rec[:, :, :], z[:, :, :], ALU.add))
            do(v.scalar_tensor_tensor(t.dt[:, :, :], u[:, :, :], 0.0, q[:, :, :], ALU.max, ALU.add))
            do(v.scalar_tensor_tensor(dta[:, :, :], t.dt[:, :, :], -1.0, wide(a_pos[:, :, :], full), ALU.mult,
                                      ALU.mult), "dta")
            dve.wait_ge(ten, 2)
            psc = [ps[i][:, 0:NT * H].rearrange("p (t h) -> p t h", h=H) for i in range(2)]
            do(v.tensor_copy(t.cum[:, :, :], psc[0]), "cum")
            do(v.tensor_tensor(gap[:, :, :], psc[1], t.cum[:, :, :], ALU.subtract), "gap")
            dve.wait_ge(sca, 7)
            do(v.tensor_tensor(t.wst[:, :, :], wexp[:, :, :], t.dt[:, :, :], ALU.mult))
            for a in range(2):
                half = slice(a * s.HD, (a + 1) * s.HD)
                do(v.tensor_copy(t.dec[half, :, :], dec8[half, :, a:8:2]))
            dve.wait_ge(ten, 4)
            for i in range(2):
                do(v.tensor_copy(rowsT[:, i, :, :], ps[2 + i][:, 0:GT * P].rearrange("p (g c) -> p g c", g=GT)),
                   f"rows{i}")
            do(v.tensor_tensor(lsum[:, :, :], t.logit2[:, :, 0, :], t.logit2[:, :, 1, :], ALU.add))
            do(v.tensor_tensor(u[:, :, :], lsum[:, :, :], wide(t.rows[:, 2:3, :], full), ALU.add))
            do(v.tensor_reduce(top[:, :, :], u[:, :, :], AX.X, ALU.max))
            do(v.tensor_tensor(lsum[:, :, :], u[:, :, :], wide(top[:, :, :], full), ALU.subtract), "shifted")
            dve.wait_ge(sca, 8)
            do(v.tensor_reduce(esum[:, :, :], ecum[:, :, :], AX.X, ALU.add))
            do(v.reciprocal(einv[:, :, :], esum[:, :, :]))
            do(v.tensor_tensor(t.gates[:, :, :], ecum[:, :, :], wide(einv[:, :, :], full), ALU.mult), "gates")
            gates_by_group = t.gates[:, :, :].rearrange("p (q g) e -> p g q e", g=GT)
            do(v.tensor_copy(gates_g[:, :, :, :], gates_by_group), "gates_g")
            dve.wait_ge(ten, 5)
            do(v.tensor_copy(t.gateT[:, :], ps[4][:, 0:SEG]))

        @block.scalar
        def _(act):
            def split(n):
                act.wait_ge(w_loaded[n], 16)
                nc.scalar.activation(t.wbc_hi[n][:, :, :], w_raw[n][:, :, :], ACT.Copy).then_inc(w_hi, 1)

            def x_split(b):
                act.wait_ge(x2_loaded[b], 16)
                nc.scalar.activation(t.x_hi[b][:, :, :], t.x2[b][:, :, :], ACT.Copy).then_inc(x_hi, 1)

            nc.scalar.activation(a_pos[:, :, :], t.rows[:, 0:1, :], ACT.Exp).then_inc(sca, 1)
            act.wait_ge(vec, steps["u"])
            nc.scalar.activation(gap[:, :, :], u[:, :, :], ACT.Abs).then_inc(sca, 1)
            act.wait_ge(sca, 2)
            nc.scalar.activation(e1[:, :, :], gap[:, :, :], ACT.Exp, scale=-1.0).then_inc(sca, 1)
            act.wait_ge(vec, steps["w1"])
            nc.scalar.activation(ln[:, :, :], w1[:, :, :], ACT.Ln).then_inc(sca, 1)
            x_split(0)
            split(0)
            split(1)
            act.wait_ge(vec, steps["cum"])
            nc.scalar.activation(ecum[:, :, :], t.cum[:, :, :], ACT.Exp).then_inc(sca, 1)
            act.wait_ge(vec, steps["gap"])
            nc.scalar.activation(wexp[:, :, :], gap[:, :, :], ACT.Exp).then_inc(sca, 1)
            nc.scalar.activation(dec8[:, :, :], ps[1][:, 0:NT * H].rearrange("p (t h) -> p t h", h=H),
                                 ACT.Exp).then_inc(sca, 1)
            def tile_copy(n):
                act.wait_ge(tile_mm, n + 1)
                nc.scalar.activation((t.bT0, t.cT0)[n // s.MT][:, n % s.MT, :], ps[6 + n % 2][:, :],
                                     ACT.Copy).then_inc(tile_out, 1)

            x_split(1)
            tile_copy(0)
            act.wait_ge(vec, steps["shifted"])
            act.wait_ge(ten, 4)
            nc.scalar.activation(ecum[:, :, :], lsum[:, :, :], ACT.Exp).then_inc(sca, 1)
            for n in range(1, 2 * s.MT):
                tile_copy(n)

        @block.tensor
        def _(pe):
            pe.wait_ge(vec, steps["dta"])
            flat = dta[:, :, :].rearrange("p t h -> p (t h)")
            pe.matmul(ps[0][:, 0:NT * H], t.tri, flat, start=True, stop=True).then_inc(ten, 1)
            pe.matmul(ps[1][:, 0:NT * H], t.ones, flat, start=True, stop=True).then_inc(ten, 1)
            for i, (src, ready, n) in enumerate(((t.cum, vec, steps["cum"]), (ecum, sca, 5))):
                pe.wait_ge(ready, n)
                for g in range(GT):
                    mm = pe.transpose(ps[2 + i][:, g * P:(g + 1) * P],
                                      src[:, g * s.NSEG:(g + 1) * s.NSEG, :].rearrange("p t h -> p (t h)"), t.ident)
                mm.then_inc(ten, 1)
            def tile(n):
                which, m = n // s.MT, n % s.MT
                pe.wait_ge(w_lo, which + 1)
                pe.wait_ge(x_lo, 1)
                if n >= 2:
                    pe.wait_ge(tile_out, n - 1)
                i = 0
                for k in range(s.MT):
                    for w, x in ((t.wbc_hi[which], t.x_hi[0]), (t.wbc_lo[which], t.x_hi[0]),
                                 (t.wbc_hi[which], t.x_lo[0])):
                        mm = pe.matmul(ps[6 + n % 2][:, :], w[:, k, m * P:(m + 1) * P], x[:, k, :],
                                       start=(i == 0), stop=(i == 3 * s.MT - 1))
                        i += 1
                mm.then_inc(tile_mm, 1)

            for n in range(s.MT):
                tile(n)
            pe.wait_ge(vec, steps["gates_g"])
            for g in range(GT):
                mm = pe.transpose(ps[4][:, g * P:(g + 1) * P],
                                  gates_g[:, g, :, :].rearrange("p q e -> p (q e)"), t.ident)
            mm.then_inc(ten, 1)
            for n in range(s.MT, 2 * s.MT):
                tile(n)

        @block.gpsimd
        def _(pool):
            def x_low(b):
                pool.wait_ge(x_hi, b + 1)
                nc.gpsimd.tensor_tensor(t.x_lo[b][:, :, :], t.x2[b][:, :, :], t.x_hi[b][:, :, :].bitcast(F32),
                                        ALU.subtract).then_inc(x_lo, 1)

            x_low(0)
            for n in range(2):
                pool.wait_ge(w_hi, n + 1)
                nc.gpsimd.tensor_tensor(t.wbc_lo[n][:, :, :], w_raw[n][:, :, :], t.wbc_hi[n][:, :, :].bitcast(F32),
                                        ALU.subtract).then_inc(w_lo, 1)
            x_low(1)

        @block.sync
        def _(sp):
            sp.dma_start(t.x2[0][:, :, :], t.x2_dram[0]).then_inc(x2_loaded[0], 16)
            for n, w in enumerate((wb_d, wc_d)):
                sp.dma_start(w_raw[n][:, :, :], w.rearrange("(k p) n -> p k n", p=P)).then_inc(w_loaded[n], 16)
            sp.dma_start(t.x2[1][:, :, :], t.x2_dram[1]).then_inc(x2_loaded[1], 16)
            sp.wait_ge(vec, steps["rows1"])
            for i, dst in enumerate((t.cum_dram, t.ecum_dram)):
                by_segment = dst.rearrange("(g t) h c -> (t h) g c", t=s.NSEG)
                sp.dma_start(by_segment, rowsT[:, i, :, :]).then_inc(stored, 16)
            sp.wait_ge(vec, steps["gates"])
            sp.dma_start(t.rows_dram[:, s.D:s.ROW].rearrange("(t p) e -> p t e", p=P), t.gates[:, :, :]).then_inc(
                stored, 16)
            sp.wait_ge(stored, 16 * 3)


def phase_scan(nc, s, t):
    MT, H, HD, NB = s.MT, s.H, s.HD, s.NB
    E, LW, GT, SEG, FIRST = s.E, s.LW, s.GT, s.SEG, s.BPB * CH
    CPRE = PRE * CH
    with ExitStack() as ctx:
        def sem(name):
            return ctx.enter_context(nc.semaphore(name))

        def sb(name, shape, dt=F32):
            return ctx.enter_context(nc.sbuf_tensor(name, shape, dt))

        (wb_hi, wc_hi), (wb_lo, wc_lo) = t.wbc_hi, t.wbc_lo
        x2, x_hi, x_lo = t.x2, t.x_hi, t.x_lo
        x_raw = [sb(f"x_raw{i}", [P, BLK]) for i in range(2)]
        bT = [t.bT0, sb("bT1", [P, MT, BLK])]
        cT = [t.cT0, sb("cT1", [P, MT, BLK])]
        cum_row = [sb(f"cum_row{i}", [P, H, P]) for i in range(2)]
        ecum_row = [sb(f"ecum_row{i}", [P, MT, P]) for i in range(2)]
        decay = sb("decay", [P, H, P])
        mix = sb("mix", [P, H, P])
        b_tok = sb("b_tok", [P, s.INNER])
        x_dt = sb("x_dt", [P, MT, 2, P])
        x_w = sb("x_w", [P, s.INNER])
        c_dec = sb("c_dec", [P, MT, P])
        state = sb("state", [P, MT, P])
        yb = [sb(f"yb{i}", [P, MT, BLK]) for i in range(2)]
        ps_g, ps_y, ps_s, ps_xb, ps_r, ps_pb, ps_pc = (t.ps[0:2], t.ps[2], t.ps[3], t.ps[4], t.ps[5], t.ps[6],
                                                       t.ps[7])
        spare = [mix[:, 4 * i:4 * i + 4, :].rearrange("p h n -> p (h n)") for i in range(2)]
        spare += [x_w[:, :], c_dec[:, :, :].rearrange("p m n -> p (m n)")]
        zero = sb("zero", [P, 1, s.D])
        chosen = sb("chosen", [P, SEG])
        bit_i = sb("bit_i", [P, C_END - C_BIT], I32)
        thr, cand, delta = (sb(f"r_{n}", [P, 1], I32) for n in ("thr", "cand", "delta"))
        part, lim, lim2 = (sb(f"r_{n}", [P, 1]) for n in ("part", "lim", "lim2"))
        counts = sb("counts", [P, 4])
        one_hi = [sb(f"one_hi{i}", [P, E, P], BF16) for i in range(2)]
        iota_b = sb("iota_b", [P, P], BF16)
        one_lo = [sb(f"one_lo{i}", [P, E, LW]) for i in range(2)]
        val_lo = [sb(f"val_lo{i}", [P, E, 2, LW], BF16) for i in range(2)]
        zero_b = sb("zero_b", [P, P], BF16)
        lists = sb("lists", [P, E, 2, LW])
        idx_f = sb("idx_f", [P, E, LW])
        hi, lo = (a.rearrange("p (t e) -> p t e", e=E) for a in (t.gateT[:, :], chosen[:, :]))

        zeroed, zero_stored = sem("b_zeroed"), sem("b_zero_stored")
        sel_step, sel_mm = sem("b_sel_step"), sem("b_sel_mm")
        part_done, total_done, bit_step = sem("b_part"), sem("b_total"), sem("b_bit")
        one_lo_done, tile_done, tile_used = sem("b_one_lo"), sem("b_tile"), sem("b_tile_used")
        steps = {}
        state_zeroed = sem("b_state_zeroed")
        x2_loaded = [sem(f"b_x2_loaded{i}") for i in range(2)]
        raw_loaded = [sem(f"b_raw_loaded{i}") for i in range(2)]
        cum_loaded = [sem(f"b_cum_loaded{i}") for i in range(2)]
        ecum_loaded = [sem(f"b_ecum_loaded{i}") for i in range(2)]
        y_stored = [sem(f"b_y_stored{i}") for i in range(2)]
        sp_waited = sem("b_sp_waited")
        waited = sem("b_waited")
        dx_ready, stat_done = sem("b_dx"), sem("b_stat")
        x_hi_ready, x_lo_ready, b_ready, c_ready, b_out, c_out = (
            sem(f"b_{n}") for n in ("x_hi", "x_lo", "b_ready", "c_ready", "b_out", "c_out"))
        x_turned, b_turned, b_tok_ready, g_ready, c_dec_ready, x_dt_ready, x_w_ready = (
            sem(f"b_{n}") for n in ("xt", "bt", "btok", "g", "cdec", "xdt", "xw"))
        gap_ready, exp_ready, decay_ready, mix_ready, y_mm, s_mm, y_ready, state_scaled, state_ready = (
            sem(f"b_{n}") for n in ("gap", "exp", "decay", "mix", "ymm", "smm", "y", "sscaled", "state"))
        block = ctx.enter_context(nc.Block())

        def at(g, back=0):
            return g + (1 + CPRE - back)

        def run(eng, body):
            for bt in range(s.B):
                body_start = bt * s.BPB // 2
                body_end = (bt + 1) * s.BPB // 2 - (1 if bt == s.B - 1 else 0)
                body(bt, None, 0, False, False)
                if body_end > body_start:
                    with eng.Fori(body_start, body_end) as j:
                        for p in range(2):
                            body(bt, 2 * j + p, p, True, True)
            for p in range(2):
                body(None, NB - 2 + p, p, p == 0, False)

        def half_value(b, p, per_pair):
            return (b - p) * (8 * per_pair) + 16 * per_pair

        @block.vector
        def _(dve):
            v = nc.vector
            for c, n in ((gap_ready, CPRE), (x_dt_ready, CPRE),
                         (x_w_ready, CPRE), (mix_ready, 2 * CPRE), (y_ready, CPRE), (state_ready, 2 * CPRE),
                         (stat_done, PRE), (y_stored[0], 16), (y_stored[1], 16)):
                dve.sem_inc(c, n)

            def gaps(g, q, loaded):
                dve.wait_ge(cum_loaded[q], loaded)
                dve.wait_ge(mix_ready, 2 * g + 2 * CPRE)
                for h in range(H):
                    n = v.tensor_scalar(decay[:, (h % 2) * MT + h // 2, :], cum_row[q][:, h, :],
                                        t.cum[:, bass.ds(g, 1), h:h + 1].rearrange("p a b -> p (a b)"), 0.0,
                                        ALU.subtract, ALU.min)
                n.then_inc(gap_ready, 1)

            def heads(ap, g):
                return ap[:, bass.ds(g, 1), :].rearrange("p a h -> p h a").to_broadcast([P, H, HD])

            n = [0]

            def do(ins, name=None):
                n[0] += 1
                ins.then_inc(sel_step, 1)
                dve.wait_ge(sel_step, n[0])
                if name:
                    steps[name] = n[0]

            def count(i):
                v.tensor_tensor(cand[:, :], thr[:, :], bit_i[:, bass.ds(i, 1)], ALU.bitwise_or).then_inc(bit_step, 1)
                dve.wait_ge(bit_step, 3 * i + 1)
                v.tensor_scalar(chosen[:, :], t.gateT[:, :], cand[:, :].bitcast(F32), 0.0, ALU.is_ge, ALU.add,
                                accum_out=part[:, :]).then_inc(part_done, 1)

            def next_bit(g):
                dve.wait_ge(total_done, g + 1)
                v.tensor_scalar(delta[:, :], ps_r[:, 0:1], float(s.CAP), t.cst[:, bass.ds(C_BIT + g, 1)],
                                ALU.is_ge, ALU.mult).then_inc(bit_step, 1)
                dve.wait_ge(bit_step, 3 * g + 2)
                v.tensor_tensor(thr[:, :], thr[:, :], delta[:, :], ALU.bitwise_or).then_inc(bit_step, 1)
                dve.wait_ge(bit_step, 3 * g + 3)
                count(g + 1)

            def select():
                dve.wait_ge(y_mm, CH * s.BPB + CPRE)
                dve.wait_ge(part_done, FIRST + 1)
                slot_i, hi_i, lo_i = (a.bitcast(I32).rearrange("p (t e) -> p t e", e=E) for a in spare[1:4])
                ones_row = t.ones[:, 0:1].to_broadcast([P, SEG])
                tf = thr[:, :].bitcast(F32)
                do(v.tensor_scalar(spare[0], t.gateT[:, :], tf, 0.0, ALU.is_gt, ALU.add, accum_out=counts[:, 0:1]))
                do(v.tensor_scalar(spare[1], t.gateT[:, :], tf, 0.0, ALU.is_equal, ALU.add, accum_out=counts[:, 1:2]),
                   "counts")
                do(v.tensor_tensor_scan(spare[2], ones_row, spare[1], 0.0, ALU.mult, ALU.add))
                dve.wait_ge(sel_mm, 1)
                do(v.tensor_scalar(lim[:, :], ps_r[:, 0:1], -1.0, float(s.CAP), ALU.mult, ALU.add))
                do(v.tensor_tensor(lim2[:, :], ps_r[:, 1:2], lim[:, :], ALU.subtract))
                do(v.tensor_scalar(lim[:, :], lim2[:, :], -1.0, None, ALU.mult))
                do(v.scalar_tensor_tensor(spare[3], spare[2], lim[:, :], spare[1], ALU.is_le, ALU.mult))
                do(v.tensor_tensor(chosen[:, :], spare[0], spare[3], ALU.add))
                do(v.tensor_tensor_scan(spare[2], ones_row, chosen[:, :], 0.0, ALU.mult, ALU.add))
                do(v.tensor_copy(counts[:, 2:3], spare[2][:, SEG - 1:SEG]), "selected")
                dve.wait_ge(sel_mm, 2)
                do(v.tensor_scalar(lim2[:, :], ps_r[:, 2:3], 0.0, None, ALU.add))
                do(v.scalar_tensor_tensor(spare[3], spare[2], lim2[:, :], chosen[:, :], ALU.add, ALU.mult))
                do(v.tensor_scalar(spare[0], spare[3], -1.0, None, ALU.add), "slot")
                dve.wait_ge(sel_mm, 3)
                do(v.tensor_copy(slot_i.rearrange("p (q g) e -> p g q e", g=GT),
                                 ps_r[:, 0:SEG].rearrange("p (g q e) -> p g q e", g=GT, e=E)),
                   "slot_i")
                do(v.tensor_scalar(hi_i, slot_i, LW.bit_length() - 1, None, ALU.arith_shift_right))
                do(v.tensor_scalar(lo_i, slot_i, LW - 1, None, ALU.bitwise_and))
                do(v.tensor_copy(hi, hi_i))
                do(v.tensor_copy(lo, lo_i), "lo")

            def token_tile(g, q):
                i = 2 * g + (q - 2 * FIRST)
                dve.wait_ge(tile_used, i + 1)
                v.tensor_tensor(one_lo[q][:, :, :], lo[:, bass.ds(i, 1), :].rearrange("p a e -> p e a")
                                .to_broadcast([P, E, LW]),
                                t.cst[:, C_LO:C_LO + LW].unsqueeze(1).to_broadcast([P, E, LW]),
                                ALU.is_equal).then_inc(one_lo_done, 1)
                for e in range(E):
                    v.tensor_scalar(one_hi[q][:, e, :], iota_b[:, :],
                                    hi[:, bass.ds(i, 1), e:e + 1].rearrange("p a e -> p (a e)"), None, ALU.is_equal)
                dve.wait_ge(one_lo_done, i + 1)
                v.tensor_scalar(val_lo[q][:, :, 0, :], one_lo[q][:, :, :], t.cst[:, bass.ds(C_TAU + i, 1)],
                                None, ALU.mult)
                v.tensor_scalar(val_lo[q][:, :, 1, :], one_lo[q][:, :, :], t.cst[:, C_PIDX:C_PIDX + 1],
                                None, ALU.mult).then_inc(tile_done, 1)

            def body(bt, b, p, nxt, nxt2):
                if b is None:
                    dve.wait_ge(s_mm, CH * bt * s.BPB + CPRE)
                    dve.wait_ge(state_ready, 2 * CH * bt * s.BPB + 2 * CPRE)
                    v.memset(state[:, :, :], 0.0).then_inc(state_zeroed, 1)
                    dve.wait_ge(state_zeroed, bt + 1)
                    if bt == 1:
                        select()
                        for q in range(2):
                            token_tile(FIRST, q)
                    return
                for c in range(CH):
                    g = CH * b + c
                    cols = slice(c * P, (c + 1) * P)
                    dve.wait_ge(y_mm, at(g, 1))
                    dve.wait_ge(x_turned, at(g))
                    x_heads = ps_xb[:, :].rearrange("p (h n) -> p h n", h=H)
                    for a in range(2):
                        n = v.tensor_tensor(x_dt[:, :, a, a * HD:(a + 1) * HD], x_heads[:, a:H:2, :],
                                            heads(t.dt, g)[:, a:H:2, :], ALU.mult)
                    n.then_inc(x_dt_ready, 1)
                    dve.wait_ge(s_mm, at(g, 1))
                    v.tensor_tensor(x_w[:, :].rearrange("p (h n) -> p h n", h=H), x_heads, heads(t.wst, g),
                                    ALU.mult).then_inc(x_w_ready, 1)
                    dve.wait_ge(decay_ready, at(g))
                    for i in range(2):
                        dve.wait_ge(g_ready, g + 1)
                        v.tensor_tensor(mix[:, 4 * i:4 * i + 4, :],
                                        ps_g[i][:, :].rearrange("p (h n) -> p h n", h=4),
                                        decay[:, 4 * i:4 * i + 4, :], ALU.mult).then_inc(mix_ready, 1)
                    if c < CH - 1 or nxt:
                        q = (c + 1) % 2
                        gaps(g + 1, q, b * 32 + (16 * ((c + 1) // 2 + 1)))
                    if bt == 0:
                        next_bit(g)
                    elif c < CH - 1 or nxt:
                        for q in range(2):
                            token_tile(g + 1, q)
                    dve.wait_ge(y_mm, at(g))
                    if c == 0:
                        dve.wait_ge(dx_ready, b + (PRE + 1))
                    v.tensor_tensor(yb[p][:, :, cols], ps_y[:, :].rearrange("p (m n) -> p m n", m=MT),
                                    yb[p][:, :, cols], ALU.add).then_inc(y_ready, 1)
                    dve.wait_ge(state_ready, 2 * g + 2 * CPRE)
                    v.tensor_tensor(state[:, :, :], state[:, :, :],
                                    t.dec[:, bass.ds(g, 1), :].rearrange("p a m -> p m a").to_broadcast([P, MT, P]),
                                    ALU.mult).then_inc(state_scaled, 1)
                    dve.wait_ge(state_scaled, g + 1)
                    dve.wait_ge(s_mm, at(g))
                    for a in range(2):
                        r = slice(a * HD, (a + 1) * HD)
                        v.tensor_tensor(state[r, :, r], ps_s[r, :].rearrange("p (m n) -> p m n", m=MT)[:, :, r],
                                        state[r, :, r], ALU.add).then_inc(state_ready, 1)
                dve.wait_ge(y_ready, at(CH * b, 1 - CH))
                for m in range(MT):
                    n = v.bn_stats(t.ystat[:, bass.ds(b, 1), m, :].rearrange("p a k -> p (a k)"), yb[p][:, m, :])
                n.then_inc(stat_done, 1)

            v.memset(zero_b[:, :], 0.0).then_inc(zeroed, 1)
            do(v.memset(thr[:, :], 0))
            do(v.tensor_copy(iota_b[:, :], t.iota))
            do(v.tensor_copy(bit_i[:, :], t.cst[:, C_BIT:C_END]))
            gaps(0, 0, 16)
            count(0)
            run(dve, body)
            dve.wait_ge(sel_mm, 4)
            do(v.tensor_copy(lists[:, :, :, :], ps_r[:, 0:2 * E * LW].rearrange("p (e k l) -> p e k l", e=E, k=2)))
            do(v.scalar_tensor_tensor(idx_f[:, :, :], lists[:, :, 0, :], float(P), lists[:, :, 1, :], ALU.mult,
                                      ALU.add))
            do(v.tensor_copy(t.idx[:, :, :], idx_f[:, :, :]))

        @block.sync
        def _(sp):
            def load_raw(b, m):
                sp.wait_ge(x_lo_ready, MT * b + (m - 2 + 1 + CPRE))
                sp.dma_start(x_raw[m % 2][:, :], t.x2_dram[b][:, m, :]).then_inc(raw_loaded[m % 2], 16)

            def load_cum(g, q):
                sp.wait_ge(gap_ready, at(g, 2))
                sp.dma_start(cum_row[q][:, :, :], t.cum_dram[g].partition_broadcast(P)).then_inc(cum_loaded[q], 16)

            def load_ecum(g, q):
                sp.wait_ge(c_dec_ready, at(g, 2))
                for a in range(2):
                    sp.dma_start(ecum_row[q][a * HD:(a + 1) * HD, :, :],
                                 t.ecum_dram[g].rearrange("(m a) c -> a m c", a=2)[a].partition_broadcast(HD)
                                 ).then_inc(ecum_loaded[q], 16)

            def load_x2(b, p):
                sp.wait_ge(dx_ready, b + (PRE - 1))
                sp.sem_inc(sp_waited, 1)
                sp.wait_ge(x_turned, at(CH * b, CH + 1))
                sp.dma_start(x2[p][:, :, :], t.x2_dram[b]).then_inc(x2_loaded[p], 16)

            def body(bt, b, p, nxt, nxt2):
                if b is None:
                    return
                if nxt:
                    load_x2(b + 1, 1 - p)
                sp.dma_start(t.ffn_blk[b], zero[:, :, :].to_broadcast([P, CH, s.D])).then_inc(zero_stored, 16)
                for c in range(CH):
                    g = CH * b + c
                    if c < CH - 2 or nxt:
                        load_cum(g + 2, c % 2)
                        load_ecum(g + 2, c % 2)
                    if nxt2:
                        load_raw(b + 2, c)
                sp.wait_ge(y_ready, at(CH * b, 1 - CH))
                sp.dma_start(t.y_dram[b], yb[p][:, :, :]).then_inc(y_stored[p], 16)

            sp.sem_inc(x2_loaded[0], 16)
            for g in range(2):
                load_cum(g, g)
                load_ecum(g, g)
            sp.wait_ge(zeroed, 3)
            run(sp, body)
            sp.wait_ge(zero_stored, 16 * NB)
            for p in range(2):
                sp.wait_ge(y_stored[p], 16 * (NB // 2 + 1))

        @block.gpsimd
        def _(pool):
            pool.sem_inc(dx_ready, PRE)
            for c in (decay_ready, x_lo_ready, c_dec_ready):
                pool.sem_inc(c, CPRE)
            pool.sem_inc(x_lo_ready, 2 * MT)
            nc.gpsimd.memset(x_dt[:, :, :, :], 0.0).then_inc(zeroed, 1)
            nc.gpsimd.memset(zero[:, :, :], 0.0).then_inc(zeroed, 1)

            def causal(g):
                pool.wait_ge(exp_ready, at(g))
                pool.sem_inc(waited, 1)
                nc.gpsimd.affine_select(out=decay[:, :, :], in_=decay[:, :, :], compare_op=ALU.is_ge, fill=0.0,
                                        base=0, pattern=[[0, H], [1, P]], channel_multiplier=-1).then_inc(
                    decay_ready, 1)

            def lo_part(b, p, m):
                pool.wait_ge(x_hi_ready, MT * b + (m + 1 + CPRE))
                nc.gpsimd.tensor_tensor(x_lo[p][:, m, :], x_raw[m % 2][:, :], x_hi[p][:, m, :].bitcast(F32),
                                        ALU.subtract).then_inc(x_lo_ready, 1)

            def decay_c(b, p, g, c):
                pool.wait_ge(c_out, CH * b + CPRE + CH)
                pool.wait_ge(ecum_loaded[c % 2], b * 64 + (32 * (c // 2 + 1)))
                pool.wait_ge(y_mm, at(g, 1))
                nc.gpsimd.tensor_tensor(c_dec[:, :, :], cT[p][:, :, c * P:(c + 1) * P], ecum_row[c % 2][:, :, :],
                                        ALU.mult).then_inc(c_dec_ready, 1)

            def scale_x(b, p, m):
                if m == 0:
                    pool.wait_ge(x2_loaded[p], half_value(b, p, 1))
                    pool.wait_ge(y_stored[p], half_value(b, p, 1))
                    pool.wait_ge(stat_done, b + (PRE - 1))
                    pool.sem_inc(waited, 1)
                n = nc.gpsimd.tensor_scalar(yb[p][:, m, :], x2[p][:, m, :], t.dcol[:, m:m + 1], 0.0, ALU.mult,
                                            ALU.add)
                if m == MT - 1:
                    n.then_inc(dx_ready, 1)

            def body(bt, b, p, nxt, nxt2):
                if b is None:
                    if bt == 1:
                        pool.wait_ge(sel_step, steps["lo"])
                    return
                for c in range(CH):
                    g = CH * b + c
                    decay_c(b, p, g, c)
                    if c < CH - 1 or nxt:
                        causal(g + 1)
                    if nxt:
                        scale_x(b + 1, 1 - p, c)
                    if nxt2:
                        lo_part(b + 2, p, c)

            for m in range(MT):
                scale_x(0, 0, m)
            causal(0)
            run(pool, body)

        @block.scalar
        def _(act):
            for c in (exp_ready, b_out, c_out, b_tok_ready, x_hi_ready):
                act.sem_inc(c, CPRE)

            def hi_part(b, p, m, loaded):
                act.wait_ge(raw_loaded[m % 2], loaded)
                act.wait_ge(c_ready, MT * b + (MT * (PRE - 1)))
                nc.scalar.activation(x_hi[p][:, m, :], x_raw[m % 2][:, :], ACT.Copy).then_inc(x_hi_ready, 1)

            def b_part(b, p, m):
                act.wait_ge(b_ready, MT * b + (m + 1 + CPRE))
                nc.scalar.activation(bT[p][:, m, :], ps_pb[:, :], ACT.Copy).then_inc(b_out, 1)

            def c_part(b, p, m):
                act.wait_ge(c_ready, MT * b + (m + 1 + CPRE))
                nc.scalar.activation(cT[p][:, m, :], ps_pc[:, :], ACT.Copy).then_inc(c_out, 1)

            def decays(g):
                act.wait_ge(gap_ready, at(g))
                nc.scalar.activation(decay[:, :, :], decay[:, :, :], ACT.Exp).then_inc(exp_ready, 1)

            def body(bt, b, p, nxt, nxt2):
                if b is None:
                    return
                for c in range(CH):
                    g = CH * b + c
                    if nxt:
                        b_part(b + 1, 1 - p, c)
                    act.wait_ge(b_turned, at(g))
                    act.wait_ge(s_mm, at(g, 1))
                    nc.scalar.activation(b_tok[:, :], ps_xb[:, :], ACT.Copy).then_inc(b_tok_ready, 1)
                    if c < CH - 1 or nxt:
                        decays(g + 1)
                    if nxt:
                        c_part(b + 1, 1 - p, c)
                    if nxt2:
                        hi_part(b + 2, p, c, b * 32 + (16 * (c // 2 + 1)))

            for c, n in ((x_hi_ready, 2), (b_out, 1), (c_out, 1)):
                act.sem_inc(c, n * MT)
            decays(0)
            run(act, body)

        @block.tensor
        def _(pe):
            for c in (b_ready, c_ready, x_turned, b_turned, y_mm, s_mm):
                pe.sem_inc(c, CPRE)
            for c in (b_ready, c_ready):
                pe.sem_inc(c, MT)

            def project(b, p, m, which):
                pe.wait_ge(x_lo_ready, MT * b + (MT + CPRE))
                for w_h, w_l, ps, ready, drained in (((wb_hi, wb_lo, ps_pb, b_ready, b_out),
                                                      (wc_hi, wc_lo, ps_pc, c_ready, c_out))[which],):
                    pe.wait_ge(drained, MT * b + (m + CPRE))
                    n = 0
                    for k in range(MT):
                        for w, x in ((w_h, x_hi[p]), (w_l, x_hi[p]), (w_h, x_lo[p])):
                            mm = pe.matmul(ps[:, :], w[:, k, m * P:(m + 1) * P], x[:, k, :],
                                           start=(n == 0), stop=(n == 3 * MT - 1))
                            n += 1
                    mm.then_inc(ready, 1)

            W = 2 * E * LW

            def select():
                pe.wait_ge(sel_step, steps["counts"])
                pe.matmul(ps_r[:, 0:1], t.rsum, counts[:, 0:1], start=True, stop=True)
                pe.matmul(ps_r[:, 1:2], t.rtri, counts[:, 1:2], start=True, stop=True).then_inc(sel_mm, 1)
                pe.wait_ge(sel_step, steps["selected"])
                pe.matmul(ps_r[:, 2:3], t.rtri, counts[:, 2:3], start=True, stop=True).then_inc(sel_mm, 1)
                pe.wait_ge(sel_step, steps["slot"])
                for g in range(GT):
                    mm = pe.transpose(ps_r[:, g * P:(g + 1) * P], spare[0][:, g * P:(g + 1) * P], t.ident)
                mm.then_inc(sel_mm, 1)
                pe.wait_ge(sel_step, steps["slot_i"])
                pe.matmul(ps_r[:, 0:W], zero_b[:, :], zero_b[:, 0:W], start=True, stop=False, skip_group_check=True)

            def list_tile(g, q):
                i = 2 * g + (q - 2 * FIRST)
                pe.wait_ge(tile_done, i + 1)
                for e in range(E):
                    mm = pe.matmul(ps_r[:, e * 2 * LW:(e + 1) * 2 * LW], one_hi[q][:, e, :],
                                   val_lo[q][:, e, :, :].rearrange("p k l -> p (k l)"),
                                   start=False, stop=False, skip_group_check=True)
                mm.then_inc(tile_used, 1)

            def body(bt, b, p, nxt, nxt2):
                if b is None:
                    if bt == 1:
                        select()
                    return
                pe.wait_ge(x2_loaded[p], half_value(b, p, 1))
                pe.wait_ge(b_out, MT * b + (MT + CPRE))
                pe.wait_ge(c_out, MT * b + (MT + CPRE))
                for c in range(CH):
                    g = CH * b + c
                    cols = slice(c * P, (c + 1) * P)
                    pe.wait_ge(b_tok_ready, at(g, 1))
                    for m in range(MT):
                        mm = pe.transpose(ps_xb[:, m * P:(m + 1) * P], x2[p][:, m, cols], t.ident)
                    mm.then_inc(x_turned, 1)
                    pe.wait_ge(mix_ready, 2 * g + 2 * CPRE)
                    for m in range(MT):
                        for a in range(2):
                            r = slice(a * HD, (a + 1) * HD)
                            mm = pe.matmul(ps_g[a][:, m * P:(m + 1) * P], bT[p][r, m, cols], cT[p][r, m, cols],
                                           start=True, stop=True)
                    mm.then_inc(g_ready, 1)
                    if bt == 0:
                        pe.wait_ge(part_done, g + 1)
                        pe.matmul(ps_r[:, 0:1], t.rsum, part[:, :], start=True, stop=True).then_inc(total_done, 1)
                    else:
                        for q in range(2):
                            list_tile(g, q)
                    if nxt:
                        project(b + 1, 1 - p, c, 0)
                    pe.wait_ge(x_w_ready, at(g))
                    pe.wait_ge(x_dt_ready, at(g))
                    for m in range(MT):
                        mm = pe.transpose(ps_xb[:, m * P:(m + 1) * P], bT[p][:, m, cols], t.ident)
                    mm.then_inc(b_turned, 1)
                    if nxt:
                        project(b + 1, 1 - p, c, 1)
                    pe.wait_ge(y_ready, at(g, 1))
                    pe.wait_ge(x_dt_ready, at(g))
                    pe.wait_ge(c_dec_ready, at(g))
                    pe.wait_ge(mix_ready, 2 * g + (2 * CPRE + 2))
                    pe.wait_ge(state_ready, 2 * g + 2 * CPRE)
                    for m in range(MT):
                        out = ps_y[:, m * P:(m + 1) * P]
                        for a in range(2):
                            pe.matmul(out, x_dt[:, m, a, :], mix[:, a * MT + m, :], start=(a == 0), stop=False)
                        mm = pe.matmul(out, state[:, m, :], c_dec[:, m, :], start=False, stop=True)
                    mm.then_inc(y_mm, 1)
                    pe.wait_ge(x_w_ready, at(g))
                    pe.wait_ge(b_tok_ready, at(g))
                    for m in range(MT):
                        mm = pe.matmul(ps_s[:, m * P:(m + 1) * P], b_tok[:, m * P:(m + 1) * P],
                                       x_w[:, m * P:(m + 1) * P], start=True, stop=True)
                    mm.then_inc(s_mm, 1)

            pe.wait_ge(zeroed, 3)
            pe.sem_inc(tile_used, 2)
            run(pe, body)
            pe.matmul(ps_r[:, 0:W], zero_b[:, :], zero_b[:, 0:W], start=False, stop=True,
                      skip_group_check=True).then_inc(sel_mm, 1)


def phase_experts(nc, s, t, wup_d, bup_d, wdn_d, wout_d, wz_d):
    MT, B, BPB = s.MT, s.B, s.BPB
    KT, FT, FR, F, HC, NH, E = s.KT, s.FT, s.FR, s.F, s.HC, s.NH, s.E
    HALF, GS = s.HALF, s.GS
    with ExitStack() as ctx:
        def sem(name):
            return ctx.enter_context(nc.semaphore(name))

        def sb(name, shape, dt=F32):
            return ctx.enter_context(nc.sbuf_tensor(name, shape, dt))

        up_raw = sb("up_raw", [P, KT, F])
        up_hi = [sb(f"up_hi{i}", [P, KT, F], F32R) for i in range(2)]
        up_lo = [sb(f"up_lo{i}", [P, KT, F], F32R) for i in range(2)]
        b_up = [sb(f"b_up{i}", [P, FT]) for i in range(2)]
        dn_raw = [sb(f"dn_raw{i}", [P, FT, s.D]) for i in range(2)]
        dn_hi = [sb(f"dn_hi{i}", [P, FT, s.D], F32R) for i in range(2)]
        dn_lo = [sb(f"dn_lo{i}", [P, FT, s.D], F32R) for i in range(2)]
        xg = [sb(f"xg{i}", [P, HC, s.ROW]) for i in range(2)]
        xg_hi = [sb(f"xg_hi{i}", [P, KT, HALF], F32R) for i in range(2)]
        xg_lo = [sb(f"xg_lo{i}", [P, KT, HALF], F32R) for i in range(2)]
        mid = [sb(f"mid{i}", [P, HALF]) for i in range(3)]
        mid_hi = [sb(f"mid_hi{i}", [P, FT, HALF], F32R) for i in range(2)]
        mid_lo = [sb(f"mid_lo{i}", [P, FT, HALF], F32R) for i in range(2)]
        one_rows = sb("one_rows", [P, HALF])
        gate_col = [sb(f"gate_col{i}", [P, HC, 1]) for i in range(2)]
        ob = [sb(f"ob{i}", [P, HC, s.D]) for i in range(2)]
        wo_raw, wz_raw = sb("wo_raw", [P, MT, s.D]), sb("wz_raw", [P, KT, s.INNER])
        n0, n1, n2, n3, n4, mean_c, var_c = (sb(f"n{i}", [P, B, MT]) for i in range(7))
        scale, shift = t.scale, t.shift
        g0, g1, g2, g3 = (sb(f"g{i}", [P, B, MT, BPB]) for i in range(4))
        moments = sb("moments", [P, 2, B, MT])
        ps_m = t.ps[7]
        vec, dev_ready, mom_ready = sem("f_vec"), sem("f_dev"), sem("f_mom")
        out_w_loaded, out_w_hi, out_w_lo, xn_loaded = sem("f_wo"), sem("f_woh"), sem("f_wol"), sem("f_xn")
        steps = {}
        ps_t, ps_u, ps_d = t.ps[0:2], t.ps[2:5], t.ps[5:8]

        up_loaded, dn_loaded = [sem(f"f_up_loaded{i}") for i in range(2)], [sem(f"f_dn_loaded{i}") for i in range(2)]
        up_hi_ready, up_lo_ready, dn_hi_ready, dn_lo_ready = (sem(f"f_{n}") for n in ("uph", "upl", "dnh", "dnl"))
        gathered = [sem(f"f_gathered{i}") for i in range(2)]
        turned, xg_hi_ready, xg_lo_ready = sem("f_turned"), sem("f_xgh"), sem("f_xgl")
        up_mm, mid_ready, mid_hi_ready, mid_lo_ready, dn_mm, out_ready = (
            sem(f"f_{n}") for n in ("up_mm", "mid", "midh", "midl", "dn_mm", "out"))
        ones_ready, gate_copied = sem("f_ones"), sem("f_gate")
        added = [sem(f"f_added{i}") for i in range(2)]
        block = ctx.enter_context(nc.Block())
        passes = [(u, u // NH, u % NH) for u in range(E * NH)]

        def rows_of(f):
            return P if f < FT - 1 else FR + 1

        @block.vector
        def _(dve):
            v = nc.vector
            n = [0]

            def do(ins, name=None):
                n[0] += 1
                ins.then_inc(vec, 1)
                dve.wait_ge(vec, n[0])
                if name:
                    steps[name] = n[0]

            half = [t.ystat[:, :, :, k].rearrange("p (a b) m -> p a m b", a=B) for k in (1, 2, 4, 5)]
            do(v.tensor_tensor(g0[:, :, :, :], half[0], half[2], ALU.add))
            do(v.tensor_reduce(n0[:, :, :].unsqueeze(3), g0[:, :, :, :], AX.X, ALU.add))
            do(v.tensor_scalar(mean_c[:, :, :], n0[:, :, :], 0.5 / BPB, None, ALU.mult))
            mb = mean_c[:, :, :].unsqueeze(3).to_broadcast([P, B, MT, BPB])
            do(v.tensor_tensor(g0[:, :, :, :], half[0], mb, ALU.subtract))
            do(v.tensor_tensor(g1[:, :, :, :], half[2], mb, ALU.subtract))
            do(v.tensor_tensor(g2[:, :, :, :], g0[:, :, :, :], g0[:, :, :, :], ALU.mult))
            do(v.tensor_tensor(g3[:, :, :, :], g1[:, :, :, :], g1[:, :, :, :], ALU.mult))
            do(v.tensor_tensor(g0[:, :, :, :], g2[:, :, :, :], g3[:, :, :, :], ALU.add))
            do(v.tensor_tensor(g1[:, :, :, :], half[1], half[3], ALU.add))
            do(v.scalar_tensor_tensor(g2[:, :, :, :].rearrange("p a m b -> p (a m b)"),
                                      g0[:, :, :, :].rearrange("p a m b -> p (a m b)"), float(BLK // 2),
                                      g1[:, :, :, :].rearrange("p a m b -> p (a m b)"), ALU.mult, ALU.add))
            do(v.tensor_reduce(n1[:, :, :].unsqueeze(3), g2[:, :, :, :], AX.X, ALU.add))
            do(v.tensor_scalar(var_c[:, :, :], n1[:, :, :], 1.0 / s.L, None, ALU.mult))
            do(v.tensor_copy(moments[:, 0, :, :], mean_c[:, :, :]))
            do(v.tensor_tensor(n0[:, :, :], mean_c[:, :, :], mean_c[:, :, :], ALU.mult))
            do(v.tensor_tensor(moments[:, 1, :, :], n0[:, :, :], var_c[:, :, :], ALU.add), "moments")
            dve.wait_ge(mom_ready, 1)
            do(v.tensor_copy(moments[:, :, :, :], ps_m[:, 0:2 * B * MT].rearrange("p (k a m) -> p k a m", k=2, a=B)),
               "moments_read")
            do(v.tensor_tensor(n0[:, :, :], moments[:, 0, :, :], moments[:, 0, :, :], ALU.mult))
            do(v.tensor_tensor(n1[:, :, :], moments[:, 1, :, :], n0[:, :, :], ALU.subtract))
            do(v.tensor_scalar(n2[:, :, :], n1[:, :, :], EPS, None, ALU.add), "var")
            dve.wait_ge(dev_ready, 1)
            do(v.reciprocal(n0[:, :, :], n3[:, :, :]))
            do(v.tensor_tensor(n1[:, :, :], n0[:, :, :], n0[:, :, :], ALU.mult))
            do(v.scalar_tensor_tensor(n4[:, :, :], n1[:, :, :], -0.5, n2[:, :, :], ALU.mult, ALU.mult))
            do(v.scalar_tensor_tensor(n1[:, :, :], n4[:, :, :], 1.5, n0[:, :, :], ALU.add, ALU.mult))
            wide = [w[:, :].unsqueeze(1).to_broadcast([P, B, MT]) for w in (t.gnw, t.gnb)]
            do(v.tensor_tensor(scale[:, :, :], n1[:, :, :], wide[0], ALU.mult))
            do(v.tensor_tensor(n0[:, :, :], moments[:, 0, :, :], scale[:, :, :], ALU.mult))
            do(v.tensor_tensor(shift[:, :, :], wide[1], n0[:, :, :], ALU.subtract), "affine")

            v.memset(one_rows[:, :], 1.0).then_inc(ones_ready, 1)
            dve.wait_ge(ones_ready, 1)
            for q in range(2):
                v.tensor_copy(mid_hi[q][:, FT - 1, :], one_rows[:, :]).then_inc(ones_ready, 1)
                v.tensor_scalar(mid_lo[q][:, FT - 1, :], one_rows[:, :], 0.0, None, ALU.mult).then_inc(ones_ready, 1)
            dve.wait_ge(ones_ready, 5)

            def split_up(g):
                dve.wait_ge(up_hi_ready, g + 1)
                v.tensor_tensor(up_lo[g % 2][:, :, :], up_raw[:, :, :], up_hi[g % 2][:, :, :].bitcast(F32),
                                ALU.subtract).then_inc(up_lo_ready, 1)

            def split_down(e):
                q = e % 2
                dve.wait_ge(dn_hi_ready, 2 * e + 2)
                for rows, f in ((P, slice(0, FT - 1)), (FR + 1, slice(FT - 1, FT))):
                    v.tensor_tensor(dn_lo[q][0:rows, f, :], dn_raw[q][0:rows, f, :],
                                    dn_hi[q][0:rows, f, :].bitcast(F32), ALU.subtract).then_inc(dn_lo_ready, 1)

            def weigh(u):
                q = u % 2
                if u >= 2:
                    dve.wait_ge(added[q], 16 * HC * (u // 2))
                for c in range(HC):
                    n = u * HC + c
                    dve.wait_ge(dn_mm, n + 1)
                    v.tensor_scalar(ob[q][:, c, :], ps_d[n % 3][:, 0:s.D], gate_col[q][:, c, :], None,
                                    ALU.mult).then_inc(out_ready, 1)

            def split_out():
                dve.wait_ge(out_w_hi, 2)
                for raw, high, low in ((wo_raw, t.wo_hi, t.wo_lo), (wz_raw, t.wz_hi, t.wz_lo)):
                    v.tensor_tensor(low[:, :, :], raw[:, :, :], high[:, :, :].bitcast(F32), ALU.subtract).then_inc(
                        out_w_lo, 1)

            def token_lo(u):
                q = u % 2
                for k in range(KT):
                    dve.wait_ge(xg_hi_ready, KT * u + k + 1)
                    v.tensor_tensor(xg_lo[q][:, k, :], ps_t[k][:, 0:HALF], xg_hi[q][:, k, :].bitcast(F32),
                                    ALU.subtract).then_inc(xg_lo_ready, 1)

            def gate(u):
                q, e = u % 2, u // NH
                if u >= 2:
                    dve.wait_ge(out_ready, HC * (u - 1))
                v.tensor_copy(gate_col[q][:, :, :], xg[q][:, :, s.D + e:s.D + e + 1]).then_inc(gate_copied, 1)

            split_up(0)
            token_lo(0)
            gate(0)
            split_down(0)
            for u, e, h in passes:
                q = u % 2
                for f in range(FT):
                    n = u * FT + f
                    R = P if f < FT - 1 else FR
                    dve.wait_ge(mid_ready, n + 1)
                    if u >= 2 and f == 0:
                        dve.wait_ge(dn_mm, HC * (u - 1))
                    v.tensor_copy(mid_hi[q][0:R, f, :], mid[n % 3][0:R, :]).then_inc(mid_hi_ready, 1)
                    dve.wait_ge(mid_hi_ready, n + 1)
                    v.tensor_tensor(mid_lo[q][0:R, f, :], mid[n % 3][0:R, :], mid_hi[q][0:R, f, :].bitcast(F32),
                                    ALU.subtract).then_inc(mid_lo_ready, 1)
                if u + 1 < len(passes):
                    token_lo(u + 1)
                if u:
                    weigh(u - 1)
                if u + 1 < len(passes):
                    gate(u + 1)
                if (u + 2) % (GS * NH) == 0 and u + 2 < len(passes):
                    split_up((u + 2) // (GS * NH))
                if h == NH - 1 and e + 1 < E:
                    split_down(e + 1)
                if u == len(passes) // 2:
                    split_out()
            weigh(len(passes) - 1)

        @block.sync
        def _(sp):
            def load_up(g):
                if g:
                    sp.wait_ge(up_lo_ready, g)
                sp.dma_start(up_raw[:, :, :], wup_d[g].rearrange("(k p) f -> p k f", p=P)).then_inc(
                    up_loaded[g % 2], 16)
                if g >= 2:
                    sp.wait_ge(mid_ready, NH * FT * GS * (g - 1))
                sp.dma_start(b_up[g % 2][:, :], bup_d[g]).then_inc(up_loaded[g % 2], 16)

            for e in range(E):
                if e % GS == 0:
                    load_up(e // GS)
                if e == 0:
                    sp.wait_ge(gathered[0], 16 * HC)
                if e >= 2:
                    sp.wait_ge(dn_lo_ready, 2 * (e - 1))
                sp.dma_start(dn_raw[e % 2][:, 0:FT - 1, :],
                             wdn_d[e, 0:(FT - 1) * P, :].rearrange("(f p) d -> p f d", p=P)).then_inc(
                    dn_loaded[e % 2], 16)
                sp.dma_start(dn_raw[e % 2][0:FR + 1, FT - 1, :], wdn_d[e, (FT - 1) * P:F + 1, :]).then_inc(
                    dn_loaded[e % 2], 16)
                if e == 2:
                    for raw, w in ((wo_raw, wout_d), (wz_raw, wz_d)):
                        sp.dma_start(raw[:, :, :], w.rearrange("(k p) n -> p k n", p=P)).then_inc(out_w_loaded, 16)
                    sp.dma_start(t.xn_first[:, :, :], t.xn_blk[0]).then_inc(xn_loaded, 16)
            sp.wait_ge(xn_loaded, 16)

        @block.gpsimd
        def _(pool):
            def gather(u, e, h):
                q = u % 2
                if u >= 2:
                    pool.wait_ge(turned, KT * (u - 1))
                    pool.wait_ge(gate_copied, u - 1)
                for c in range(HC):
                    pool.indirect_dma_start(
                        out=xg[q][:, c, :], out_offset=None, in_=t.rows_dram,
                        in_offset=bass.IndirectOffsetOnAxis(ap=t.idx[:, e, h * HC + c:h * HC + c + 1], axis=0),
                    ).then_inc(gathered[q], 16)

            def scatter(u, e, h):
                q = u % 2
                if h == 0 and e:
                    for k in range(2):
                        pool.wait_ge(added[k], 16 * HC * ((u + 1 - k) // 2))
                for c in range(HC):
                    pool.wait_ge(out_ready, HC * u + c + 1)
                    pool.indirect_dma_start(
                        out=t.ffn_dram, out_offset=bass.IndirectOffsetOnAxis(
                            ap=t.idx[:, e, h * HC + c:h * HC + c + 1], axis=0),
                        in_=ob[q][:, c, :], in_offset=None, compute_op=ALU.add).then_inc(added[q], 16)

            gather(*passes[0])
            for u in range(len(passes)):
                if u + 1 < len(passes):
                    gather(*passes[u + 1])
                if u:
                    scatter(*passes[u - 1])
            scatter(*passes[-1])
            for k in range(2):
                pool.wait_ge(added[k], 16 * HC * ((len(passes) + 1 - k) // 2))

        @block.scalar
        def _(act):
            def split_up(g):
                act.wait_ge(up_loaded[g % 2], 32 * (g // 2 + 1))
                if g >= 2:
                    act.wait_ge(up_mm, NH * FT * GS * (g - 1))
                nc.scalar.activation(up_hi[g % 2][:, :, :], up_raw[:, :, :], ACT.Copy).then_inc(up_hi_ready, 1)

            def split_down(e):
                act.wait_ge(dn_loaded[e % 2], 32 * (e // 2 + 1))
                if e >= 2:
                    act.wait_ge(dn_mm, HC * NH * (e - 1))
                nc.scalar.activation(dn_hi[e % 2][:, 0:FT - 1, :], dn_raw[e % 2][:, 0:FT - 1, :],
                                     ACT.Copy).then_inc(dn_hi_ready, 1)
                nc.scalar.activation(dn_hi[e % 2][0:FR + 1, FT - 1, :], dn_raw[e % 2][0:FR + 1, FT - 1, :],
                                     ACT.Copy).then_inc(dn_hi_ready, 1)

            def split_out():
                act.wait_ge(out_w_loaded, 32)
                nc.scalar.activation(t.wo_hi[:, :, :], wo_raw[:, :, :], ACT.Copy).then_inc(out_w_hi, 1)
                nc.scalar.activation(t.wz_hi[:, :, :], wz_raw[:, :, :], ACT.Copy).then_inc(out_w_hi, 1)

            def token_hi(u):
                for k in range(KT):
                    act.wait_ge(turned, KT * u + k + 1)
                    if u >= 2:
                        act.wait_ge(up_mm, FT * (u - 1))
                    nc.scalar.activation(xg_hi[u % 2][:, k, :], ps_t[k][:, 0:HALF], ACT.Copy).then_inc(xg_hi_ready, 1)

            act.wait_ge(vec, steps["var"])
            nc.scalar.activation(n3[:, :, :], n2[:, :, :], ACT.Sqrt).then_inc(dev_ready, 1)
            split_up(0)
            token_hi(0)
            split_down(0)
            for u, e, h in passes:
                for f in range(FT):
                    n = u * FT + f
                    R = P if f < FT - 1 else FR
                    act.wait_ge(up_mm, n + 1)
                    if n >= 3:
                        act.wait_ge(mid_lo_ready, n - 2)
                    nc.scalar.activation(mid[n % 3][0:R, :], ps_u[n % 3][0:R, 0:HALF], ACT.Silu,
                                         bias=b_up[(e // GS) % 2][0:R, f:f + 1]).then_inc(mid_ready, 1)
                if u + 1 < len(passes):
                    token_hi(u + 1)
                if (u + 2) % (GS * NH) == 0 and u + 2 < len(passes):
                    split_up((u + 2) // (GS * NH))
                if h == NH - 1 and e + 1 < E:
                    split_down(e + 1)
                if u == len(passes) // 2:
                    split_out()

        @block.tensor
        def _(pe):
            def turn(u):
                q = u % 2
                pe.wait_ge(gathered[q], 16 * HC * (u // 2 + 1))
                for k in range(KT):
                    if u:
                        pe.wait_ge(xg_lo_ready, KT * (u - 1) + k + 1)
                    for c in range(HC):
                        mm = pe.transpose(ps_t[k][:, c * P:(c + 1) * P], xg[q][:, c, k * P:(k + 1) * P], t.ident)
                    mm.then_inc(turned, 1)

            def up(u, e):
                q, w = u % 2, (e // GS) % 2
                pe.wait_ge(xg_lo_ready, KT * (u + 1))
                pe.wait_ge(up_lo_ready, e // GS + 1)
                for f in range(FT):
                    n = u * FT + f
                    R = P if f < FT - 1 else FR
                    if n >= 3:
                        pe.wait_ge(mid_ready, n - 2)
                    i = 0
                    for k in range(KT):
                        for wgt, x in ((up_hi[w], xg_hi[q]), (up_lo[w], xg_hi[q]), (up_hi[w], xg_lo[q])):
                            mm = pe.matmul(ps_u[n % 3][0:R, 0:HALF], wgt[:, k, f * P:f * P + R], x[:, k, :],
                                           start=(i == 0), stop=(i == 3 * KT - 1))
                            i += 1
                    mm.then_inc(up_mm, 1)

            def down(u, e):
                q, w = u % 2, e % 2
                pe.wait_ge(mid_lo_ready, FT * (u + 1))
                pe.wait_ge(dn_lo_ready, 2 * e + 2)
                for c in range(HC):
                    n = u * HC + c
                    if n >= 3:
                        pe.wait_ge(out_ready, n - 2)
                    i = 0
                    for f in range(FT):
                        R = rows_of(f)
                        for x, wgt in ((mid_hi[q], dn_hi[w]), (mid_lo[q], dn_hi[w]), (mid_hi[q], dn_lo[w])):
                            mm = pe.matmul(ps_d[n % 3][:, 0:s.D], x[0:R, f, c * P:(c + 1) * P], wgt[0:R, f, :],
                                           start=(i == 0), stop=(i == 3 * FT - 1))
                            i += 1
                    mm.then_inc(dn_mm, 1)

            pe.wait_ge(vec, steps["moments"])
            pe.matmul(ps_m[:, 0:2 * B * MT], t.headavg, moments[:, :, :, :].rearrange("p k a m -> p (k a m)"),
                      start=True, stop=True).then_inc(mom_ready, 1)
            pe.wait_ge(vec, steps["moments_read"])
            turn(0)
            for u, e, h in passes:
                up(u, e)
                if u + 1 < len(passes):
                    turn(u + 1)
                if u:
                    down(u - 1, passes[u - 1][1])
            down(*passes[-1][0:2])


def phase_output(nc, s, t, x_blk, out_blk):
    KT, MT, B, BPB, NB = s.KT, s.MT, s.B, s.BPB, s.NB
    CPRE = PRE * CH
    with ExitStack() as ctx:
        def sem(name):
            return ctx.enter_context(nc.semaphore(name))

        def sb(name, shape, dt=F32):
            return ctx.enter_context(nc.sbuf_tensor(name, shape, dt))

        w_hi, w_lo, wz_hi, wz_lo, scale, shift = t.wo_hi, t.wo_lo, t.wz_hi, t.wz_lo, t.scale, t.shift
        xn = [t.xn_first, sb("c_xn1", [P, CH, s.D])]
        xn_hi = [sb(f"c_xn_hi{i}", [P, KT, BLK], F32R) for i in range(2)]
        xn_lo = [sb(f"c_xn_lo{i}", [P, KT, BLK], F32R) for i in range(2)]
        yc = [sb(f"yc{i}", [P, MT, BLK]) for i in range(2)]
        zs = [sb(f"zs{i}", [P, MT, BLK]) for i in range(2)]
        xc = [sb(f"xc{i}", [P, CH, s.D]) for i in range(2)]
        fc = [sb(f"fc{i}", [P, CH, s.D]) for i in range(2)]
        gh = [sb(f"gh{i}", [P, MT, BLK], F32R) for i in range(2)]
        gl = [sb(f"gl{i}", [P, MT, BLK], F32R) for i in range(2)]
        oc = [sb(f"oc{i}", [P, CH, s.D]) for i in range(2)]
        ps_t, ps_z, ps_o = t.ps[0:2], t.ps[2:4], t.ps[4:8]

        loaded = [sem(f"c_loaded{i}") for i in range(2)]
        y_loaded = [sem(f"c_y_loaded{i}") for i in range(2)]
        xn_loaded = [sem(f"c_xn_loaded{i}") for i in range(2)]
        waited, sp_waited = sem("c_waited"), sem("c_sp_waited")
        xnT_ready, xn_hi_ready, xn_lo_ready = (sem(f"c_{n}") for n in ("xnT", "xnh", "xnl"))
        z_ready, zs_ready = sem("c_z"), sem("c_zs")
        gate_ready = sem("c_gate")
        normed, gated, hi_ready, lo_ready, mm_done, mul_done, sum_done = (
            sem(f"c_{n}") for n in ("normed", "gated", "hi", "lo", "mm", "mul", "sum"))
        out_stored = [sem(f"c_out{i}") for i in range(2)]
        block = ctx.enter_context(nc.Block())

        def run(eng, body):
            for bt in range(B):
                with eng.Fori(bt * BPB // 2, (bt + 1) * BPB // 2 - 1) as j:
                    for p in range(2):
                        body(bt, 2 * j + p, p, True, True, j)
                j = (bt + 1) * BPB // 2 - 1
                for p in range(2):
                    last = bt == B - 1
                    body(min(bt + 1, B - 1), 2 * j + p, p, not last or p == 0, not last, j)

        @block.vector
        def _(dve):
            v = nc.vector
            for c, k in ((gated, MT * PRE), (lo_ready, MT * PRE), (mul_done, CPRE), (xn_lo_ready, KT * PRE)):
                dve.sem_inc(c, k)

            def xn_lo_parts(b, p):
                for k in range(KT):
                    dve.wait_ge(xn_hi_ready, KT * b + (KT * PRE + k + 1))
                    v.tensor_tensor(xn_lo[p][:, k, :], ps_t[k][:, :], xn_hi[p][:, k, :].bitcast(F32),
                                    ALU.subtract).then_inc(xn_lo_ready, 1)

            for p in range(2):
                xn_lo_parts(p, p)
            def gate_parts(b, p):
                for m in range(MT + 1):
                    if m < MT:
                        dve.wait_ge(normed, MT * b + (MT * PRE + m + 1))
                        dve.wait_ge(zs_ready, MT * b + (MT * PRE + m + 1))
                        v.tensor_tensor(yc[p][:, m, :], yc[p][:, m, :], zs[p][:, m, :], ALU.mult).then_inc(gated, 1)
                    if m:
                        if m == 1:
                            dve.wait_ge(mm_done, CH * b + (CPRE - CH))
                        dve.wait_ge(hi_ready, MT * b + (MT * PRE + m))
                        v.tensor_tensor(gl[p][:, m - 1, :], yc[p][:, m - 1, :], gh[p][:, m - 1, :].bitcast(F32),
                                        ALU.subtract).then_inc(lo_ready, 1)

            def body(bt2, b, p, nxt, nxt2, j):
                if nxt:
                    gate_parts(b + 1, 1 - p)
                if nxt2:
                    xn_lo_parts(b + 2, p)
                dve.wait_ge(gate_ready, b + (PRE + 1))
                dve.wait_ge(out_stored[p], 16 * j + 16)
                for c in range(CH):
                    dve.wait_ge(mm_done, CH * b + (CPRE + c + 1))
                    v.tensor_tensor(oc[p][:, c, :], ps_o[c][:, 0:s.D], fc[p][:, c, :], ALU.mult).then_inc(
                        mul_done, 1)

            gate_parts(0, 0)
            run(dve, body)

        @block.scalar
        def _(act):
            for c, k in ((hi_ready, MT * PRE), (gate_ready, PRE), (xn_hi_ready, KT * PRE), (zs_ready, MT * PRE)):
                act.sem_inc(c, k)

            def xn_hi_parts(b, p):
                act.wait_ge(z_ready, MT * b + MT * (PRE - 1))
                for k in range(KT):
                    act.wait_ge(xnT_ready, KT * b + (KT * PRE + k + 1))
                    nc.scalar.activation(xn_hi[p][:, k, :], ps_t[k][:, :], ACT.Copy).then_inc(xn_hi_ready, 1)

            def gate_parts(b, p):
                act.wait_ge(mm_done, CH * b + (CPRE - CH))
                for m in range(MT + 1):
                    if m < MT:
                        act.wait_ge(z_ready, MT * b + (MT * PRE + m + 1))
                        act.wait_ge(gated, MT * b + (MT * (PRE - 2) + m + 1))
                        nc.scalar.activation(zs[p][:, m, :], ps_z[m % 2][:, :], ACT.Silu).then_inc(zs_ready, 1)
                    if m:
                        act.wait_ge(gated, MT * b + (MT * PRE + m))
                        nc.scalar.activation(gh[p][:, m - 1, :], yc[p][:, m - 1, :], ACT.Copy).then_inc(hi_ready, 1)

            def body(bt2, b, p, nxt, nxt2, j):
                if nxt:
                    gate_parts(b + 1, 1 - p)
                if nxt2:
                    xn_hi_parts(b + 2, p)
                act.wait_ge(loaded[p], 32 * j + 32)
                nc.scalar.activation(fc[p][:, :, :], fc[p][:, :, :], ACT.Silu).then_inc(gate_ready, 1)

            for p in range(2):
                xn_hi_parts(p, p)
            gate_parts(0, 0)
            run(act, body)

        @block.gpsimd
        def _(pool):
            for c, k in ((sum_done, PRE), (normed, MT * PRE)):
                pool.sem_inc(c, k)

            def group_norm(bt, b, p, pair):
                pool.wait_ge(y_loaded[p], 16 * pair + 16)
                pool.sem_inc(waited, 1)
                for m in range(MT):
                    nc.gpsimd.tensor_scalar(yc[p][:, m, :], yc[p][:, m, :], scale[:, bt, m:m + 1],
                                            shift[:, bt, m:m + 1], ALU.mult, ALU.add).then_inc(normed, 1)

            def body(bt2, b, p, nxt, nxt2, j):
                if nxt2:
                    group_norm(bt2, b + 2, p, j + 1)
                pool.wait_ge(mul_done, CH * b + (CPRE + CH))
                nc.gpsimd.tensor_tensor(oc[p][:, :, :], oc[p][:, :, :], xc[p][:, :, :], ALU.add).then_inc(sum_done, 1)

            for p in range(2):
                group_norm(0, p, p, 0)
            run(pool, body)

        @block.tensor
        def _(pe):
            for c, k in ((mm_done, CPRE), (xnT_ready, KT * PRE), (z_ready, MT * PRE)):
                pe.sem_inc(c, k)

            def turn(b, p, pair):
                pe.wait_ge(xn_loaded[p], 16 * pair + 16)
                for k in range(KT):
                    pe.wait_ge(xn_lo_ready, KT * b + (KT * (PRE - 1) + k + 1))
                    for c in range(CH):
                        mm = pe.transpose(ps_t[k][:, c * P:(c + 1) * P], xn[p][:, c, k * P:(k + 1) * P], t.ident)
                    mm.then_inc(xnT_ready, 1)

            def project_z(b, p):
                pe.wait_ge(xn_lo_ready, KT * b + KT * (PRE + 1))
                for m in range(MT):
                    pe.wait_ge(zs_ready, MT * b + (MT * PRE + m - 2 + 1))
                    n = 0
                    for k in range(KT):
                        for wgt, x in ((wz_hi, xn_hi[p]), (wz_lo, xn_hi[p]), (wz_hi, xn_lo[p])):
                            mm = pe.matmul(ps_z[m % 2][:, :], wgt[:, k, m * P:(m + 1) * P], x[:, k, :],
                                           start=(n == 0), stop=(n == 3 * KT - 1))
                            n += 1
                    mm.then_inc(z_ready, 1)

            def body(bt2, b, p, nxt, nxt2, j):
                if nxt:
                    project_z(b + 1, 1 - p)
                if nxt2:
                    turn(b + 2, p, j + 1)
                pe.wait_ge(lo_ready, MT * b + MT * (PRE + 1))
                for c in range(CH):
                    pe.wait_ge(mul_done, CH * b + (CPRE - CH + c + 1))
                    n = 0
                    for k in range(MT):
                        for g, w in ((gh[p], w_hi), (gl[p], w_hi), (gh[p], w_lo)):
                            mm = pe.matmul(ps_o[c][:, 0:s.D], g[:, k, c * P:(c + 1) * P], w[:, k, :],
                                           start=(n == 0), stop=(n == 3 * MT - 1))
                            n += 1
                    mm.then_inc(mm_done, 1)

            turn(0, 0, 0)
            turn(1, 1, 0)
            project_z(0, 0)
            run(pe, body)

        @block.sync
        def _(sp):
            for p in range(2):
                sp.sem_inc(out_stored[p], 16)

            def load_early(b, p):
                sp.dma_start(xn[p][:, :, :], t.xn_blk[b]).then_inc(xn_loaded[p], 16)
                sp.dma_start(yc[p][:, :, :], t.y_dram[b]).then_inc(y_loaded[p], 16)

            def load_late(b, p):
                for dst, src in ((xc, x_blk[b]), (fc, t.ffn_blk[b])):
                    sp.dma_start(dst[p][:, :, :], src).then_inc(loaded[p], 16)

            def store(b, p):
                sp.wait_ge(sum_done, b + (PRE + 1))
                sp.dma_start(out_blk[b], oc[p][:, :, :]).then_inc(out_stored[p], 16)

            def reload_early(b, p):
                sp.wait_ge(xnT_ready, KT * b + KT * (PRE - 1))
                sp.wait_ge(lo_ready, MT * b + MT * (PRE - 1))
                sp.sem_inc(sp_waited, 1)
                load_early(b, p)

            def load_xn(b, p):
                sp.dma_start(xn[p][:, :, :], t.xn_blk[b]).then_inc(xn_loaded[p], 16)

            sp.sem_inc(xn_loaded[0], 16)
            load_xn(1, 1)
            for p in range(2):
                sp.dma_start(yc[p][:, :, :], t.y_dram[p]).then_inc(y_loaded[p], 16)
            for p in range(2):
                load_late(p, p)
            reload_early(2, 0)
            with sp.Fori(0, NB // 2 - 2) as j:
                for p in range(2):
                    reload_early(2 * j + p + 3, 1 - p)
                    store(2 * j + p, p)
                    load_late(2 * j + p + 2, p)
            for p in range(2):
                if p == 0:
                    reload_early(NB - 1, 1)
                store(NB - 4 + p, p)
                load_late(NB - 2 + p, p)
            for p in range(2):
                store(NB - 2 + p, p)
            for p in range(2):
                sp.wait_ge(out_stored[p], 16 * (NB // 2 + 1))


def build(nc, ins, outs):
    x_d = ins["x"]
    s = Shapes(x_d, ins["wx"], ins["wdt"], ins["wr"], ins["wup"])
    x_blk = x_d.rearrange("b (i c p) d -> (b i) p c d", c=CH, p=P)
    t = Tiles()

    def dram(name, shape):
        return nc.dram_tensor(name, shape, F32, kind="Internal").ap()

    t.rows_dram = dram("rows_dram", [s.T, s.ROW])
    t.x2_dram = dram("x2_dram", [s.NB, P, s.MT, BLK])
    t.y_dram = dram("y_dram", [s.NB, P, s.MT, BLK])
    t.ffn_dram = dram("ffn_dram", [s.T, s.D])
    t.cum_dram = dram("cum_dram", [s.NT, s.H, P])
    t.ecum_dram = dram("ecum_dram", [s.NT, s.H, P])
    t.ffn_blk = t.ffn_dram.rearrange("(i c p) d -> i p c d", c=CH, p=P)
    t.xn_blk = t.rows_dram[:, 0:s.D].rearrange("(i c p) d -> i p c d", c=CH, p=P)
    with ExitStack() as ctx:
        def sb(name, shape, dt=F32):
            return ctx.enter_context(nc.sbuf_tensor(name, shape, dt))

        t.ps = [ctx.enter_context(nc.psum_tensor(f"ps{i}", [P, 512], F32)) for i in range(8)]
        t.cst = sb("cst", [P, C_END])
        t.ident = t.cst[:, C_ID:C_ID + P]
        t.tri = t.cst[:, C_TRI:C_TRI + P]
        t.ones = t.cst[:, C_ONES:C_ONES + P]
        t.rsum = t.cst[:, C_RSUM:C_RSUM + P]
        t.rtri = t.cst[:, C_RTRI:C_RTRI + P]
        t.iota = t.cst[:, C_IOTA:C_IOTA + P]
        t.headavg = t.cst[:, C_HEAD:C_HEAD + P]
        t.rows = sb("rows", [P, 3, 8])
        t.dcol, t.gnw, t.gnb, t.cb = (sb(n, [P, s.MT]) for n in ("dcol", "gnw", "gnb", "cb"))
        t.cw = sb("cw", [P, s.MT, 4])
        t.norm = sb("norm", [P, 2, s.NT])
        t.dt_all = sb("dt", [P, CH + s.NT, s.H])
        t.dt = t.dt_all[:, CH:, :]
        t.cum = sb("cum", [P, s.NT, s.H])
        t.wst = sb("wst", [P, s.NT, s.H])
        t.dec = sb("dec", [P, s.NT, s.MT])
        t.gates = sb("gates", [P, s.NT, s.E])
        t.idx = sb("idx", [P, s.E, s.LW], U32)
        t.ystat = sb("ystat", [P, s.NB, s.MT, 6])
        with ExitStack() as mid:
            t.wbc_hi = [mid.enter_context(nc.sbuf_tensor(f"w_hi_{n}", [P, s.MT, s.INNER], F32R)) for n in "bc"]
            t.wbc_lo = [mid.enter_context(nc.sbuf_tensor(f"w_lo_{n}", [P, s.MT, s.INNER], F32R)) for n in "bc"]
            t.x2, t.x_hi, t.x_lo = (
                [mid.enter_context(nc.sbuf_tensor(f"{n}{i}", [P, s.MT, BLK], dt)) for i in range(2)]
                for n, dt in (("x2_", F32), ("x_hi", F32R), ("x_lo", F32R)))
            t.bT0, t.cT0 = (mid.enter_context(nc.sbuf_tensor(n, [P, s.MT, BLK], F32)) for n in ("bT0", "cT0"))
            t.gateT = mid.enter_context(nc.sbuf_tensor("gateT", [P, s.SEG], F32))
            with ExitStack() as early:
                def sbe(name, shape, dt=F32):
                    return early.enter_context(nc.sbuf_tensor(name, shape, dt))

                t.wx = sbe("wx", [P, s.KT, s.INNER])
                t.wr = sbe("wr", [P, s.KT, s.E])
                t.wx_hi, t.wx_lo = (sbe(f"wx_{n}", [P, s.KT, s.INNER], F32R) for n in ("hi", "lo"))
                t.wr2 = sbe("wr2", [P, s.KT, 2, s.E], F32R)
                t.wdt = sbe("wdt", [P, s.MT, s.H])
                t.logit2 = sbe("logit2", [P, s.NT, 2, s.E])
                consts = [(t.cst[:, :], ins["const"]), (t.rows[:, :, :], ins["rows"]), (t.dcol[:, :], ins["dcol"]),
                          (t.gnw[:, :], ins["gnw"]), (t.gnb[:, :], ins["gnb"]), (t.cb[:, :], ins["cb"]),
                          (t.cw[:, :, :], ins["cw"]),
                          (t.wx[:, :, :], ins["wx"].rearrange("(k p) n -> p k n", p=P)),
                          (t.wr[:, :, :], ins["wr"].rearrange("(k p) n -> p k n", p=P)),
                          (t.wdt[:, :, :], ins["wdt"].rearrange("(k p) n -> p k n", p=P))]
                phase_stats(nc, s, t, x_blk, consts)
                phase_project(nc, s, t, x_blk)
                phase_decays(nc, s, t, ins["wb"], ins["wc"])
            phase_scan(nc, s, t)
        t.wo_hi, t.wo_lo = (sb(n, [P, s.MT, s.D], F32R) for n in ("wo_hi", "wo_lo"))
        t.wz_hi, t.wz_lo = (sb(n, [P, s.KT, s.INNER], F32R) for n in ("wz_hi", "wz_lo"))
        t.scale, t.shift = (sb(n, [P, s.B, s.MT]) for n in ("gn_scale", "gn_shift"))
        t.xn_first = sb("xn_first", [P, CH, s.D])
        phase_experts(nc, s, t, ins["wup"], ins["bup"], ins["wdn"], ins["wout"], ins["wz"])
        phase_output(nc, s, t, x_blk, outs["out"].rearrange("b (i c p) d -> (b i) p c d", c=CH, p=P))


def shape_constants(T, E):
    import numpy as np

    i = np.arange(P)
    c = np.zeros((P, C_END), np.float32)
    c[:, C_ID:C_ID + P] = np.eye(P)
    c[:, C_TRI:C_TRI + P] = i[:, None] <= i[None, :]
    c[:, C_ONES:C_ONES + P] = 1
    same = i[:, None] % E == i[None, :] % E
    c[:, C_RSUM:C_RSUM + P] = same
    c[:, C_RTRI:C_RTRI + P] = same & (i[:, None] < i[None, :])
    c[:, C_IOTA:C_IOTA + P] = i[None, :]
    c[:, C_HEAD:C_HEAD + P] = (i[:, None] // 64 == i[None, :] // 64) / 64.0
    c[:, C_TAU:C_TAU + 64] = np.arange(64)[None, :]
    c[:, C_PIDX] = i
    c[:, C_LO:C_LO + 8] = np.arange(8)[None, :]
    c[:, C_BIT:C_BIT + BITS] = 2.0 ** np.arange(BITS - 1, -1, -1)[None, :]
    return c


def lay_out(v):
    import numpy as np

    a = {k.split("_", 2)[2]: np.asarray(x) for k, x in v.items()}
    con = np.ascontiguousarray

    def column(row, width=P):
        return con(row.reshape(-1, width).T)

    d = a["d_param"]
    F = a["W_down"].shape[1]
    FT = -(-F // P)
    bup = np.zeros((a["b_up"].shape[0], FT * P), a["b_up"].dtype)
    bup[:, :F] = a["b_up"]
    x = a["input_tensor"]
    return {
        "x": con(x),
        "wx": con(a["Wx"].T), "wz": con(a["Wz"].T), "wb": con(a["Wb"].T), "wc": con(a["Wc"].T),
        "wdt": con(a["Wdt"].T), "wout": con(a["Wout"].T), "wr": con(a["Wr"]),
        "cw": con(a["conv_w"][:, 0, :].reshape(-1, P, 4).transpose(1, 0, 2)), "cb": column(a["conv_b"]),
        "rows": con(np.broadcast_to(np.stack([a["log_a"], a["b_dt"], a["br"]])[None], (P, 3, 8))),
        "dcol": column(np.repeat(d, a["gn_w"].shape[0] // d.shape[0])),
        "gnw": column(a["gn_w"]), "gnb": column(a["gn_b"]),
        "wup": con(a["W_up"]), "bup": con(bup.reshape(-1, FT, P).transpose(0, 2, 1)),
        "wdn": con(np.concatenate([a["W_down"], a["b_down"][:, None, :]], axis=1)),
        "const": shape_constants(x.shape[0] * x.shape[1], a["Wr"].shape[1]),
    }


def kernel(**inputs):
    import numpy as _np
    import concourse.bacc as _bacc
    from concourse import mybir as _mybir
    from concourse.bass_utils import run_bass_kernel_spmd as _run

    nc = _bacc.Bacc("TRN2", target_bir_lowering=False, num_devices=1)
    arrays = {f"in_{k}": v for k, v in lay_out(inputs).items()}
    ins = {k[3:]: nc.dram_tensor(k, v.shape, _mybir.dt.from_np(v.dtype), kind="ExternalInput").ap()
           for k, v in arrays.items()}
    shape = arrays["in_x"].shape
    out = nc.dram_tensor("out_dram", shape, _mybir.dt.float32, kind="ExternalOutput").ap()
    build(nc, ins, {"out": out})
    r = _run(nc, [arrays], core_ids=[0])
    return r.results[0]["out_dram"]
```
